# Optimizing a Trainium2 kernel written in Bass

```python
import numpy as np
import jax
import jax.numpy as jnp

def _softmax(x, axis=-1):
    return jax.nn.softmax(x, axis=axis)
def _gelu(x):
    return jax.nn.gelu(x, approximate=True)
def _silu(x):
    return jax.nn.silu(x)
def _sigmoid(x):
    return jax.nn.sigmoid(x)
def _layernorm(x, axis=-1, eps=1e-5):
    m = jnp.mean(x, axis=axis, keepdims=True)
    v = jnp.var(x, axis=axis, keepdims=True)
    return (x - m) / jnp.sqrt(v + eps)
def _scatter_add(tgt, idx, src, axis=0):
    return tgt.at[idx].add(src)
def _segment_sum(src, seg, n):
    return jax.ops.segment_sum(src, seg, n)

kernel_name = 'mk_conv_attn_hybrid_d2_conv_nhwc128_851eda'

def setup_inputs(seed: int = 0):
    np.random.seed(seed)
    _w = jnp.asarray
    def _rec_inputs():
        import jax
        import jax.numpy as jnp
        _gk = jax.random.key(seed)
        x = -0.000929 + 1 * jax.random.normal(jax.random.fold_in(_gk, 1), (8, 64, 16, 128), jnp.float32)
        return x
    x = _rec_inputs()
    def _L0_conv_setup():
        import jax, jax.numpy as jnp
        import numpy as np
        B, L, F, C, H, FF = (8, 64, 16, 128, 8, 512)

        def _layer_norm(x, g, b, eps=1e-05):
            m = jnp.mean(x, axis=-1, keepdims=True)
            v = jnp.mean(jnp.square(x - m), axis=-1, keepdims=True)
            return (x - m) * jax.lax.rsqrt(v + eps) * g + b
        key = jax.random.key(seed)
        ks = jax.random.split(key, 5)
        s = jnp.float32(0.02)
        return {'x': jax.random.normal(ks[0], (B, L, F, C), jnp.float32), 'wq': jax.random.normal(ks[1], (C * H, C), jnp.float32) * s, 'bq': jnp.zeros((C * H,), jnp.float32), 'wk': jax.random.normal(ks[2], (C * H, C), jnp.float32) * s, 'bk': jnp.zeros((C * H,), jnp.float32), 'wv': jax.random.normal(ks[3], (C * H, C), jnp.float32) * s, 'bv': jnp.zeros((C * H,), jnp.float32), 'wo': jax.random.normal(ks[4], (C, C * H), jnp.float32) * s, 'bo': jnp.zeros((C,), jnp.float32), 'ln1_g': jnp.ones((C,), jnp.float32), 'ln1_b': jnp.zeros((C,), jnp.float32), 'w1': jax.random.normal(jax.random.fold_in(key, 10), (FF, C), jnp.float32) * s, 'b1': jnp.zeros((FF,), jnp.float32), 'w2': jax.random.normal(jax.random.fold_in(key, 11), (C, FF), jnp.float32) * s, 'b2': jnp.zeros((C,), jnp.float32), 'ln2_g': jnp.ones((C,), jnp.float32), 'ln2_b': jnp.zeros((C,), jnp.float32)}
    _L0_conv_all = _L0_conv_setup()
    _L0_conv_in = {k: v for k, v in _L0_conv_all.items() if k in ('wq', 'bq', 'wk', 'bk', 'wv', 'bv', 'wo', 'bo', 'ln1_g', 'ln1_b', 'w1', 'b1', 'w2', 'b2', 'ln2_g', 'ln2_b', )}
    del _L0_conv_all

    def _L1_attn_setup():
        import jax, jax.numpy as jnp
        import numpy as np
        CHUNK = 64
        D_MODEL = 128
        D_STATE = 64
        HEADDIM = 64
        D_INNER = 2 * D_MODEL
        NHEADS = D_INNER // HEADDIM
        CONV_DIM = D_INNER + 2 * D_STATE
        K = 4
        D_IN_PROJ = 2 * D_INNER + 2 * D_STATE + NHEADS
        EPS = 1e-05

        def _segsum(t):
            L = t.shape[-1]
            cs = jnp.cumsum(t, -1)
            seg = cs[..., :, None] - cs[..., None, :]
            mask = jnp.tril(jnp.ones((L, L), bool))
            return jnp.where(mask, seg, -jnp.inf)

        def _ssd(xh, dt, A, Bm, Cm):
            b, l, h, p = xh.shape
            n = Bm.shape[-1]
            c = l // CHUNK
            xdt = xh * dt[..., None]
            dA = dt * A
            rc = lambda t: t.reshape(b, c, CHUNK, *t.shape[2:])
            xc, dAc, Bc, Cc = (rc(xdt), rc(dA), rc(Bm), rc(Cm))
            Acs = jnp.cumsum(dAc, axis=2)
            Lmat = jnp.exp(_segsum(dAc.transpose(0, 1, 3, 2)))
            Y_diag = jnp.einsum('bcln,bcsn,bchls,bcshp->bclhp', Cc, Bc, Lmat, xc)
            decay_st = jnp.exp(Acs[:, :, -1:, :] - Acs)
            states = jnp.einsum('bcln,bclh,bclhp->bchpn', Bc, decay_st, xc)
            chunk_decay = jnp.exp(Acs[:, :, -1])

            def step(carry, inp):
                st, dec = inp
                new = st + carry * dec[:, :, None, None]
                return (new, carry)
            init = jnp.zeros((b, h, p, n), xh.dtype)
            _, prev = jax.lax.scan(step, init, (states.transpose(1, 0, 2, 3, 4), chunk_decay.transpose(1, 0, 2)))
            prev = prev.transpose(1, 0, 2, 3, 4)
            Y_off = jnp.einsum('bcln,bchpn,bclh->bclhp', Cc, prev, jnp.exp(Acs))
            return (Y_diag + Y_off).reshape(b, l, h, p)

        def _mamba3(x, in_proj, conv_w, conv_b, A_log, dt_bias, D, norm_w, out_proj):
            b, l, _ = x.shape
            zxbcdt = x @ in_proj
            z, xbc, dt = jnp.split(zxbcdt, [D_INNER, D_INNER + CONV_DIM], axis=-1)
            xp = jnp.pad(xbc, ((0, 0), (K - 1, 0), (0, 0)))
            conv = sum((xp[:, i:i + l, :] * conv_w[:, i] for i in range(K))) + conv_b
            xbc = jax.nn.silu(conv)
            xh, Bm, Cm = jnp.split(xbc, [D_INNER, D_INNER + D_STATE], axis=-1)
            xh = xh.reshape(b, l, NHEADS, HEADDIM)
            dt = jax.nn.softplus(dt + dt_bias)
            A = -jnp.exp(A_log)
            y = _ssd(xh, dt, A, Bm, Cm) + xh * D[None, None, :, None]
            yg = y.reshape(b, l, D_INNER) * jax.nn.silu(z)
            yn = yg * jax.lax.rsqrt(jnp.mean(yg * yg, -1, keepdims=True) + EPS) * norm_w
            return yn @ out_proj
        key = jax.random.key(seed)
        ks = jax.random.split(key, 19)
        inp = {'x': jax.random.normal(ks[0], (16, 4096, D_MODEL), jnp.float32)}
        for i, pre in enumerate(['fwd', 'bwd']):
            o = 1 + 9 * i
            inp[pre + '_in_proj'] = jax.random.normal(ks[o], (D_MODEL, D_IN_PROJ), jnp.float32) * D_MODEL ** (-0.5)
            inp[pre + '_conv_w'] = jax.random.normal(ks[o + 1], (CONV_DIM, K), jnp.float32) * 0.3
            inp[pre + '_conv_b'] = jnp.zeros((CONV_DIM,), jnp.float32)
            inp[pre + '_A_log'] = jnp.log(jax.random.uniform(ks[o + 2], (NHEADS,), jnp.float32, 1.0, 16.0))
            inp[pre + '_dt_bias'] = jax.random.normal(ks[o + 3], (NHEADS,), jnp.float32) * 0.5
            inp[pre + '_D'] = jnp.ones((NHEADS,), jnp.float32)
            inp[pre + '_norm_w'] = jnp.ones((D_INNER,), jnp.float32)
            inp[pre + '_out_proj'] = jax.random.normal(ks[o + 4], (D_INNER, D_MODEL), jnp.float32) * D_INNER ** (-0.5)
        return inp
    _L1_attn_all = _L1_attn_setup()
    _L1_attn_in = {k: v for k, v in _L1_attn_all.items() if k in ('fwd_in_proj', 'fwd_conv_w', 'fwd_conv_b', 'fwd_A_log', 'fwd_dt_bias', 'fwd_D', 'fwd_norm_w', 'fwd_out_proj', 'bwd_in_proj', 'bwd_conv_w', 'bwd_conv_b', 'bwd_A_log', 'bwd_dt_bias', 'bwd_D', 'bwd_norm_w', 'bwd_out_proj', )}
    del _L1_attn_all

    def _L1_ffn_setup():
        import jax, jax.numpy as jnp
        import numpy as np
        B, S, D, E, H, O, K = (512, 2048, 128, 64, 512, 128, 8)
        key = jax.random.key(seed)
        k0, k1, k2, k3 = jax.random.split(key, 4)
        x = jax.random.normal(k0, (B, S, D), dtype=jnp.float32)
        gate_w = jax.random.normal(k1, (E, D), dtype=jnp.float32) * (1.0 / np.sqrt(D))
        gate_b = jnp.zeros((E,), dtype=jnp.float32)
        weight1 = jax.random.uniform(k2, (E, D + 1, H), dtype=jnp.float32, minval=-1.0, maxval=1.0) * (1.0 / np.sqrt(D + 1))
        weight2 = jax.random.uniform(k3, (E, H + 1, O), dtype=jnp.float32, minval=-1.0, maxval=1.0) * (1.0 / np.sqrt(H + 1))
        return {'x': x, 'gate_w': gate_w, 'gate_b': gate_b, 'weight1': weight1, 'weight2': weight2}
    _L1_ffn_all = _L1_ffn_setup()
    _L1_ffn_in = {k: v for k, v in _L1_ffn_all.items() if k in ('gate_w', 'gate_b', 'weight1', 'weight2', )}
    del _L1_ffn_all

    return {
        "x": x,
        "L0_conv_wq": _L0_conv_in["wq"],
        "L0_conv_bq": _L0_conv_in["bq"],
        "L0_conv_wk": _L0_conv_in["wk"],
        "L0_conv_bk": _L0_conv_in["bk"],
        "L0_conv_wv": _L0_conv_in["wv"],
        "L0_conv_bv": _L0_conv_in["bv"],
        "L0_conv_wo": _L0_conv_in["wo"],
        "L0_conv_bo": _L0_conv_in["bo"],
        "L0_conv_ln1_g": _L0_conv_in["ln1_g"],
        "L0_conv_ln1_b": _L0_conv_in["ln1_b"],
        "L0_conv_w1": _L0_conv_in["w1"],
        "L0_conv_b1": _L0_conv_in["b1"],
        "L0_conv_w2": _L0_conv_in["w2"],
        "L0_conv_b2": _L0_conv_in["b2"],
        "L0_conv_ln2_g": _L0_conv_in["ln2_g"],
        "L0_conv_ln2_b": _L0_conv_in["ln2_b"],
        "L1_attn_fwd_in_proj": _L1_attn_in["fwd_in_proj"],
        "L1_attn_fwd_conv_w": _L1_attn_in["fwd_conv_w"],
        "L1_attn_fwd_conv_b": _L1_attn_in["fwd_conv_b"],
        "L1_attn_fwd_A_log": _L1_attn_in["fwd_A_log"],
        "L1_attn_fwd_dt_bias": _L1_attn_in["fwd_dt_bias"],
        "L1_attn_fwd_D": _L1_attn_in["fwd_D"],
        "L1_attn_fwd_norm_w": _L1_attn_in["fwd_norm_w"],
        "L1_attn_fwd_out_proj": _L1_attn_in["fwd_out_proj"],
        "L1_attn_bwd_in_proj": _L1_attn_in["bwd_in_proj"],
        "L1_attn_bwd_conv_w": _L1_attn_in["bwd_conv_w"],
        "L1_attn_bwd_conv_b": _L1_attn_in["bwd_conv_b"],
        "L1_attn_bwd_A_log": _L1_attn_in["bwd_A_log"],
        "L1_attn_bwd_dt_bias": _L1_attn_in["bwd_dt_bias"],
        "L1_attn_bwd_D": _L1_attn_in["bwd_D"],
        "L1_attn_bwd_norm_w": _L1_attn_in["bwd_norm_w"],
        "L1_attn_bwd_out_proj": _L1_attn_in["bwd_out_proj"],
        "L1_ffn_gate_w": _L1_ffn_in["gate_w"],
        "L1_ffn_gate_b": _L1_ffn_in["gate_b"],
        "L1_ffn_weight1": _L1_ffn_in["weight1"],
        "L1_ffn_weight2": _L1_ffn_in["weight2"],
    }

def reference(x, L0_conv_wq, L0_conv_bq, L0_conv_wk, L0_conv_bk, L0_conv_wv, L0_conv_bv, L0_conv_wo, L0_conv_bo, L0_conv_ln1_g, L0_conv_ln1_b, L0_conv_w1, L0_conv_b1, L0_conv_w2, L0_conv_b2, L0_conv_ln2_g, L0_conv_ln2_b, L1_attn_fwd_in_proj, L1_attn_fwd_conv_w, L1_attn_fwd_conv_b, L1_attn_fwd_A_log, L1_attn_fwd_dt_bias, L1_attn_fwd_D, L1_attn_fwd_norm_w, L1_attn_fwd_out_proj, L1_attn_bwd_in_proj, L1_attn_bwd_conv_w, L1_attn_bwd_conv_b, L1_attn_bwd_A_log, L1_attn_bwd_dt_bias, L1_attn_bwd_D, L1_attn_bwd_norm_w, L1_attn_bwd_out_proj, L1_ffn_gate_w, L1_ffn_gate_b, L1_ffn_weight1, L1_ffn_weight2):
    import jax
    import jax.numpy as jnp
    def _L0_conv_ref(x, wq, bq, wk, bk, wv, bv, wo, bo, ln1_g, ln1_b, w1, b1, w2, b2, ln2_g, ln2_b):
        import jax, jax.numpy as jnp
        import numpy as np
        B, L, F, C, H, FF = (8, 64, 16, 128, 8, 512)

        def _layer_norm(x, g, b, eps=1e-05):
            m = jnp.mean(x, axis=-1, keepdims=True)
            v = jnp.mean(jnp.square(x - m), axis=-1, keepdims=True)
            return (x - m) * jax.lax.rsqrt(v + eps) * g + b
        b_, l, f, c = x.shape
        h = wq.shape[0] // c

        def proj(w, bias):
            y = x @ w.T + bias
            y = y.reshape(b_, l, f, c, h)
            return jnp.transpose(y, (0, 4, 1, 2, 3))
        q = proj(wq, bq)
        k = proj(wk, bk)
        v = proj(wv, bv)
        scores = jnp.einsum('bhlfc,bhmgc->bhlfmg', q, k) / jnp.sqrt(jnp.float32(c))
        a = jax.nn.softmax(scores, axis=4)
        a = jax.nn.softmax(a, axis=5)
        z = jnp.einsum('bhlfmg,bhmgc->bhlfc', a, v)
        z = jnp.transpose(z, (0, 2, 3, 4, 1)).reshape(b_, l, f, c * h)
        attn_out = z @ wo.T + bo
        z1 = _layer_norm(attn_out + x, ln1_g, ln1_b)
        ffy = jax.nn.relu(z1 @ w1.T + b1) @ w2.T + b2
        return _layer_norm(ffy + z1, ln2_g, ln2_b)

    def _L1_attn_ref(x, fwd_in_proj, fwd_conv_w, fwd_conv_b, fwd_A_log, fwd_dt_bias, fwd_D, fwd_norm_w, fwd_out_proj, bwd_in_proj, bwd_conv_w, bwd_conv_b, bwd_A_log, bwd_dt_bias, bwd_D, bwd_norm_w, bwd_out_proj):
        import jax, jax.numpy as jnp
        import numpy as np
        CHUNK = 64
        D_MODEL = 128
        D_STATE = 64
        HEADDIM = 64
        D_INNER = 2 * D_MODEL
        NHEADS = D_INNER // HEADDIM
        CONV_DIM = D_INNER + 2 * D_STATE
        K = 4
        D_IN_PROJ = 2 * D_INNER + 2 * D_STATE + NHEADS
        EPS = 1e-05

        def _segsum(t):
            L = t.shape[-1]
            cs = jnp.cumsum(t, -1)
            seg = cs[..., :, None] - cs[..., None, :]
            mask = jnp.tril(jnp.ones((L, L), bool))
            return jnp.where(mask, seg, -jnp.inf)

        def _ssd(xh, dt, A, Bm, Cm):
            b, l, h, p = xh.shape
            n = Bm.shape[-1]
            c = l // CHUNK
            xdt = xh * dt[..., None]
            dA = dt * A
            rc = lambda t: t.reshape(b, c, CHUNK, *t.shape[2:])
            xc, dAc, Bc, Cc = (rc(xdt), rc(dA), rc(Bm), rc(Cm))
            Acs = jnp.cumsum(dAc, axis=2)
            Lmat = jnp.exp(_segsum(dAc.transpose(0, 1, 3, 2)))
            Y_diag = jnp.einsum('bcln,bcsn,bchls,bcshp->bclhp', Cc, Bc, Lmat, xc)
            decay_st = jnp.exp(Acs[:, :, -1:, :] - Acs)
            states = jnp.einsum('bcln,bclh,bclhp->bchpn', Bc, decay_st, xc)
            chunk_decay = jnp.exp(Acs[:, :, -1])

            def step(carry, inp):
                st, dec = inp
                new = st + carry * dec[:, :, None, None]
                return (new, carry)
            init = jnp.zeros((b, h, p, n), xh.dtype)
            _, prev = jax.lax.scan(step, init, (states.transpose(1, 0, 2, 3, 4), chunk_decay.transpose(1, 0, 2)))
            prev = prev.transpose(1, 0, 2, 3, 4)
            Y_off = jnp.einsum('bcln,bchpn,bclh->bclhp', Cc, prev, jnp.exp(Acs))
            return (Y_diag + Y_off).reshape(b, l, h, p)

        def _mamba3(x, in_proj, conv_w, conv_b, A_log, dt_bias, D, norm_w, out_proj):
            b, l, _ = x.shape
            zxbcdt = x @ in_proj
            z, xbc, dt = jnp.split(zxbcdt, [D_INNER, D_INNER + CONV_DIM], axis=-1)
            xp = jnp.pad(xbc, ((0, 0), (K - 1, 0), (0, 0)))
            conv = sum((xp[:, i:i + l, :] * conv_w[:, i] for i in range(K))) + conv_b
            xbc = jax.nn.silu(conv)
            xh, Bm, Cm = jnp.split(xbc, [D_INNER, D_INNER + D_STATE], axis=-1)
            xh = xh.reshape(b, l, NHEADS, HEADDIM)
            dt = jax.nn.softplus(dt + dt_bias)
            A = -jnp.exp(A_log)
            y = _ssd(xh, dt, A, Bm, Cm) + xh * D[None, None, :, None]
            yg = y.reshape(b, l, D_INNER) * jax.nn.silu(z)
            yn = yg * jax.lax.rsqrt(jnp.mean(yg * yg, -1, keepdims=True) + EPS) * norm_w
            return yn @ out_proj
        h_f = _mamba3(x, fwd_in_proj, fwd_conv_w, fwd_conv_b, fwd_A_log, fwd_dt_bias, fwd_D, fwd_norm_w, fwd_out_proj)
        xr = x[:, ::-1, :]
        h_b = _mamba3(xr, bwd_in_proj, bwd_conv_w, bwd_conv_b, bwd_A_log, bwd_dt_bias, bwd_D, bwd_norm_w, bwd_out_proj)[:, ::-1, :]
        return h_f + h_b

    def _L1_ffn_ref(x, gate_w, gate_b, weight1, weight2):
        import jax, jax.numpy as jnp
        import numpy as np
        B, S, D, E, H, O, K = (512, 2048, 128, 64, 512, 128, 8)
        Bn, Sn, Dn = x.shape
        logits = jnp.einsum('bsd,ed->bse', x, gate_w) + gate_b
        probs = jax.nn.softmax(logits, axis=1)
        vals, idx = jax.lax.top_k(probs.transpose(0, 2, 1), K)
        topv = vals.transpose(0, 2, 1)
        topi = idx.transpose(0, 2, 1)
        flat_idx = topi.reshape(Bn, K * E)
        gathered = jnp.take_along_axis(x, flat_idx[:, :, None], axis=1)
        gathered = gathered.reshape(Bn, K, E, Dn)
        pooled = jnp.einsum('bked,bke->bed', gathered, topv)
        ones = jnp.ones((E, Bn, 1), dtype=x.dtype)
        h = jnp.concatenate([pooled.transpose(1, 0, 2), ones], axis=-1)
        h = jax.nn.gelu(jnp.einsum('ebd,edh->ebh', h, weight1), approximate=False)
        h = jnp.concatenate([h, ones], axis=-1)
        out = jnp.einsum('ebh,eho->ebo', h, weight2)
        out = out.transpose(1, 0, 2)
        weighted = jnp.einsum('beo,bke->bkeo', out, topv).reshape(Bn, K * E, O)
        outputs = jnp.zeros((Bn, Sn, O), dtype=x.dtype)
        outputs = outputs.at[jnp.arange(Bn)[:, None], flat_idx].add(weighted)
        return outputs

    def _gn(v, G=32, eps=1e-5):
        B_, H_, W_, C_ = v.shape
        g = v.reshape(B_, H_, W_, G, C_ // G)
        m = jnp.mean(g, axis=(1, 2, 4), keepdims=True)
        s = jnp.var(g, axis=(1, 2, 4), keepdims=True)
        return ((g - m) / jnp.sqrt(s + eps)).reshape(v.shape)

    def _ln_c(v, eps=1e-6):
        m = jnp.mean(v, axis=-1, keepdims=True)
        s = jnp.var(v, axis=-1, keepdims=True)
        return (v - m) / jnp.sqrt(s + eps)

    def _ln_t(v, eps=1e-5):
        m = jnp.mean(v, axis=-1, keepdims=True)
        s = jnp.var(v, axis=-1, keepdims=True)
        return (v - m) / jnp.sqrt(s + eps)

    def _to_tokens(v):
        B_, H_, W_, C_ = v.shape
        return v.reshape(B_, H_ * W_, C_)
    def _from_tokens(t, like):
        return t.reshape(like.shape)

    x = _L0_conv_ref(x, L0_conv_wq, L0_conv_bq, L0_conv_wk, L0_conv_bk, L0_conv_wv, L0_conv_bv, L0_conv_wo, L0_conv_bo, L0_conv_ln1_g, L0_conv_ln1_b, L0_conv_w1, L0_conv_b1, L0_conv_w2, L0_conv_b2, L0_conv_ln2_g, L0_conv_ln2_b)
    t = _to_tokens(x)
    t = t + _L1_attn_ref(_ln_t(t), L1_attn_fwd_in_proj, L1_attn_fwd_conv_w, L1_attn_fwd_conv_b, L1_attn_fwd_A_log, L1_attn_fwd_dt_bias, L1_attn_fwd_D, L1_attn_fwd_norm_w, L1_attn_fwd_out_proj, L1_attn_bwd_in_proj, L1_attn_bwd_conv_w, L1_attn_bwd_conv_b, L1_attn_bwd_A_log, L1_attn_bwd_dt_bias, L1_attn_bwd_D, L1_attn_bwd_norm_w, L1_attn_bwd_out_proj)
    t = t + _L1_ffn_ref(_ln_t(t), L1_ffn_gate_w, L1_ffn_gate_b, L1_ffn_weight1, L1_ffn_weight2)
    x = _from_tokens(t, x)
    return x


_drawn_inputs = setup_inputs


def setup_inputs(seed=0):
    import zlib

    import numpy as np

    out = dict(_drawn_inputs(seed))
    spreads = {'L0_conv_bq': (0.0, 2.0),
     'L0_conv_bk': (0.0, 2.0),
     'L0_conv_bv': (0.0, 0.1),
     'L0_conv_bo': (0.0, 0.361),
     'L0_conv_ln1_g': (1.0, 0.2),
     'L0_conv_ln1_b': (0.0, 0.1),
     'L0_conv_b1': (0.0, 0.1),
     'L0_conv_b2': (0.0, 0.1),
     'L0_conv_ln2_g': (1.0, 0.2),
     'L0_conv_ln2_b': (0.0, 0.1),
     'L1_attn_fwd_conv_b': (0.0, 0.1),
     'L1_attn_fwd_D': (1.0, 0.2),
     'L1_attn_fwd_norm_w': (1.0, 0.2),
     'L1_attn_bwd_conv_b': (0.0, 0.1),
     'L1_attn_bwd_D': (1.0, 0.2),
     'L1_attn_bwd_norm_w': (1.0, 0.2),
     'L1_ffn_gate_b': (0.0, 0.8)}
    factors = {'L0_conv_wq': 8.0,
     'L0_conv_wk': 8.0,
     'L1_attn_fwd_A_log': 8.0,
     'L1_attn_fwd_dt_bias': 4.473,
     'L1_attn_bwd_A_log': 8.0,
     'L1_attn_bwd_dt_bias': 6.066,
     'L1_ffn_gate_w': 8.0,
     'L1_ffn_weight1': 8.0,
     'L1_ffn_weight2': 8.0}
    for name, (base, spread) in spreads.items():
        noise = np.random.default_rng([zlib.crc32(name.encode()), seed]).standard_normal(out[name].shape)
        drawn = base * np.exp(spread * noise) if base else spread * noise
        out[name] = jnp.asarray(drawn.astype(out[name].dtype))
    for name, factor in factors.items():
        out[name] = (out[name] * factor).astype(out[name].dtype)
    return out
```

```python
from contextlib import ExitStack

import concourse.bass as bass
from concourse import mybir

F32 = mybir.dt.float32
ALU = mybir.AluOpType
ACT = mybir.ActivationFunctionType
AX = mybir.AxisListType

P = 128
B, L, F, C = 8, 64, 16, 128
T = L * F
TILES = T // P
ALL = B * TILES
H = 8
FF = 512
FC = FF // P
GROUP = 4
GROUPS = ALL // GROUP
EPS = 1e-5
SLOT = 3 * P + 2

D_INNER, D_STATE, HEADS, HEAD = 256, 64, 4, 64
CONV = D_INNER + 2 * D_STATE
TAPS = 4
HALO = TAPS - 1
IN_PROJ = 2 * D_INNER + 2 * D_STATE + HEADS
DIRS = ("fwd", "bwd")

E = 64
TOP = 8


def transpose(nc, out, in_, ident):
    return nc.tensor.transpose(out, in_, ident)


def semaphores(nc, ctx, pre=""):
    taken = []

    def clear(*_):
        numbers = sorted(s.num for s in taken)
        with nc.Block() as block:
            @block.gpsimd
            def _(pool):
                first = 0
                for i in range(1, len(numbers) + 1):
                    if i == len(numbers) or numbers[i] != numbers[i - 1] + 1:
                        pool.sem_clear(range(numbers[first], numbers[i - 1] + 1))
                        first = i

    def sem(name):
        taken.append(hold.enter_context(nc.semaphore(pre + name)))
        return taken[-1]
    hold = ctx.enter_context(ExitStack())
    ctx.callback(clear)
    return sem


def setup(nc, d, k):
    with ExitStack() as ctx:
        sb = lambda name, shape: ctx.enter_context(nc.sbuf_tensor(name, shape, F32))
        sem = semaphores(nc, ctx)
        x_in = sb("s_x_in", [P, 2, GROUP, C])
        x_t = sb("s_x_t", [P, 2, GROUP * P])
        w_qkv = sb("s_w_qkv", [P, 3, H, C])
        w_o = sb("s_w_o", [P, H * C])
        wo_t = sb("s_wo_t", [P, H, P])
        b_v = sb("s_b_v", [P, H])
        b_vb = sb("s_b_vb", [P, H, P])
        b_qk = sb("s_b_qk", [P, 2, H])
        b_o = sb("s_b_o", [P, C])
        ones = sb("s_ones", [P, P])
        ps_x = ctx.enter_context(nc.psum_tensor("s_ps_x", [P, 2, 512], F32))
        ps_w = ctx.enter_context(nc.psum_tensor("s_ps_w", [P, 2, 512], F32))
        ps_b = ctx.enter_context(nc.psum_tensor("s_ps_b", [P, 512], F32))
        blank, masks = sem("blank"), sem("masks")
        x_loaded = [sem("x_loaded0"), sem("x_loaded1")]
        x_turned, x_copied = sem("x_turned"), sem("x_copied")
        x_stored = [sem("x_stored0"), sem("x_stored1")]
        w_loaded, w_turned, w_copied = sem("w_loaded"), sem("w_turned"), sem("w_copied")
        vo_done, vo_copied = sem("vo_done"), sem("vo_copied")
        bias_scaled, bias_spread, bias_done, bias_added = sem("bias_scaled"), sem("bias_spread"), sem("bias_done"), sem("bias_added")
        block = ctx.enter_context(nc.Block())
        x_tiles = d["x"].rearrange("b l f c -> (b l f) c").rearrange("(g i p) c -> g p i c", i=GROUP, p=P)

        @block.sync
        def _(sp):
            for n, name in enumerate(("wq", "wk", "wv")):
                sp.dma_start(w_qkv[:, n], d["L0_conv_" + name].rearrange("(c h) d -> c h d", h=H)).then_inc(w_loaded, 16)
            sp.dma_start(w_o[:], d["L0_conv_wo"]).then_inc(w_loaded, 16)
            sp.dma_start(b_v[:], d["L0_conv_bv"].rearrange("(c h) -> c h", h=H)).then_inc(w_loaded, 16)
            sp.dma_start(b_qk[:, 0], d["L0_conv_bq"].rearrange("(c h) -> c h", h=H)).then_inc(w_loaded, 16)
            sp.dma_start(b_qk[:, 1], d["L0_conv_bk"].rearrange("(c h) -> c h", h=H)).then_inc(w_loaded, 16)
            sp.dma_start(b_o[:], d["L0_conv_bo"].rearrange("(a c) -> a c", a=1).to_broadcast([P, C])).then_inc(w_loaded, 16)
            for s in range(2):
                sp.dma_start(x_in[:, s], x_tiles[s]).then_inc(x_loaded[s], 16)
            with sp.Fori(1, GROUPS // 2) as i:
                for s in range(2):
                    sp.wait_ge(x_turned, 2 * i + s - 1)
                    sp.dma_start(x_in[:, s], x_tiles[2 * i + s]).then_inc(x_loaded[s], 16)

        @block.gpsimd
        def _(pool):
            pool.memset(k["ident"][:], 0.0).then_inc(blank, 1)
            pool.memset(ones[:], 1.0).then_inc(blank, 1)
            pool.memset(k["acc"][:], 0.0).then_inc(blank, 1)
            pool.wait_ge(blank, 3)
            pool.affine_select(out=k["ident"][:], in_=k["ident"][:], compare_op=ALU.not_equal, fill=1.0, base=0,
                               pattern=[[-1, P]], channel_multiplier=1).then_inc(masks, 1)
            for name, row, op in (("le", -1, ALU.is_ge), ("gt", 1, ALU.is_gt), ("ge", 1, ALU.is_ge), ("lt", -1, ALU.is_gt)):
                pool.affine_select(out=k[name][:], in_=ones[:], compare_op=op, fill=0.0, base=0,
                                   pattern=[[-row, P]], channel_multiplier=row).then_inc(masks, 1)
            pool.wait_ge(w_loaded, 16 * 8)
            pool.tensor_scalar(b_v[:], b_v[:], float(L), None, ALU.mult).then_inc(bias_scaled, 1)
            pool.wait_ge(bias_scaled, 1)
            pool.tensor_tensor(b_vb[:], ones[:, None, :].to_broadcast([P, H, P]),
                               b_v[:, :, None].to_broadcast([P, H, P]), ALU.mult).then_inc(bias_spread, 1)

        @block.tensor
        def _(pe):
            pe.wait_ge(masks, 5)
            pe.wait_ge(w_loaded, 16 * 8)
            for n in range(6):
                if n >= 2:
                    pe.wait_ge(w_copied, n - 1)
                for i in range(4):
                    h = 4 * (n % 2) + i
                    src = w_qkv[:, n // 2, h, :] if n < 4 else w_o[:, h::H]
                    last = transpose(nc, ps_w[:, n % 2, i * P:(i + 1) * P], src, k["ident"][:])
                last.then_inc(w_turned, 1)
            pe.wait_ge(w_copied, 6)
            for n in range(2):
                for i in range(4):
                    h = 4 * n + i
                    last = nc.tensor.matmul(ps_w[:, n, i * P:(i + 1) * P], w_qkv[:, 2, h, :], wo_t[:, h, :], start=True, stop=True)
                last.then_inc(vo_done, 1)
            pe.wait_ge(bias_spread, 1)
            for h in range(H):
                last = nc.tensor.matmul(ps_b[:, 0:C], b_vb[:, h, :], wo_t[:, h, :], start=(h == 0), stop=(h == H - 1))
            last.then_inc(bias_done, 1)

            def turn(n, g):
                pe.wait_ge(x_loaded[n], 16 * (g // 2 + 1) if isinstance(g, int) else 16 * g[0] + 16)
                for i in range(GROUP):
                    last = transpose(nc, ps_x[:, n, i * P:(i + 1) * P], x_in[:, n, i, :], k["ident"][:])
                last.then_inc(x_turned, 1)
            for s in range(2):
                turn(s, s)
            with pe.Fori(1, GROUPS // 2) as i:
                for s in range(2):
                    pe.wait_ge(x_copied, 2 * i + s - 1)
                    turn(s, (i,))

        @block.scalar
        def _(act):
            for n in range(6):
                act.wait_ge(w_turned, n + 1)
                heads = slice(4 * (n % 2), 4 * (n % 2) + 4)
                out = k["w_att"][:, heads, (n // 2) * P:(n // 2 + 1) * P] if n < 4 else wo_t[:, heads, :]
                nc.scalar.activation(out, ps_w[:, n % 2, :].rearrange("p (h c) -> p h c", h=4), ACT.Copy).then_inc(w_copied, 1)
            for n in range(2):
                act.wait_ge(vo_done, n + 1)
                nc.scalar.activation(k["w_att"][:, 4 * n:4 * n + 4, 2 * P:3 * P],
                                     ps_w[:, n, :].rearrange("p (h c) -> p h c", h=4), ACT.Copy).then_inc(vo_copied, 1)
            nc.scalar.activation(k["w_att"][:, :, 3 * P], b_qk[:, 0], ACT.Copy, scale=float(C) ** -0.5).then_inc(vo_copied, 1)
            nc.scalar.activation(k["w_att"][:, :, 3 * P + 1], b_qk[:, 1], ACT.Copy).then_inc(vo_copied, 1)

            def copy(s, i):
                if i is not None:
                    act.wait_ge(x_stored[s], 16 * i)
                act.wait_ge(x_turned, s + 1 if i is None else 2 * i + s + 1)
                nc.scalar.activation(x_t[:, s], ps_x[:, s, :], ACT.Copy).then_inc(x_copied, 1)
                at = s if i is None else 2 * i + s
                act.wait_ge(x_copied, at + 1)
                act.dma_start(d["x_t"][:, bass.ds(at * 512, 512)], x_t[:, s]).then_inc(x_stored[s], 16)
            copy(0, None)
            copy(1, None)
            with act.Fori(1, GROUPS // 2) as i:
                copy(0, i)
                copy(1, i)
            for s in range(2):
                act.wait_ge(x_stored[s], 16 * (GROUPS // 2))

        @block.vector
        def _(dve):
            dve.wait_ge(bias_done, 1)
            nc.vector.tensor_tensor(k["att_bias"][:], ps_b[:, 0:C], b_o[:], ALU.add).then_inc(bias_added, 1)
            dve.wait_ge(bias_added, 1)


def attention(nc, d, k, pairs=B * H // 2):
    QB = 8
    with ExitStack() as ctx:
        sb = lambda name, shape: ctx.enter_context(nc.sbuf_tensor(name, shape, F32))
        sem = semaphores(nc, ctx)
        ps = lambda name, shape: ctx.enter_context(nc.psum_tensor(name, shape, F32))
        xs, ws = sb("a_xs", [P, 2, T]), sb("a_ws", [P, 2, SLOT])
        q_t, k_t, v = sb("a_q_t", [P, 2, T]), sb("a_k_t", [P, 2, T]), sb("a_v", [P, 2, TILES, C])
        s = sb("a_s", [P, QB, T])
        top = sb("a_top", [P, 2, F])
        row_sum, row_inv = sb("a_row_sum", [P, 2, F]), sb("a_row_inv", [P, 2, F])
        col_sum, col_inv = sb("a_col_sum", [P, 2, L]), sb("a_col_inv", [P, 2, L])
        a_t = sb("a_a_t", [P, 2, TILES, P])
        ps_s, ps_t = ps("a_ps_s", [P, 2, T]), ps("a_ps_t", [P, 2, 512])
        ps_p, ps_z = ps("a_ps_p", [P, 512]), ps("a_ps_z", [P, 4, P])
        head_loaded = [sem("head_loaded0"), sem("head_loaded1")]
        projected, project_copied = sem("projected"), sem("project_copied")
        scored, maxed, shifted, exp1 = sem("scored"), sem("maxed"), sem("shifted"), sem("exp1")
        row_summed, row_inverted, scaled1, exp2 = sem("row_summed"), sem("row_inverted"), sem("scaled1"), sem("exp2")
        col_summed, col_inverted, scaled2 = sem("col_summed"), sem("col_inverted"), sem("scaled2")
        turned, turn_copied, weighted, added = sem("turned"), sem("turn_copied"), sem("weighted"), sem("added")
        block = ctx.enter_context(nc.Block())
        PROJ = 6
        AT = {0: 0, 1: 1, 2: 2, 3: 3, 5: 4, 6: 5}

        def heads(eng, head, tail):
            head(0, 0, True)
            head(1, 1, True)
            with eng.Fori(1, pairs) as i:
                head(2 * i, 0, False)
                head(2 * i + 1, 1, False)
            tail(2 * pairs)

        def lagged(n, par, j, lag, first):
            if first and 8 * n + j - lag < 0:
                return None, None
            return 8 * n + (j - lag), (8 * par + j - lag) % 16

        @block.sync
        def _(sp):
            def load(n, par, b, h):
                sp.dma_start(xs[:, par], d["x_t"][:, bass.ds(b * T, T)]).then_inc(head_loaded[par], 16)
                sp.dma_start(ws[:, par], k["w_att"][:, h, :]).then_inc(head_loaded[par], 16)
            load(0, 0, 0, 0)
            load(1, 1, 0, 1)
            with sp.Fori(1, pairs) as i:
                for par in range(2):
                    n = 2 * i + par
                    sp.wait_ge(projected, PROJ * (n - 1))
                    load(n, par, n // H, n % H)
            sp.wait_ge(projected, PROJ * (2 * pairs - 1))
            load(2 * pairs, 0, 0, 0)

        def project(pe, n, par, c):
            if c == 0:
                pe.wait_ge(head_loaded[par], 32 * (n // 2) + 32)
            if not isinstance(n, int) or PROJ * n + c > 0:
                pe.wait_ge(project_copied, PROJ * n + c)
            half = slice(512 * (c % 2), 512 * (c % 2) + 512)
            if c < 4:
                last = nc.tensor.matmul(ps_p[:], ws[:, par, (c // 2) * P:(c // 2 + 1) * P], xs[:, par, half], start=True, stop=True)
            else:
                for i in range(4):
                    at = (4 * (c - 4) + i) * P
                    last = nc.tensor.matmul(ps_p[:, i * P:(i + 1) * P], xs[:, par, at:at + P], ws[:, par, 2 * P:3 * P], start=True, stop=True)
            last.then_inc(projected, 1)

        @block.tensor
        def _(pe):
            def turn(t, u, half):
                if half == 0:
                    pe.wait_ge(scaled2, t + 1)
                if not isinstance(t, int) or t >= 1:
                    pe.wait_ge(turn_copied, 2 * t + half - 1)
                for i in range(4):
                    at = (4 * half + i) * P
                    last = transpose(nc, ps_t[:, half, i * P:(i + 1) * P], s[:, u % QB, at:at + P], k["ident"][:])
                last.then_inc(turned, 1)

            def weigh(t, u, four):
                pe.wait_ge(turn_copied, 2 * t + 2)
                if (not isinstance(t, int) or t >= 4) and u % 4 == 0:
                    pe.wait_ge(added, four)
                for i in range(TILES):
                    last = nc.tensor.matmul(ps_z[:, u % 4, :], a_t[:, u % 2, i, :], v[:, u // 8, i, :],
                                            start=(i == 0), stop=(i == TILES - 1))
                last.then_inc(weighted, 1)

            def head(n, par, first):
                for j in range(8):
                    t, u = lagged(n, par, j, 0, first)
                    if j == 0:
                        pe.wait_ge(project_copied, PROJ * (n + 1))
                    if not first or t >= 2:
                        pe.wait_ge(shifted, t - 1)
                    for half in range(2):
                        last = nc.tensor.matmul(ps_s[:, u % 2, half * 512:half * 512 + 512], q_t[:, par, j * P:(j + 1) * P],
                                                k_t[:, par, half * 512:half * 512 + 512], start=True, stop=True)
                    last.then_inc(scored, 1)
                    t5, u5 = lagged(n, par, j, 5, first)
                    if t5 is not None:
                        weigh(t5, u5, 2 * n + (j - 5) // 4)
                    t4, u4 = lagged(n, par, j, 4, first)
                    if t4 is not None:
                        turn(t4, u4, 0)
                        turn(t4, u4, 1)
                    if j in AT:
                        project(pe, n + 1, 1 - par, AT[j])

            for c in range(PROJ):
                project(pe, 0, 0, c)

            def tail(n):
                for j in range(5):
                    weigh(8 * n + j - 5, (j - 5) % 16, 2 * n + (j - 5) // 4)
                    if j < 4:
                        turn(8 * n + j - 4, (j - 4) % 16, 0)
                        turn(8 * n + j - 4, (j - 4) % 16, 1)
            heads(pe, head, tail)

        @block.scalar
        def _(act):
            def project_copy(n, par, c):
                act.wait_ge(projected, PROJ * n + c + 1)
                half = slice(512 * (c % 2), 512 * (c % 2) + 512)
                if c < 2:
                    i = nc.scalar.activation(q_t[:, par, half], ps_p[:], ACT.Identity, bias=ws[:, par, 3 * P:3 * P + 1], scale=float(C) ** -0.5)
                elif c < 4:
                    i = nc.scalar.activation(k_t[:, par, half], ps_p[:], ACT.Identity, bias=ws[:, par, 3 * P + 1:3 * P + 2])
                else:
                    at = 4 * (c - 4)
                    i = nc.scalar.activation(v[:, par, at:at + 4, :], ps_p[:].rearrange("p (i c) -> p i c", c=C), ACT.Copy)
                i.then_inc(project_copied, 1)

            def turn_copy(t, u):
                if not isinstance(t, int) or t >= 2:
                    act.wait_ge(weighted, t - 1)
                for half in range(2):
                    act.wait_ge(turned, 2 * t + half + 1)
                    nc.scalar.activation(a_t[:, u % 2, 4 * half:4 * half + 4, :], ps_t[:, half, :].rearrange("p (i q) -> p i q", q=P),
                                         ACT.Copy).then_inc(turn_copied, 1)

            def second(t, u):
                act.wait_ge(scaled1, t + 1)
                nc.scalar.activation(s[:, u % QB], s[:, u % QB], ACT.Exp).then_inc(exp2, 1)

            def head(n, par, first):
                for j in range(8):
                    t2, u2 = lagged(n, par, j, 2, first)
                    if t2 is not None:
                        second(t2, u2)
                    t4, u4 = lagged(n, par, j, 4, first)
                    if t4 is not None:
                        turn_copy(t4, u4)
                    t, u = lagged(n, par, j, 0, first)
                    act.wait_ge(shifted, t + 1)
                    nc.scalar.activation(s[:, u % QB], s[:, u % QB], ACT.Exp).then_inc(exp1, 1)
                    if j in AT:
                        project_copy(n + 1, 1 - par, AT[j])

            for c in range(PROJ):
                if c == 0:
                    act.wait_ge(head_loaded[0], 32)
                project_copy(0, 0, c)

            def tail(n):
                for j in range(4):
                    if j < 2:
                        second(8 * n + j - 2, (j - 2) % 16)
                    turn_copy(8 * n + j - 4, (j - 4) % 16)
            heads(act, head, tail)

        @block.gpsimd
        def _(pool):
            def rows(t, u):
                pool.wait_ge(row_inverted, t + 1)
                view = s[:, u % QB].rearrange("p (m g) -> p m g", g=F)
                pool.tensor_tensor(view, view, row_inv[:, u % 2, None, :].to_broadcast([P, L, F]), ALU.mult).then_inc(scaled1, 1)

            def columns(t, u):
                pool.wait_ge(col_inverted, t + 1)
                view = s[:, u % QB].rearrange("p (m g) -> p m g", g=F)
                pool.tensor_tensor(view, view, col_inv[:, u % 2, :, None].to_broadcast([P, L, F]), ALU.mult).then_inc(scaled2, 1)

            def head(n, par, first):
                for j in range(8):
                    t3, u3 = lagged(n, par, j, 3, first)
                    if t3 is not None:
                        columns(t3, u3)
                    t1, u1 = lagged(n, par, j, 1, first)
                    if t1 is not None:
                        rows(t1, u1)

            def tail(n):
                for j in range(3):
                    columns(8 * n + j - 3, (j - 3) % 16)
                    if j < 1:
                        rows(8 * n + j - 1, (j - 1) % 16)
            heads(pool, head, tail)

        @block.vector
        def _(dve):
            def columns(t, u):
                dve.wait_ge(exp2, t + 1)
                if not isinstance(t, int) or t >= 2:
                    dve.wait_ge(scaled2, t - 1)
                nc.vector.tensor_reduce(col_sum[:, u % 2], s[:, u % QB].rearrange("p (m g) -> p m g", g=F), AX.X, ALU.add).then_inc(col_summed, 1)
                dve.wait_ge(col_summed, t + 1)
                nc.vector.reciprocal(col_inv[:, u % 2], col_sum[:, u % 2]).then_inc(col_inverted, 1)

            def rows(t, u):
                dve.wait_ge(exp1, t + 1)
                if not isinstance(t, int) or t >= 2:
                    dve.wait_ge(scaled1, t - 1)
                nc.vector.tensor_reduce(row_sum[:, u % 2], s[:, u % QB].rearrange("p (m g) -> p g m", g=F), AX.X, ALU.add).then_inc(row_summed, 1)
                dve.wait_ge(row_summed, t + 1)
                nc.vector.reciprocal(row_inv[:, u % 2], row_sum[:, u % 2]).then_inc(row_inverted, 1)

            def add(t, u, n, four):
                dve.wait_ge(weighted, t + 1)
                at = (n // H) * TILES + (u % 8 - 3)
                out = k["acc"][:, bass.ds(at, 4), :]
                if not isinstance(t, int) or t >= 4:
                    dve.wait_ge(added, four)
                nc.vector.tensor_tensor(out, ps_z[:], out, ALU.add).then_inc(added, 1)

            def head(n, par, first):
                for j in range(8):
                    t6, u6 = lagged(n, par, j, 6, first)
                    if t6 is not None and u6 % 4 == 3:
                        add(t6, u6, n if j >= 6 else n - 1, 2 * n + (j - 6) // 4)
                    t, u = lagged(n, par, j, 0, first)
                    dve.wait_ge(scored, t + 1)
                    nc.vector.tensor_reduce(top[:, u % 2], ps_s[:, u % 2].rearrange("p (m g) -> p g m", g=F), AX.X, ALU.max).then_inc(maxed, 1)
                    t3, u3 = lagged(n, par, j, 3, first)
                    if t3 is not None:
                        columns(t3, u3)
                    dve.wait_ge(maxed, t + 1)
                    if not first or t >= QB:
                        dve.wait_ge(turned, 2 * (t - QB) + 2)
                    nc.vector.tensor_tensor(s[:, u % QB].rearrange("p (m g) -> p m g", g=F), ps_s[:, u % 2].rearrange("p (m g) -> p m g", g=F),
                                            top[:, u % 2, None, :].to_broadcast([P, L, F]), ALU.subtract).then_inc(shifted, 1)
                    t1, u1 = lagged(n, par, j, 1, first)
                    if t1 is not None:
                        rows(t1, u1)

            def tail(n):
                for j in range(6):
                    if j < 3:
                        columns(8 * n + j - 3, (j - 3) % 16)
                    if j < 1:
                        rows(8 * n + j - 1, (j - 1) % 16)
                    if (j - 6) % 4 == 3:
                        add(8 * n + j - 6, (j - 6) % 16, n - 1, 2 * n + (j - 6) // 4)
            heads(dve, head, tail)


def two_by_two(eng, count, step, depth):
    head = depth + depth % 2
    for n in range(head):
        step(n, n % 2, 0)
    with eng.Fori(head // 2, count // 2) as i:
        step(2 * i, 0, None)
        step(2 * i + 1, 1, None)
    for n in range(count, count + depth):
        step(n, n % 2, count)


def live(n, edge, lag, count):
    return edge is None or 0 <= n - lag < count


def past(n, k):
    return not isinstance(n, int) or n >= k


def feed_forward(nc, d, k):
    with ExitStack() as ctx:
        sb = lambda name, shape: ctx.enter_context(nc.sbuf_tensor(name, shape, F32))
        sem = semaphores(nc, ctx)
        ps = lambda name, shape: ctx.enter_context(nc.psum_tensor(name, shape, F32))
        x = sb("f_x", [P, 2, GROUP, C])
        z = sb("f_z", [P, 2, GROUP, C])
        z_t, h_t = sb("f_z_t", [P, GROUP * P]), sb("f_h_t", [P, FC, GROUP * P])
        t, u, u_t = sb("f_t", [P, 2, GROUP, C]), sb("f_u", [P, 2, GROUP, C]), sb("f_u_t", [P, 2, GROUP * P])
        stats, mean_var = sb("f_stats", [P, 3, GROUP, 6]), sb("f_mean_var", [P, 3, GROUP, 2])
        rstd = sb("f_rstd", [P, 3, GROUP])
        w1, w2 = sb("f_w1", [P, FC, C]), sb("f_w2", [P, FC, P])
        w1_t, w2_t = sb("f_w1_t", [P, FC, P]), sb("f_w2_t", [P, FC, C])
        rows = sb("f_rows", [P, 5, C])
        b1, b1_rows = sb("f_b1", [P, FC]), sb("f_b1_rows", [FC, P])
        w_dt, b_dt = sb("f_w_dt", [P, 2 * HEADS]), sb("f_b_dt", [P, 2 * HEADS])
        zero, power, eps, pause = sb("f_zero", [P, B, HALO]), sb("f_power", [P, GROUP]), sb("f_eps", [P, GROUP]), sb("f_pause", [P, 1])
        ps_w, ps_z, ps_h = ps("f_ps_w", [P, 512]), ps("f_ps_z", [P, 512]), ps("f_ps_h", [P, 2, 512])
        ps_y, ps_u, ps_dt = ps("f_ps_y", [P, GROUP, C]), ps("f_ps_u", [P, 512]), ps("f_ps_dt", [P, GROUP, 2 * HEADS])
        w_loaded, w_turned, w_copied, constants = sem("f_w_loaded"), sem("f_w_turned"), sem("f_w_copied"), sem("f_constants")
        x_loaded = [sem("f_x_loaded0"), sem("f_x_loaded1")]
        summed, biased = sem("f_summed"), sem("f_biased")
        ln = [{s: sem(f"f_ln{n}_{s}") for s in ("stats", "aggr", "eps", "rstd", "unit", "gain", "done")} for n in range(3)]
        z_turned, z_copied, h_made, h_copied, y_made = sem("f_z_turned"), sem("f_z_copied"), sem("f_h_made"), sem("f_h_copied"), sem("f_y_made")
        y_summed, y_biased = sem("f_y_summed"), sem("f_y_biased")
        kept, u_turned, u_copied, dt_made, dt_kept = sem("f_kept"), sem("f_u_turned"), sem("f_u_copied"), sem("f_dt_made"), sem("f_dt_kept")
        u_stored, edges_stored = [sem("f_u_stored0"), sem("f_u_stored1")], sem("f_edges_stored")
        block = ctx.enter_context(nc.Block())
        x_tiles = d["x"].rearrange("b l f c -> (b l f) c").rearrange("(g i p) c -> g p i c", i=GROUP, p=P)
        BO, G1, B1, G2, B2 = range(5)
        WLOADS = 5 + 3 + 4
        row = lambda name: d["L0_conv_" + name].rearrange("(a c) -> a c", a=1).to_broadcast([P, C])

        @block.sync
        def _(sp):
            for i, name in enumerate(("b2", "ln1_g", "ln1_b", "ln2_g", "ln2_b")):
                sp.dma_start(rows[:, i], row(name)).then_inc(w_loaded, 16)
            sp.dma_start(w1[:], d["L0_conv_w1"].rearrange("(j p) c -> p j c", p=P)).then_inc(w_loaded, 16)
            sp.dma_start(w2[:], d["L0_conv_w2"].rearrange("c (j p) -> c j p", p=P)).then_inc(w_loaded, 16)
            sp.dma_start(b1_rows[:], d["L0_conv_b1"].rearrange("(j p) -> j p", p=P)).then_inc(w_loaded, 16)
            for i, name in enumerate(DIRS):
                sp.dma_start(w_dt[:, HEADS * i:HEADS * i + HEADS], d[f"L1_attn_{name}_in_proj"][:, IN_PROJ - HEADS:IN_PROJ]).then_inc(w_loaded, 16)
                sp.dma_start(b_dt[:, HEADS * i:HEADS * i + HEADS],
                             d[f"L1_attn_{name}_dt_bias"].rearrange("(a h) -> a h", a=1).to_broadcast([P, HEADS])).then_inc(w_loaded, 16)
            sp.wait_ge(constants, 2)
            sp.dma_start(d["u_t"][:, :, 0:HALO], zero[:]).then_inc(edges_stored, 16)
            sp.dma_start(d["u_t"][:, :, HALO + T:], zero[:]).then_inc(edges_stored, 16)

            def step(n, par, edge):
                if live(n, edge, 0, GROUPS):
                    if past(n, 2):
                        sp.wait_ge(summed, n - 1)
                    sp.dma_start(x[:, par], x_tiles[n]).then_inc(x_loaded[par], 16)
                if live(n, edge, 1, GROUPS):
                    sp.wait_ge(u_copied, n)
                    half = HALO + 512 * (1 - par)
                    sp.dma_start(d["u_t"][:, (n - 1) // 2, half:half + 512], u_t[:, 1 - par]).then_inc(u_stored[1 - par], 16)
            two_by_two(sp, GROUPS, step, 1)
            sp.wait_ge(edges_stored, 32)
            for par in range(2):
                sp.wait_ge(u_stored[par], 16 * (GROUPS // 2))

        @block.tensor
        def _(pe):
            pe.wait_ge(w_loaded, 16 * WLOADS)
            for j in range(FC):
                last = transpose(nc, ps_w[:, j * P:(j + 1) * P], w1[:, j, :], k["ident"][:])
            last.then_inc(w_turned, 1)
            pe.wait_ge(w_copied, 1)
            for j in range(FC):
                last = transpose(nc, ps_w[:, j * P:(j + 1) * P], w2[:, j, :], k["ident"][:])
            last.then_inc(w_turned, 1)
            pe.wait_ge(w_copied, 2)
            transpose(nc, ps_w[:, 0:FC], b1_rows[:], k["ident"][0:FC, 0:FC]).then_inc(w_turned, 1)

            def step(n, par, edge):
                if live(n, edge, 0, GROUPS):
                    pe.wait_ge(ln[0]["done"], n + 1)
                    if past(n, 1):
                        pe.wait_ge(z_copied, n)
                    for i in range(GROUP):
                        last = transpose(nc, ps_z[:, i * P:(i + 1) * P], z[:, par, i, :], k["ident"][:])
                    last.then_inc(z_turned, 1)
                    pe.wait_ge(z_copied, n + 1)
                    for j in range(FC):
                        if past(n, 1) or j >= 2:
                            pe.wait_ge(h_copied, FC * n + j - 1)
                        nc.tensor.matmul(ps_h[:, j % 2, :], w1_t[:, j, :], z_t[:], start=True, stop=True).then_inc(h_made, 1)
                    pe.wait_ge(h_copied, FC * n + FC)
                    if past(n, 1):
                        pe.wait_ge(y_summed, n)
                    for i in range(GROUP):
                        for j in range(FC):
                            last = nc.tensor.matmul(ps_y[:, i, :], h_t[:, j, i * P:(i + 1) * P], w2_t[:, j, :], start=(j == 0), stop=(j == FC - 1))
                    last.then_inc(y_made, 1)
                if live(n, edge, 1, GROUPS):
                    pe.wait_ge(ln[2]["unit"], n)
                    if past(n, 2):
                        pe.wait_ge(u_copied, n - 1)
                    for i in range(GROUP):
                        last = transpose(nc, ps_u[:, i * P:(i + 1) * P], u[:, 1 - par, i, :], k["ident"][:])
                    last.then_inc(u_turned, 1)
                    pe.wait_ge(u_copied, n)
                    if past(n, 2):
                        pe.wait_ge(dt_kept, n - 1)
                    for i in range(GROUP):
                        last = nc.tensor.matmul(ps_dt[:, i, :], u_t[:, 1 - par, i * P:(i + 1) * P], w_dt[:], start=True, stop=True)
                    last.then_inc(dt_made, 1)
            two_by_two(pe, GROUPS, step, 1)

        @block.scalar
        def _(act):
            act.wait_ge(w_turned, 1)
            nc.scalar.activation(w1_t[:].rearrange("p j c -> p (j c)"), ps_w[:], ACT.Copy).then_inc(w_copied, 1)
            act.wait_ge(w_turned, 2)
            nc.scalar.activation(w2_t[:].rearrange("p j c -> p (j c)"), ps_w[:], ACT.Copy).then_inc(w_copied, 1)
            act.wait_ge(w_turned, 3)
            nc.scalar.activation(b1[:], ps_w[:, 0:FC], ACT.Copy).then_inc(w_copied, 1)
            act.wait_ge(w_copied, 3)

            def step(n, par, edge):
                if live(n, edge, 0, GROUPS):
                    act.wait_ge(z_turned, n + 1)
                    if past(n, 1):
                        act.wait_ge(h_made, FC * n)
                    nc.scalar.activation(z_t[:], ps_z[:], ACT.Copy).then_inc(z_copied, 1)
                    if past(n, 1):
                        act.wait_ge(y_made, n)
                    for j in range(FC):
                        act.wait_ge(h_made, FC * n + j + 1)
                        nc.scalar.activation(h_t[:, j, :], ps_h[:, j % 2, :], ACT.Relu, bias=b1[:, j:j + 1]).then_inc(h_copied, 1)
                if live(n, edge, 1, GROUPS):
                    act.wait_ge(u_turned, n)
                    if past(n, 3):
                        act.wait_ge(dt_made, n - 2)
                        act.wait_ge(u_stored[1 - par], 16 * ((n - 1) // 2))
                    nc.scalar.activation(u_t[:, 1 - par], ps_u[:], ACT.Copy).then_inc(u_copied, 1)
            two_by_two(act, GROUPS, step, 1)

        @block.gpsimd
        def _(pool):
            pool.memset(power[:], -0.5).then_inc(constants, 1)
            pool.memset(zero[:], 0.0).then_inc(constants, 1)
            pool.memset(eps[:], EPS).then_inc(constants, 1)
            pool.wait_ge(constants, 3)

            def root(m, n):
                pool.wait_ge(ln[m]["aggr"], n + 1)
                pool.tensor_tensor(rstd[:, m], mean_var[:, m, :, 1], eps[:], ALU.add).then_inc(ln[m]["eps"], 1)
                pool.wait_ge(ln[m]["eps"], n + 1)
                pool.tensor_tensor(rstd[:, m], rstd[:, m], power[:], ALU.pow).then_inc(ln[m]["rstd"], 1)

            def step(n, par, edge):
                if live(n, edge, 0, GROUPS):
                    root(0, n)
                if live(n, edge, 1, GROUPS):
                    root(1, n - 1)
                    pool.wait_ge(ln[1]["done"], n)
                    pool.tensor_copy(k["acc"][:, bass.ds((n - 1) * GROUP, GROUP), :], t[:, 1 - par]).then_inc(kept, 1)
                    root(2, n - 1)
            two_by_two(pool, GROUPS, step, 1)

        @block.vector
        def _(dve):
            dve.wait_ge(w_loaded, 16 * WLOADS)

            def wide(r):
                return rows[:, r, None, :].to_broadcast([P, GROUP, C])

            def norm(m, n, a, out, gain):
                for i in range(GROUP):
                    last = nc.vector.bn_stats(stats[:, m, i, :], a[:, i, :])
                last.then_inc(ln[m]["stats"], 1)
                dve.wait_ge(ln[m]["stats"], n + 1)
                nc.vector.memset(pause[:], 0.0)
                for i in range(GROUP):
                    last = nc.vector.bn_aggr(mean_var[:, m, i, :], stats[:, m, i, :])
                last.then_inc(ln[m]["aggr"], 1)
                dve.wait_ge(ln[m]["rstd"], n + 1)
                for i in range(GROUP):
                    last = nc.vector.tensor_scalar(out[:, i, :], a[:, i, :], mean_var[:, m, i, 0:1], rstd[:, m, i:i + 1],
                                                   ALU.subtract, ALU.mult)
                last.then_inc(ln[m]["unit"], 1)
                if gain is None:
                    return
                dve.wait_ge(ln[m]["unit"], n + 1)
                nc.vector.tensor_tensor(out, out, wide(gain[0]), ALU.mult).then_inc(ln[m]["gain"], 1)
                dve.wait_ge(ln[m]["gain"], n + 1)
                nc.vector.tensor_tensor(out, out, wide(gain[1]), ALU.add).then_inc(ln[m]["done"], 1)

            def step(n, par, edge):
                if live(n, edge, 0, GROUPS):
                    dve.wait_ge(x_loaded[par], 16 * (n // 2 + 1))
                    if past(n, 1):
                        dve.wait_ge(z_turned, n)
                    nc.vector.tensor_tensor(z[:, par], x[:, par], k["acc"][:, bass.ds(n * GROUP, GROUP), :], ALU.add).then_inc(summed, 1)
                    dve.wait_ge(summed, n + 1)
                    nc.vector.tensor_tensor(z[:, par], z[:, par], k["att_bias"][:, None, :].to_broadcast([P, GROUP, C]), ALU.add).then_inc(biased, 1)
                    dve.wait_ge(biased, n + 1)
                    norm(0, n, z[:, par], z[:, par], (G1, B1))
                if live(n, edge, 1, GROUPS):
                    q = 1 - par
                    if past(n, 3):
                        dve.wait_ge(kept, n - 2)
                        dve.wait_ge(u_turned, n - 2)
                    dve.wait_ge(y_made, n)
                    nc.vector.tensor_tensor(t[:, q], ps_y[:], z[:, q], ALU.add).then_inc(y_summed, 1)
                    dve.wait_ge(y_summed, n)
                    nc.vector.tensor_tensor(t[:, q], t[:, q], wide(BO), ALU.add).then_inc(y_biased, 1)
                    dve.wait_ge(y_biased, n)
                    norm(1, n - 1, t[:, q], t[:, q], (G2, B2))
                    dve.wait_ge(ln[1]["done"], n)
                    norm(2, n - 1, t[:, q], u[:, q], None)
                    dve.wait_ge(dt_made, n)
                    nc.vector.tensor_tensor(k["dt"][:, bass.ds((n - 1) * GROUP, GROUP), :], ps_dt[:],
                                            b_dt[:, None, :].to_broadcast([P, GROUP, 2 * HEADS]), ALU.add).then_inc(dt_kept, 1)
            two_by_two(dve, GROUPS, step, 1)


def scan(nc, d, k, side):
    fwd = side == 0
    name = "L1_attn_" + DIRS[side] + "_"
    inc, exc = (k["le"], k["gt"]) if fwd else (k["ge"], k["lt"])
    pre = f"m{side}_"
    HP = HEADS * HEAD
    with ExitStack() as ctx:
        sb = lambda n, shape: ctx.enter_context(nc.sbuf_tensor(pre + n, shape, F32))
        sem = semaphores(nc, ctx, pre)
        ps = lambda n, shape: ctx.enter_context(nc.psum_tensor(pre + n, shape, F32))
        in_proj, conv_w = sb("in_proj", [P, IN_PROJ]), sb("conv_w", [P, CONV, TAPS])
        w_conv, rows = sb("w_conv", [P, TAPS, CONV]), sb("rows", [5, P])
        cols, half_b = sb("cols", [P, 5]), sb("half_b", [P, 3])
        w_out_in, w_out = sb("w_out_in", [P, 2, C]), sb("w_out", [P, 2, C])
        a_log, a_pos, skip = sb("a_log", [P, HEADS]), sb("a_pos", [P, HEADS]), sb("skip", [P, HEADS])
        ones, power, eps = sb("ones", [P, P]), sb("power", [P, 1]), sb("eps", [P, 1])
        size, soft = sb("size", [P, ALL, HEADS]), sb("soft", [P, ALL, HEADS])
        dt, da = sb("dt", [P, ALL * HEADS]), sb("da", [P, ALL * HEADS])
        since, until = sb("since", [P, ALL * HEADS]), sb("until", [P, ALL * HEADS])
        whole = sb("whole", [D_STATE, ALL * HEADS])
        u_t = sb("u_t", [P, 2, P + 2 * HALO])
        gate_c, gate_z = sb("gate_c", [P, 3, P]), sb("gate_z", [P, D_INNER])
        x_t = sb("x_t", [P, 2, 2, P])
        b_t, c_t = sb("b_t", [D_STATE, 2, P]), sb("c_t", [D_STATE, 2, P])
        silu_z = sb("silu_z", [P, 2, D_INNER])
        spread, decay = sb("spread", [P, 2, HEADS, P]), sb("decay", [P, 2, HEADS, P])
        bc, weight = sb("bc", [P, 2, P]), sb("weight", [P, 2, HEADS, P])
        b_n = sb("b_n", [P, 2, D_STATE])
        x_dt, x_until, x_skip = sb("x_dt", [P, 2, HP]), sb("x_until", [P, 2, HP]), sb("x_skip", [P, 2, HP])
        state, faded = sb("state", [D_STATE, B * HP]), sb("faded", [D_STATE, 2, HP])
        y0, y1, y2, y3 = sb("y0", [P, 2, HP]), sb("y1", [P, 2, HP]), sb("y2", [P, 2, HP]), sb("y3", [P, 2, HP])
        square, mean, rstd = sb("square", [P, HP]), sb("mean", [P, 2]), sb("rstd", [P, 2])
        y_t = sb("y_t", [P, 2, P])
        ps_c, ps_z = ps("ps_c", [P, 3, P]), ps("ps_z", [P, 512])
        ps_n, ps_g, ps_l = ps("ps_n", [P, 512]), ps("ps_g", [P, 512]), ps("ps_l", [P, HEADS, P])
        ps_y, ps_s, ps_o = ps("ps_y", [P, 2, HP]), ps("ps_s", [P, 512]), ps("ps_o", [P, 512])
        w_loaded, const, rows_turned, rows_copied, taps_made = sem("w_loaded"), sem("const"), sem("rows_turned"), sem("rows_copied"), sem("taps_made")
        soft_step, dt_made, da_made, sums_made, sums_exp, steps_made = (sem("soft_step"), sem("dt_made"), sem("da_made"), sem("sums_made"),
                                                                         sem("sums_exp"), sem("steps_made"))
        u_loaded = [sem("u_loaded0"), sem("u_loaded1")]
        conv_made, z_made, conv_tanh, z_tanh = sem("conv_made"), sem("z_made"), sem("conv_tanh"), sem("z_tanh")
        conv_gate, z_gate, conv_done, z_done = sem("conv_gate"), sem("z_gate"), sem("conv_done"), sem("z_done")
        spread_made, decay_summed, decayed = sem("spread_made"), sem("decay_summed"), sem("decayed")
        x_turned, bc_made, bc_masked, x_scaled, weighted = sem("x_turned"), sem("bc_made"), sem("bc_masked"), sem("x_scaled"), sem("weighted")
        y_made, state_made, state_faded, state_done = sem("y_made"), sem("state_made"), sem("state_faded"), sem("state_done")
        y_since, y_summed, y_skipped, y_gated = sem("y_since"), sem("y_summed"), sem("y_skipped"), sem("y_gated")
        squared, averaged, rooted = sem("squared"), sem("averaged"), sem("rooted")
        y_turned, y_copied, out_made, out_added = sem("y_turned"), sem("y_copied"), sem("out_made"), sem("out_added")
        block = ctx.enter_context(nc.Block())
        ITEMS = B * TILES
        WLOADS = 7

        def where(n):
            return n % B, n // B if fwd else TILES - 1 - n // B

        def tile(n):
            b, c = where(n)
            return b * TILES + c

        def steps(eng, step):
            two_by_two(eng, ITEMS, step, 3)

        def heads4(v):
            return v.rearrange("p (h e) -> p h e", h=HEADS)

        def per_head(v, n):
            return v[:, bass.ds(tile(n) * HEADS, HEADS)][:, :, None]

        @block.sync
        def _(sp):
            sp.dma_start(in_proj[:], d[name + "in_proj"]).then_inc(w_loaded, 16)
            sp.dma_start(conv_w[:].rearrange("p c i -> p (c i)"),
                         d[name + "conv_w"].rearrange("(a c) i -> a (c i)", a=1).to_broadcast([P, CONV * TAPS])).then_inc(w_loaded, 16)
            sp.dma_start(rows[0:3], d[name + "conv_b"].rearrange("(j p) -> j p", p=P)).then_inc(w_loaded, 16)
            sp.dma_start(rows[3:5], d[name + "norm_w"].rearrange("(j p) -> j p", p=P)).then_inc(w_loaded, 16)
            sp.dma_start(w_out_in[:], d[name + "out_proj"].rearrange("(j p) c -> p j c", p=P)).then_inc(w_loaded, 16)
            sp.dma_start(a_log[:], d[name + "A_log"].rearrange("(a h) -> a h", a=1).to_broadcast([P, HEADS])).then_inc(w_loaded, 16)
            sp.dma_start(skip[:], d[name + "D"].rearrange("(a h) -> a h", a=1).to_broadcast([P, HEADS])).then_inc(w_loaded, 16)

            def step(n, par, edge):
                if live(n, edge, 0, ITEMS):
                    if past(n, 2):
                        sp.wait_ge(z_made, n - 1)
                    b, c = where(n)
                    sp.dma_start(u_t[:, par], d["u_t"].rearrange("p b t -> p (b t)")[:, bass.ds(b * (T + 2 * HALO) + c * P, P + 2 * HALO)]).then_inc(u_loaded[par], 16)
            steps(sp, step)

        @block.tensor
        def _(pe):
            pe.wait_ge(w_loaded, 16 * WLOADS)
            transpose(nc, ps_o[:, 0:5], rows[:], k["ident"][0:5, 0:5]).then_inc(rows_turned, 1)
            pe.wait_ge(da_made, 1)
            pe.wait_ge(const, 4)
            nc.tensor.matmul(ps_n[:, 0:ALL * HEADS], inc[:], da[:], start=True, stop=True).then_inc(sums_made, 1)
            nc.tensor.matmul(ps_g[:, 0:ALL * HEADS], exc[:], da[:], start=True, stop=True).then_inc(sums_made, 1)
            nc.tensor.matmul(ps_s[0:D_STATE, 0:ALL * HEADS], ones[:, 0:D_STATE], da[:], start=True, stop=True).then_inc(sums_made, 1)
            pe.wait_ge(rows_copied, 1)
            pe.wait_ge(taps_made, TAPS)
            pe.wait_ge(steps_made, 2)

            def step(n, par, edge):
                if live(n, edge, 3, ITEMS):
                    i, q = n - 3, 1 - par
                    pe.wait_ge(y_gated, i + 1)
                    if past(i, 1):
                        pe.wait_ge(out_added, i)
                    for j in range(2):
                        last = transpose(nc, ps_o[:, j * P:(j + 1) * P], y3[:, q, j * P:(j + 1) * P], k["ident"][:])
                    last.then_inc(y_turned, 1)
                    pe.wait_ge(y_copied, i + 1)
                    for j in range(2):
                        last = nc.tensor.matmul(ps_o[:, 2 * P:3 * P], y_t[:, j, :], w_out[:, j, :], start=(j == 0), stop=(j == 1))
                    last.then_inc(out_made, 1)
                if live(n, edge, 2, ITEMS):
                    i, q = n - 2, par
                    pe.wait_ge(weighted, i + 1)
                    pe.wait_ge(x_scaled, i + 1)
                    if past(i, 1):
                        pe.wait_ge(y_summed, i)
                    for h in range(HEADS):
                        nc.tensor.matmul(ps_y[:, 0, h * HEAD:(h + 1) * HEAD], weight[:, q, h, :], x_dt[:, q, h * HEAD:(h + 1) * HEAD], start=True, stop=True)
                    nc.tensor.matmul(ps_y[:, 1, :], c_t[:, q, :], state[:, bass.ds((i % B) * HP, HP)], start=True, stop=True).then_inc(y_made, 1)
                    if past(i, 1):
                        pe.wait_ge(state_done, i)
                    nc.tensor.matmul(ps_s[0:D_STATE, 0:HP], b_n[:, q, :], x_until[:, q, :], start=True, stop=True).then_inc(state_made, 1)
                if live(n, edge, 1, ITEMS):
                    i, q = n - 1, 1 - par
                    pe.wait_ge(conv_done, i + 1)
                    if past(i, 1):
                        pe.wait_ge(x_scaled, i)
                    for j in range(2):
                        transpose(nc, ps_n[:, j * P:(j + 1) * P], x_t[:, q, j, :], k["ident"][:])
                    transpose(nc, ps_n[:, 2 * P:2 * P + D_STATE], b_t[:, q, :], k["ident"][0:D_STATE, 0:D_STATE]).then_inc(x_turned, 1)
                    if past(i, 1):
                        pe.wait_ge(bc_masked, i)
                    nc.tensor.matmul(ps_g[:, 0:P], b_t[:, q, :], c_t[:, q, :], start=True, stop=True).then_inc(bc_made, 1)
                    pe.wait_ge(spread_made, i + 1)
                    if past(i, 1):
                        pe.wait_ge(decayed, i)
                    nc.tensor.matmul(ps_l[:].rearrange("p h l -> p (h l)"), exc[:], spread[:, q].rearrange("p h l -> p (h l)"), start=True, stop=True).then_inc(decay_summed, 1)
                if live(n, edge, 0, ITEMS):
                    pe.wait_ge(u_loaded[par], 16 * (n // 2 + 1))
                    if past(n, 1):
                        pe.wait_ge(conv_done, n)
                    for j in range(3):
                        for i in range(TAPS):
                            at = i if fwd else 2 * HALO - i
                            last = nc.tensor.matmul(ps_c[:, j, :], w_conv[:, i, j * P:(j + 1) * P], u_t[:, par, at:at + P], start=(i == 0), stop=(i == TAPS - 1))
                    last.then_inc(conv_made, 1)
                    if past(n, 1):
                        pe.wait_ge(z_done, n)
                    nc.tensor.matmul(ps_z[:, 0:D_INNER], u_t[:, par, HALO:HALO + P], in_proj[:, 0:D_INNER], start=True, stop=True).then_inc(z_made, 1)
            steps(pe, step)

        @block.scalar
        def _(act):
            raw = k["dt"][:, :, HEADS * side:HEADS * side + HEADS]
            nc.scalar.activation(size[:], raw, ACT.Abs).then_inc(soft_step, 1)
            act.wait_ge(soft_step, 1)
            nc.scalar.activation(soft[:], size[:], ACT.Exp, scale=-1.0).then_inc(soft_step, 1)
            act.wait_ge(soft_step, 2)
            nc.scalar.activation(size[:], soft[:], ACT.Ln, bias=1.0).then_inc(soft_step, 1)
            act.wait_ge(w_loaded, 16 * WLOADS)
            nc.scalar.activation(a_pos[:], a_log[:], ACT.Exp).then_inc(soft_step, 1)
            act.wait_ge(rows_turned, 1)
            nc.scalar.activation(cols[:], ps_o[:, 0:5], ACT.Copy).then_inc(rows_copied, 1)
            act.wait_ge(rows_copied, 1)
            nc.scalar.activation(half_b[:], cols[:, 0:3], ACT.Copy, scale=0.5).then_inc(rows_copied, 1)
            act.wait_ge(rows_copied, 2)
            for i, (out, src) in enumerate(((since, ps_n), (until, ps_g), (whole, ps_s))):
                act.wait_ge(sums_made, i + 1)
                nc.scalar.activation(out[:], src[0:out.shape[0], 0:ALL * HEADS], ACT.Exp).then_inc(sums_exp, 1)
            act.wait_ge(sums_exp, 3)

            def step(n, par, edge):
                if live(n, edge, 3, ITEMS):
                    i = n - 3
                    act.wait_ge(y_turned, i + 1)
                    if past(i, 1):
                        act.wait_ge(out_made, i)
                    nc.scalar.activation(y_t[:].rearrange("p j l -> p (j l)"), ps_o[:, 0:2 * P], ACT.Copy).then_inc(y_copied, 1)
                if live(n, edge, 1, ITEMS):
                    i, q = n - 1, 1 - par
                    act.wait_ge(decay_summed, i + 1)
                    if past(i, 2):
                        act.wait_ge(weighted, i - 1)
                    nc.scalar.activation(decay[:, q], ps_l[:], ACT.Exp).then_inc(decayed, 1)
                if live(n, edge, 0, ITEMS):
                    act.wait_ge(conv_made, n + 1)
                    if past(n, 1):
                        act.wait_ge(conv_done, n)
                    for j in range(3):
                        last = nc.scalar.activation(gate_c[:, j, :], ps_c[:, j, :], ACT.Tanh, bias=half_b[:, j:j + 1], scale=0.5)
                    last.then_inc(conv_tanh, 1)
                    act.wait_ge(z_made, n + 1)
                    if past(n, 1):
                        act.wait_ge(z_done, n)
                    nc.scalar.activation(gate_z[:], ps_z[:, 0:D_INNER], ACT.Tanh, scale=0.5).then_inc(z_tanh, 1)
                if live(n, edge, 2, ITEMS):
                    i, q = n - 2, par
                    act.wait_ge(y_gated, i + 1)
                    if past(i, 2):
                        act.wait_ge(averaged, i - 1)
                    if past(i, 1):
                        act.wait_ge(squared, i)
                    nc.scalar.activation(square[:], y3[:, q], ACT.Square, scale=D_INNER ** -0.5, accum_out=mean[:, q:q + 1]).then_inc(squared, 1)
            steps(act, step)

        @block.gpsimd
        def _(pool):
            pool.memset(ones[:], 1.0).then_inc(const, 1)
            pool.memset(power[:], -0.5).then_inc(const, 1)
            pool.memset(state[:], 0.0).then_inc(const, 1)
            pool.memset(eps[:], EPS).then_inc(const, 1)
            pool.wait_ge(steps_made, 2)
            pool.wait_ge(const, 4)

            def step(n, par, edge):
                if live(n, edge, 2, ITEMS):
                    i, q = n - 2, par
                    pool.tensor_tensor(heads4(faded[:, q]), heads4(state[:, bass.ds((i % B) * HP, HP)]),
                                       per_head(whole, i).to_broadcast([D_STATE, HEADS, HEAD]), ALU.mult).then_inc(state_faded, 1)
                    pool.wait_ge(y_summed, i + 1)
                    pool.tensor_tensor(y2[:, q], y1[:, q], x_skip[:, q], ALU.add).then_inc(y_skipped, 1)
                    pool.wait_ge(y_skipped, i + 1)
                    if past(i, 2):
                        pool.wait_ge(squared, i - 1)
                        pool.wait_ge(y_turned, i - 1)
                    pool.tensor_tensor(y3[:, q], y2[:, q], silu_z[:, q], ALU.mult).then_inc(y_gated, 1)
                if live(n, edge, 0, ITEMS):
                    if past(n, 2):
                        pool.wait_ge(decay_summed, n - 1)
                    pool.tensor_tensor(spread[:, par], inc[:, None, :].to_broadcast([P, HEADS, P]),
                                       per_head(da, n).to_broadcast([P, HEADS, P]), ALU.mult).then_inc(spread_made, 1)
                if live(n, edge, 1, ITEMS):
                    i, q = n - 1, 1 - par
                    pool.wait_ge(decayed, i + 1)
                    pool.wait_ge(bc_masked, i + 1)
                    if past(i, 2):
                        pool.wait_ge(y_made, i - 1)
                    pool.tensor_tensor(weight[:, q], decay[:, q], bc[:, q, None, :].to_broadcast([P, HEADS, P]), ALU.mult).then_inc(weighted, 1)
                if live(n, edge, 2, ITEMS):
                    i, q = n - 2, par
                    pool.wait_ge(squared, i + 1)
                    if past(i, 2):
                        pool.wait_ge(out_added, i - 1)
                    pool.tensor_tensor(rstd[:, q:q + 1], mean[:, q:q + 1], eps[:], ALU.add).then_inc(averaged, 1)
                    pool.wait_ge(averaged, i + 1)
                    pool.tensor_tensor(rstd[:, q:q + 1], rstd[:, q:q + 1], power[:], ALU.pow).then_inc(rooted, 1)
            steps(pool, step)

        @block.vector
        def _(dve):
            dve.wait_ge(w_loaded, 16 * WLOADS)
            for i in range(TAPS):
                nc.vector.tensor_tensor(w_conv[:, i, :], in_proj[:, D_INNER:D_INNER + CONV], conv_w[:, :, i], ALU.mult).then_inc(taps_made, 1)
            dve.wait_ge(soft_step, 4)
            raw = k["dt"][:, :, HEADS * side:HEADS * side + HEADS]
            dt3, da3 = (v[:].rearrange("p (t h) -> p t h", h=HEADS) for v in (dt, da))
            nc.vector.scalar_tensor_tensor(out=dt3, in0=raw, scalar=0.0, in1=size[:], op0=ALU.max, op1=ALU.add).then_inc(dt_made, 1)
            dve.wait_ge(dt_made, 1)
            nc.vector.scalar_tensor_tensor(out=da3, in0=dt3, scalar=-1.0, in1=a_pos[:, None, :].to_broadcast([P, ALL, HEADS]),
                                           op0=ALU.mult, op1=ALU.mult).then_inc(da_made, 1)
            dve.wait_ge(rows_copied, 2)
            for j in range(2):
                last = nc.vector.tensor_scalar(w_out[:, j, :], w_out_in[:, j, :], cols[:, 3 + j:4 + j], None, ALU.mult)
            last.then_inc(steps_made, 1)
            dve.wait_ge(sums_exp, 3)
            nc.vector.tensor_tensor(until[:], until[:], dt[:], ALU.mult).then_inc(steps_made, 1)
            dve.wait_ge(steps_made, 2)

            def step(n, par, edge):
                if live(n, edge, 3, ITEMS):
                    i, q = n - 3, 1 - par
                    dve.wait_ge(out_made, i + 1)
                    dve.wait_ge(rooted, i + 1)
                    out = k["acc"][:].rearrange("p t c -> p (t c)")[:, bass.ds(tile(i) * C, C)]
                    nc.vector.scalar_tensor_tensor(out=out, in0=ps_o[:, 2 * P:3 * P], scalar=rstd[:, q:q + 1], in1=out,
                                                   op0=ALU.mult, op1=ALU.add).then_inc(out_added, 1)
                if live(n, edge, 2, ITEMS):
                    i, q = n - 2, par
                    dve.wait_ge(y_made, i + 1)
                    nc.vector.tensor_tensor(heads4(y0[:, q]), heads4(ps_y[:, 1, :]), per_head(since, i).to_broadcast([P, HEADS, HEAD]), ALU.mult).then_inc(y_since, 1)
                    dve.wait_ge(state_made, i + 1)
                    dve.wait_ge(state_faded, i + 1)
                    nc.vector.tensor_tensor(state[:, bass.ds((i % B) * HP, HP)], faded[:, q], ps_s[0:D_STATE, 0:HP], ALU.add).then_inc(state_done, 1)
                    dve.wait_ge(y_since, i + 1)
                    if past(i, 2):
                        dve.wait_ge(y_skipped, i - 1)
                    nc.vector.tensor_tensor(y1[:, q], ps_y[:, 0, :], y0[:, q], ALU.add).then_inc(y_summed, 1)
                if live(n, edge, 1, ITEMS):
                    i, q = n - 1, 1 - par
                    dve.wait_ge(bc_made, i + 1)
                    if past(i, 2):
                        dve.wait_ge(weighted, i - 1)
                    nc.vector.tensor_tensor(bc[:, q], ps_g[:, 0:P], inc[:], ALU.mult).then_inc(bc_masked, 1)
                    dve.wait_ge(x_turned, i + 1)
                    if past(i, 2):
                        dve.wait_ge(state_made, i - 1)
                        dve.wait_ge(y_skipped, i - 1)
                    for out, factor in ((x_dt, per_head(dt, i)), (x_until, per_head(until, i)), (x_skip, skip[:, :, None])):
                        nc.vector.tensor_tensor(heads4(out[:, q]), heads4(ps_n[:, 0:HP]), factor.to_broadcast([P, HEADS, HEAD]), ALU.mult)
                    nc.vector.tensor_copy(b_n[:, q], ps_n[:, 2 * P:2 * P + D_STATE]).then_inc(x_scaled, 1)
                if live(n, edge, 0, ITEMS):
                    dve.wait_ge(conv_tanh, n + 1)
                    nc.vector.tensor_scalar(gate_c[:], gate_c[:], 0.5, 0.5, ALU.mult, ALU.add).then_inc(conv_gate, 1)
                    dve.wait_ge(z_tanh, n + 1)
                    nc.vector.tensor_scalar(gate_z[:], gate_z[:], 0.5, 0.5, ALU.mult, ALU.add).then_inc(z_gate, 1)
                    dve.wait_ge(conv_gate, n + 1)
                    if past(n, 2):
                        dve.wait_ge(bc_made, n - 1)
                        dve.wait_ge(y_made, n - 1)
                    for j in range(2):
                        nc.vector.scalar_tensor_tensor(out=x_t[:, par, j, :], in0=ps_c[:, j, :], scalar=cols[:, j:j + 1], in1=gate_c[:, j, :],
                                                       op0=ALU.add, op1=ALU.mult)
                    for out, lo in ((b_t, 0), (c_t, D_STATE)):
                        rng = slice(lo, lo + D_STATE)
                        last = nc.vector.scalar_tensor_tensor(out=out[:, par], in0=ps_c[rng, 2, :], scalar=cols[rng, 2:3], in1=gate_c[rng, 2, :],
                                                              op0=ALU.add, op1=ALU.mult)
                    last.then_inc(conv_done, 1)
                    dve.wait_ge(z_gate, n + 1)
                    if past(n, 2):
                        dve.wait_ge(y_gated, n - 1)
                    nc.vector.tensor_tensor(silu_z[:, par], ps_z[:, 0:D_INNER], gate_z[:], ALU.mult).then_inc(z_done, 1)
            steps(dve, step)


def route(nc, d, k):
    with ExitStack() as ctx:
        sb = lambda name, shape: ctx.enter_context(nc.sbuf_tensor(name, shape, F32))
        sem = semaphores(nc, ctx)
        ps = lambda name, shape: ctx.enter_context(nc.psum_tensor(name, shape, F32))
        u, u_t = sb("r_u", [P, 2, GROUP, C]), sb("r_u_t", [P, 2, GROUP * P])
        stats, mean_var, rstd = sb("r_stats", [P, 2, GROUP, 6]), sb("r_mean_var", [P, 2, GROUP, 2]), sb("r_rstd", [P, 2, GROUP])
        gate_w, gate_t, gate_b = sb("r_gate_w", [E, C]), sb("r_gate_t", [C, E]), sb("r_gate_b", [P, 1])
        gate_row, ones, power = sb("r_gate_row", [1, 2 * E]), sb("r_ones", [1, 1]), sb("r_power", [P, GROUP])
        eps_row, pause = sb("r_eps_row", [P, GROUP]), sb("r_pause", [P, 1])
        prob, rest = sb("r_prob", [P, T]), sb("r_rest", [P, T])
        top, total, eight = sb("r_top", [P, 1]), sb("r_total", [P, 2]), sb("r_eight", [P, TOP])
        turned_c = sb("r_turned_c", [P, 2, 4, P])
        ps_w, ps_u, ps_r = ps("r_ps_w", [P, 512]), ps("r_ps_u", [P, 2, 512]), ps("r_ps_r", [P, 2, 512])
        ps_c, ps_p = ps("r_ps_c", [P, 2, 512]), ps("r_ps_p", [P, 4 * P])
        w_loaded, const, w_turned, w_copied = sem("r_w_loaded"), sem("r_const"), sem("r_w_turned"), sem("r_w_copied")
        seen, averaged, eps, rooted, normed, kept = sem("r_seen"), sem("r_averaged"), sem("r_eps"), sem("r_rooted"), sem("r_normed"), sem("r_kept")
        u_turned, u_copied, routed, biased = sem("r_u_turned"), sem("r_u_copied"), sem("r_routed"), sem("r_biased")
        maxed, exped, inverted, scaled, ranked, removed, chosen = (sem("r_maxed"), sem("r_exped"), sem("r_inverted"), sem("r_scaled"),
                                                                   sem("r_ranked"), sem("r_removed"), sem("r_chosen"))
        c_turned, c_copied, pooled, pool_copied = sem("r_c_turned"), sem("r_c_copied"), sem("r_pooled"), sem("r_pool_copied")
        block = ctx.enter_context(nc.Block())
        SETS = B // 2
        logits = k["chosen"]

        @block.sync
        def _(sp):
            sp.dma_start(gate_w[:], d["L1_ffn_gate_w"]).then_inc(w_loaded, 16)
            for i in range(2):
                sp.dma_start(gate_row[:, E * i:E * i + E], d["L1_ffn_gate_b"].rearrange("(a e) -> a e", a=1)).then_inc(w_loaded, 16)

        @block.tensor
        def _(pe):
            pe.wait_ge(w_loaded, 48)
            transpose(nc, ps_w[:, 0:E], gate_w[:], k["ident"][0:E, 0:E])
            pe.wait_ge(const, 3)
            nc.tensor.matmul(ps_w[:, E:E + 1], gate_row[:], ones[:], start=True, stop=True).then_inc(w_turned, 1)
            pe.wait_ge(w_copied, 2)

            def tokens(g, s, s_int):
                pe.wait_ge(normed, g + 1)
                if s_int or s >= 2:
                    pe.wait_ge(u_copied, g - 1)
                for i in range(GROUP):
                    last = transpose(nc, ps_u[:, s % 2, i * P:(i + 1) * P], u[:, s % 2, i, :], k["ident"][:])
                last.then_inc(u_turned, 1)
                pe.wait_ge(u_copied, g + 1)
                if s_int or s >= 2:
                    pe.wait_ge(biased, g - 1)
                rows = slice(E * (s // 2), E * (s // 2) + E)
                nc.tensor.matmul(ps_r[rows, s % 2, :], gate_t[:], u_t[:, s % 2, :], start=True, stop=True).then_inc(routed, 1)
            for s in range(4):
                tokens(s, s, False)
            with pe.Fori(1, SETS) as i:
                for s in range(4):
                    tokens(4 * i + s, s, True)
            for s in range(SETS):
                pe.wait_ge(chosen, s + 1)
                for half in range(2):
                    n = 2 * s + half
                    if n >= 2:
                        pe.wait_ge(c_copied, n - 1)
                    for i in range(4):
                        at = (4 * half + i) * P
                        last = transpose(nc, ps_c[:, half, i * P:(i + 1) * P], logits[:, s, at:at + P], k["ident"][:])
                    last.then_inc(c_turned, 1)
                pe.wait_ge(c_copied, 2 * s + 2)
                pe.wait_ge(kept, GROUPS)
                for b in range(2):
                    for i in range(TILES):
                        last = nc.tensor.matmul(ps_p[:, 2 * P * (s % 2) + E * b:2 * P * (s % 2) + E * b + E], k["u"][:, (2 * s + b) * TILES + i, :],
                                                turned_c[:, i // 4, i % 4, E * b:E * b + E], start=(i == 0), stop=(i == TILES - 1))
                last.then_inc(pooled, 1)
                pe.wait_ge(pool_copied, s + 1)

        @block.scalar
        def _(act):
            act.wait_ge(w_turned, 1)
            nc.scalar.activation(gate_t[:], ps_w[:, 0:E], ACT.Copy).then_inc(w_copied, 1)
            nc.scalar.activation(gate_b[:], ps_w[:, E:E + 1], ACT.Copy).then_inc(w_copied, 1)
            act.wait_ge(w_copied, 2)

            def tokens(g, s, s_int, i):
                act.wait_ge(u_turned, g + 1)
                if s_int or s >= 2:
                    act.wait_ge(routed, g - 1)
                nc.scalar.activation(u_t[:, s % 2], ps_u[:, s % 2, :], ACT.Copy).then_inc(u_copied, 1)
                act.wait_ge(routed, g + 1)
                rows = slice(E * (s // 2), E * (s // 2) + E)
                out = logits[:].rearrange("p s t -> p (s t)")[rows, bass.ds(i * T + 512 * (s % 2), 512)]
                nc.scalar.activation(out, ps_r[rows, s % 2, :], ACT.Identity, bias=gate_b[rows, :]).then_inc(biased, 1)
            for s in range(4):
                tokens(s, s, False, 0)
            with act.Fori(1, SETS) as i:
                for s in range(4):
                    tokens(4 * i + s, s, True, i)
            for s in range(SETS):
                act.wait_ge(maxed, s + 1)
                if s >= 1:
                    act.wait_ge(chosen, s)
                nc.scalar.activation(prob[:], logits[:, s, :], ACT.Exp, bias=top[:], accum_out=total[:, 0:1]).then_inc(exped, 1)
                if s >= 1:
                    act.wait_ge(pooled, s)
                for half in range(2):
                    act.wait_ge(c_turned, 2 * s + half + 1)
                    nc.scalar.activation(turned_c[:, half].rearrange("p i e -> p (i e)"), ps_c[:, half, :], ACT.Copy).then_inc(c_copied, 1)
                act.wait_ge(pooled, s + 1)
                for b in range(2):
                    at = 2 * P * (s % 2) + E * b
                    last = nc.scalar.activation(k["pooled"][:, :, 2 * s + b], ps_p[:, at:at + E], ACT.Copy)
                last.then_inc(pool_copied, 1)

        @block.gpsimd
        def _(pool):
            pool.memset(power[:], -0.5).then_inc(const, 1)
            pool.memset(ones[:], 1.0).then_inc(const, 1)
            pool.memset(eps_row[:], EPS).then_inc(const, 1)
            pool.wait_ge(const, 3)

            def step(n, par, edge):
                if live(n, edge, 0, GROUPS):
                    pool.wait_ge(averaged, n + 1)
                    pool.tensor_tensor(rstd[:, par], mean_var[:, par, :, 1], eps_row[:], ALU.add).then_inc(eps, 1)
                    pool.wait_ge(eps, n + 1)
                    pool.tensor_tensor(rstd[:, par], rstd[:, par], power[:], ALU.pow).then_inc(rooted, 1)
                if live(n, edge, 1, GROUPS):
                    pool.wait_ge(normed, n)
                    pool.tensor_copy(k["u"][:, bass.ds((n - 1) * GROUP, GROUP), :], u[:, 1 - par]).then_inc(kept, 1)
            two_by_two(pool, GROUPS, step, 1)

        @block.vector
        def _(dve):
            def step(n, par, edge):
                if live(n, edge, 0, GROUPS):
                    if past(n, 2):
                        dve.wait_ge(averaged, n - 1)
                        dve.wait_ge(normed, n - 1)
                    for i in range(GROUP):
                        at = (n * GROUP + i) * C
                        last = nc.vector.bn_stats(stats[:, par, i, :], k["acc"][:].rearrange("p t c -> p (t c)")[:, bass.ds(at, C)])
                    last.then_inc(seen, 1)
                    dve.wait_ge(seen, n + 1)
                    nc.vector.memset(pause[:], 0.0)
                    for i in range(GROUP):
                        last = nc.vector.bn_aggr(mean_var[:, par, i, :], stats[:, par, i, :])
                    last.then_inc(averaged, 1)
                if live(n, edge, 1, GROUPS):
                    q, m = 1 - par, n - 1
                    dve.wait_ge(rooted, m + 1)
                    if past(m, 2):
                        dve.wait_ge(kept, m - 1)
                        dve.wait_ge(u_turned, m - 1)
                    for i in range(GROUP):
                        at = (m * GROUP + i) * C
                        last = nc.vector.tensor_scalar(u[:, q, i, :], k["acc"][:].rearrange("p t c -> p (t c)")[:, bass.ds(at, C)],
                                                       mean_var[:, q, i, 0:1], rstd[:, q, i:i + 1], ALU.subtract, ALU.mult)
                    last.then_inc(normed, 1)
            two_by_two(dve, GROUPS, step, 1)
            dve.wait_ge(biased, GROUPS)
            for s in range(SETS):
                if s >= 1:
                    dve.wait_ge(exped, s)
                nc.vector.tensor_reduce(top[:], logits[:, s, :], AX.X, ALU.max, negate=True).then_inc(maxed, 1)
                dve.wait_ge(exped, s + 1)
                nc.vector.reciprocal(total[:, 1:2], total[:, 0:1]).then_inc(inverted, 1)
                dve.wait_ge(inverted, s + 1)
                nc.vector.tensor_scalar(prob[:], prob[:], total[:, 1:2], None, ALU.mult).then_inc(scaled, 1)
                dve.wait_ge(scaled, s + 1)
                nc.vector.max(eight[:], prob[:]).then_inc(ranked, 1)
                dve.wait_ge(ranked, s + 1)
                nc.vector.match_replace(rest[:], eight[:], prob[:], 0.0).then_inc(removed, 1)
                dve.wait_ge(removed, s + 1)
                nc.vector.tensor_tensor(logits[:, s, :], prob[:], rest[:], ALU.subtract).then_inc(chosen, 1)


def experts(nc, d, k):
    R = 8
    H1 = 4
    with ExitStack() as ctx:
        sb = lambda name, shape: ctx.enter_context(nc.sbuf_tensor(name, shape, F32))
        sem = semaphores(nc, ctx)
        ps = lambda name, shape: ctx.enter_context(nc.psum_tensor(name, shape, F32))
        w1, w2 = sb("e_w1", [P, R, H1, P]), sb("e_w2", [P, R, H1, C])
        b1_rows, b1, b2 = sb("e_b1_rows", [E, H1, P]), sb("e_b1", [P, E, H1]), sb("e_b2", [E, C])
        h_sum, h = sb("e_h_sum", [P, R, H1, B]), sb("e_h", [P, 2, R, H1, B])
        y_t, y = sb("e_y_t", [P, E, B]), sb("e_y", [P, B // 2, C])
        out = sb("e_out", [P, 4, 4, C])
        ps_b, ps_h, ps_y = ps("e_ps_b", [P, H1, P]), ps("e_ps_h", [P, 2, 2 * R * H1 * B]), ps("e_ps_y", [P, 512])
        ps_t, ps_o = ps("e_ps_t", [P, 512]), ps("e_ps_o", [P, 2, 4 * C])
        b_loaded, b_turned, b_copied = sem("e_b_loaded"), sem("e_b_turned"), sem("e_b_copied")
        w1_loaded = [sem(f"e_w1_loaded{r}") for r in range(R)]
        w2_loaded = [sem(f"e_w2_loaded{r}") for r in range(R)]
        h_made, h_biased, h_done, y_made, y_copied = sem("e_h_made"), sem("e_h_biased"), sem("e_h_done"), sem("e_y_made"), sem("e_y_copied")
        y_turned, y_biased, returned, summed = sem("e_y_turned"), sem("e_y_biased"), sem("e_returned"), sem("e_summed")
        stored = [sem(f"e_stored{i}") for i in range(4)]
        block = ctx.enter_context(nc.Block())
        w1_d, w2_d = d["L1_ffn_weight1"], d["L1_ffn_weight2"]
        out_tiles = d["out"].rearrange("b l f c -> (b l f) c").rearrange("(g i p) c -> g p i c", i=4, p=P)
        HID = H1 * P

        @block.sync
        def _(sp):
            sp.dma_start(b1_rows[:].rearrange("e j p -> e (j p)"), w1_d[:, C, :]).then_inc(b_loaded, 16)
            sp.dma_start(b2[:], w2_d[:, HID, :]).then_inc(b_loaded, 16)

            def load(e, r):
                sp.dma_start(w1[:, r].rearrange("p j q -> p (j q)"),
                             w1_d.rearrange("e c h -> (e c) h")[bass.ds(e * (C + 1), C), :]).then_inc(w1_loaded[r], 16)
                sp.dma_start(w2[:, r], w2_d.rearrange("e c h -> (e c) h")[bass.ds(e * (HID + 1), HID), :].rearrange("(j p) c -> p j c", p=P)).then_inc(w2_loaded[r], 16)
            for r in range(R):
                load(r, r)
            with sp.Fori(1, E // R) as i:
                for r in range(R):
                    sp.wait_ge(y_made, R * i + r - (R - 1))
                    load(R * i + r, r)
            for g in range(GROUPS):
                sp.wait_ge(summed, g + 1)
                sp.dma_start(out_tiles[g], out[:, g % 4]).then_inc(stored[g % 4], 16)
            for g in range(4):
                sp.wait_ge(stored[g], 16 * (GROUPS // 4))

        @block.tensor
        def _(pe):
            pe.wait_ge(b_loaded, 32)
            for j in range(H1):
                last = transpose(nc, ps_b[:, j, 0:E], b1_rows[:, j, :], k["ident"][0:E, 0:E])
            last.then_inc(b_turned, 1)

            def hidden(n, first):
                if not first:
                    pe.wait_ge(h_biased, n)
                for r in range(R):
                    pe.wait_ge(w1_loaded[r], 16 * n + 16)
                    for j in range(H1):
                        last = nc.tensor.matmul(ps_h[:, 0, (r * H1 + j) * B:(r * H1 + j + 1) * B], w1[:, r, j, :],
                                                k["pooled"][:].rearrange("p e b -> p (e b)")[:, bass.ds((n * R + r) * B, B)], start=True, stop=True)
                last.then_inc(h_made, 1)

            def outputs(n):
                pe.wait_ge(h_done, n + 1)
                if not isinstance(n, int) or n > 0:
                    pe.wait_ge(y_copied, n)
                for r in range(R):
                    pe.wait_ge(w2_loaded[r], 16 * n + 16)
                    for j in range(H1):
                        last = nc.tensor.matmul(ps_y[:, r * B:(r + 1) * B], w2[:, r, j, :], h[:, 0, r, j, :], start=(j == 0), stop=(j == H1 - 1))
                    last.then_inc(y_made, 1)
            hidden(0, True)
            outputs(0)
            with pe.Fori(1, E // R) as i:
                hidden(i, False)
                outputs(i)
            pe.wait_ge(y_copied, E // R)
            for b in range(B):
                if b >= 1:
                    pe.wait_ge(y_biased, b)
                transpose(nc, ps_t[0:E, 0:C], y_t[:, :, b], k["ident"][:]).then_inc(y_turned, 1)
            pe.wait_ge(y_biased, B)
            for g in range(GROUPS):
                if g >= 2:
                    pe.wait_ge(summed, g - 1)
                b = g // 2
                rows = slice(E * (b % 2), E * (b % 2) + E)
                for i in range(4):
                    at = (4 * (g % 2) + i) * P
                    last = nc.tensor.matmul(ps_o[:, g % 2, i * C:(i + 1) * C], k["chosen"][rows, b // 2, at:at + P], y[rows, b // 2, :], start=True, stop=True)
                last.then_inc(returned, 1)

        @block.scalar
        def _(act):
            act.wait_ge(b_turned, 1)
            nc.scalar.activation(b1[:].rearrange("p e j -> p j e"), ps_b[:, :, 0:E], ACT.Copy).then_inc(b_copied, 1)
            with act.Fori(0, E // R) as i:
                act.wait_ge(h_biased, i + 1)
                nc.scalar.activation(h[:, 0], h_sum[:], ACT.Gelu).then_inc(h_done, 1)
                act.wait_ge(y_made, R * i + R)
                nc.scalar.activation(y_t[:].rearrange("p e b -> p (e b)")[:, bass.ds(i * R * B, R * B)], ps_y[:, 0:R * B], ACT.Copy).then_inc(y_copied, 1)

        @block.vector
        def _(dve):
            dve.wait_ge(b_copied, 1)
            def biased(n, first):
                dve.wait_ge(h_made, n + 1)
                if not first:
                    dve.wait_ge(h_done, n)
                bias = b1[:].rearrange("p e j -> p (e j)")[:, bass.ds(n * R * H1, R * H1)]
                nc.vector.tensor_tensor(h_sum[:].rearrange("p r j b -> p (r j) b"), ps_h[:, 0, 0:R * H1 * B].rearrange("p (r b) -> p r b", b=B),
                                        bias[:, :, None].to_broadcast([P, R * H1, B]), ALU.add).then_inc(h_biased, 1)
            biased(0, True)
            with dve.Fori(1, E // R) as i:
                biased(i, False)
            for b in range(B):
                dve.wait_ge(y_turned, b + 1)
                rows = slice(E * (b % 2), E * (b % 2) + E)
                nc.vector.tensor_tensor(y[rows, b // 2, :], ps_t[0:E, 0:C], b2[:], ALU.add).then_inc(y_biased, 1)
            for g in range(GROUPS):
                dve.wait_ge(returned, g + 1)
                if g >= 4:
                    dve.wait_ge(stored[g % 4], 16 * (g // 4))
                nc.vector.tensor_tensor(out[:, g % 4], ps_o[:, g % 2, :].rearrange("p (i c) -> p i c", c=C), k["acc"][:, 4 * g:4 * g + 4, :], ALU.add).then_inc(summed, 1)


def hybrid(nc, d):
    with ExitStack() as ctx:
        k = {}

        def keep(name, shape):
            k[name] = ctx.enter_context(nc.sbuf_tensor(name, shape, F32))
        for name in ("ident", "le", "gt", "ge", "lt", "att_bias"):
            keep(name, [P, P])
        keep("acc", [P, ALL, C])
        keep("dt", [P, ALL, 2 * HEADS])
        with ExitStack() as early:
            k["w_att"] = early.enter_context(nc.sbuf_tensor("w_att", [P, H, SLOT], F32))
            setup(nc, d, k)
            attention(nc, d, k)
        feed_forward(nc, d, k)
        scan(nc, d, k, 0)
        scan(nc, d, k, 1)
        keep("chosen", [P, B // 2, T])
        keep("pooled", [P, E, B])
        with ExitStack() as late:
            k["u"] = late.enter_context(nc.sbuf_tensor("u", [P, ALL, C], F32))
            route(nc, d, k)
        experts(nc, d, k)


def kernel(**inputs):
    import numpy as np
    import concourse.bacc as bacc
    from concourse.bass_utils import run_bass_kernel_spmd as run

    nc = bacc.Bacc("TRN2", target_bir_lowering=False, num_devices=1)
    arrays, d = {}, {}
    for name, value in inputs.items():
        arrays["in_" + name] = a = np.ascontiguousarray(value)
        d[name] = nc.dram_tensor("in_" + name, a.shape, mybir.dt.from_np(a.dtype), kind="ExternalInput").ap()
    d["out"] = nc.dram_tensor("out", (B, L, F, C), F32, kind="ExternalOutput").ap()
    d["x_t"] = nc.dram_tensor("x_t", (P, ALL * P), F32, kind="Internal").ap()
    d["u_t"] = nc.dram_tensor("u_t", (P, B, T + 2 * HALO), F32, kind="Internal").ap()
    hybrid(nc, d)
    return run(nc, [arrays], core_ids=[0]).results[0]["out"]
```

```python
from contextlib import ExitStack

import concourse.bass as bass
from concourse import mybir

F32 = mybir.dt.float32
ALU = mybir.AluOpType
ACT = mybir.ActivationFunctionType
AX = mybir.AxisListType

P = 128
B, L, F, C = 8, 64, 16, 128
T = L * F
TILES = T // P
ALL = B * TILES
H = 8
FF = 512
FC = FF // P
GROUP = 4
GROUPS = ALL // GROUP
EPS = 1e-5
SLOT = 3 * P + 2

D_INNER, D_STATE, HEADS, HEAD = 256, 64, 4, 64
CONV = D_INNER + 2 * D_STATE
TAPS = 4
HALO = TAPS - 1
IN_PROJ = 2 * D_INNER + 2 * D_STATE + HEADS
DIRS = ("fwd", "bwd")

E = 64
TOP = 8


def transpose(nc, out, in_, ident):
    return nc.tensor.transpose(out, in_, ident)


def semaphores(nc, ctx, pre=""):
    taken = []

    def clear(*_):
        numbers = sorted(s.num for s in taken)
        with nc.Block() as block:
            @block.gpsimd
            def _(pool):
                first = 0
                for i in range(1, len(numbers) + 1):
                    if i == len(numbers) or numbers[i] != numbers[i - 1] + 1:
                        pool.sem_clear(range(numbers[first], numbers[i - 1] + 1))
                        first = i

    def sem(name):
        taken.append(hold.enter_context(nc.semaphore(pre + name)))
        return taken[-1]
    hold = ctx.enter_context(ExitStack())
    ctx.callback(clear)
    return sem


def setup(nc, d, k):
    with ExitStack() as ctx:
        sb = lambda name, shape: ctx.enter_context(nc.sbuf_tensor(name, shape, F32))
        sem = semaphores(nc, ctx)
        x_in = sb("s_x_in", [P, 2, GROUP, C])
        x_t = sb("s_x_t", [P, 2, GROUP * P])
        w_qkv = sb("s_w_qkv", [P, 3, H, C])
        w_o = sb("s_w_o", [P, H * C])
        wo_t = sb("s_wo_t", [P, H, P])
        b_v = sb("s_b_v", [P, H])
        b_vb = sb("s_b_vb", [P, H, P])
        b_qk = sb("s_b_qk", [P, 2, H])
        b_o = sb("s_b_o", [P, C])
        ones = sb("s_ones", [P, P])
        ps_x = ctx.enter_context(nc.psum_tensor("s_ps_x", [P, 2, 512], F32))
        ps_w = ctx.enter_context(nc.psum_tensor("s_ps_w", [P, 2, 512], F32))
        ps_b = ctx.enter_context(nc.psum_tensor("s_ps_b", [P, 512], F32))
        blank, masks = sem("blank"), sem("masks")
        x_loaded = [sem("x_loaded0"), sem("x_loaded1")]
        x_turned, x_copied = sem("x_turned"), sem("x_copied")
        x_stored = [sem("x_stored0"), sem("x_stored1")]
        w_loaded, w_turned, w_copied = sem("w_loaded"), sem("w_turned"), sem("w_copied")
        vo_done, vo_copied = sem("vo_done"), sem("vo_copied")
        bias_scaled, bias_spread, bias_done, bias_added = sem("bias_scaled"), sem("bias_spread"), sem("bias_done"), sem("bias_added")
        block = ctx.enter_context(nc.Block())
        x_tiles = d["x"].rearrange("b l f c -> (b l f) c").rearrange("(g i p) c -> g p i c", i=GROUP, p=P)

        @block.sync
        def _(sp):
            for n, name in enumerate(("wq", "wk", "wv")):
                sp.dma_start(w_qkv[:, n], d["L0_conv_" + name].rearrange("(c h) d -> c h d", h=H)).then_inc(w_loaded, 16)
            sp.dma_start(w_o[:], d["L0_conv_wo"]).then_inc(w_loaded, 16)
            sp.dma_start(b_v[:], d["L0_conv_bv"].rearrange("(c h) -> c h", h=H)).then_inc(w_loaded, 16)
            sp.dma_start(b_qk[:, 0], d["L0_conv_bq"].rearrange("(c h) -> c h", h=H)).then_inc(w_loaded, 16)
            sp.dma_start(b_qk[:, 1], d["L0_conv_bk"].rearrange("(c h) -> c h", h=H)).then_inc(w_loaded, 16)
            sp.dma_start(b_o[:], d["L0_conv_bo"].rearrange("(a c) -> a c", a=1).to_broadcast([P, C])).then_inc(w_loaded, 16)
            for s in range(2):
                sp.dma_start(x_in[:, s], x_tiles[s]).then_inc(x_loaded[s], 16)
            with sp.Fori(1, GROUPS // 2) as i:
                for s in range(2):
                    sp.wait_ge(x_turned, 2 * i + s - 1)
                    sp.dma_start(x_in[:, s], x_tiles[2 * i + s]).then_inc(x_loaded[s], 16)

        @block.gpsimd
        def _(pool):
            pool.memset(k["ident"][:], 0.0).then_inc(blank, 1)
            pool.memset(ones[:], 1.0).then_inc(blank, 1)
            pool.memset(k["acc"][:], 0.0).then_inc(blank, 1)
            pool.wait_ge(blank, 3)
            pool.affine_select(out=k["ident"][:], in_=k["ident"][:], compare_op=ALU.not_equal, fill=1.0, base=0,
                               pattern=[[-1, P]], channel_multiplier=1).then_inc(masks, 1)
            for name, row, op in (("le", -1, ALU.is_ge), ("gt", 1, ALU.is_gt), ("ge", 1, ALU.is_ge), ("lt", -1, ALU.is_gt)):
                pool.affine_select(out=k[name][:], in_=ones[:], compare_op=op, fill=0.0, base=0,
                                   pattern=[[-row, P]], channel_multiplier=row).then_inc(masks, 1)
            pool.wait_ge(w_loaded, 16 * 8)
            pool.tensor_scalar(b_v[:], b_v[:], float(L), None, ALU.mult).then_inc(bias_scaled, 1)
            pool.wait_ge(bias_scaled, 1)
            pool.tensor_tensor(b_vb[:], ones[:, None, :].to_broadcast([P, H, P]),
                               b_v[:, :, None].to_broadcast([P, H, P]), ALU.mult).then_inc(bias_spread, 1)

        @block.tensor
        def _(pe):
            pe.wait_ge(masks, 5)
            pe.wait_ge(w_loaded, 16 * 8)
            for n in range(6):
                if n >= 2:
                    pe.wait_ge(w_copied, n - 1)
                for i in range(4):
                    h = 4 * (n % 2) + i
                    src = w_qkv[:, n // 2, h, :] if n < 4 else w_o[:, h::H]
                    last = transpose(nc, ps_w[:, n % 2, i * P:(i + 1) * P], src, k["ident"][:])
                last.then_inc(w_turned, 1)
            pe.wait_ge(w_copied, 6)
            for n in range(2):
                for i in range(4):
                    h = 4 * n + i
                    last = nc.tensor.matmul(ps_w[:, n, i * P:(i + 1) * P], w_qkv[:, 2, h, :], wo_t[:, h, :], start=True, stop=True)
                last.then_inc(vo_done, 1)
            pe.wait_ge(bias_spread, 1)
            for h in range(H):
                last = nc.tensor.matmul(ps_b[:, 0:C], b_vb[:, h, :], wo_t[:, h, :], start=(h == 0), stop=(h == H - 1))
            last.then_inc(bias_done, 1)

            def turn(n, g):
                pe.wait_ge(x_loaded[n], 16 * (g // 2 + 1) if isinstance(g, int) else 16 * g[0] + 16)
                for i in range(GROUP):
                    last = transpose(nc, ps_x[:, n, i * P:(i + 1) * P], x_in[:, n, i, :], k["ident"][:])
                last.then_inc(x_turned, 1)
            for s in range(2):
                turn(s, s)
            with pe.Fori(1, GROUPS // 2) as i:
                for s in range(2):
                    pe.wait_ge(x_copied, 2 * i + s - 1)
                    turn(s, (i,))

        @block.scalar
        def _(act):
            for n in range(6):
                act.wait_ge(w_turned, n + 1)
                heads = slice(4 * (n % 2), 4 * (n % 2) + 4)
                out = k["w_att"][:, heads, (n // 2) * P:(n // 2 + 1) * P] if n < 4 else wo_t[:, heads, :]
                nc.scalar.activation(out, ps_w[:, n % 2, :].rearrange("p (h c) -> p h c", h=4), ACT.Copy).then_inc(w_copied, 1)
            for n in range(2):
                act.wait_ge(vo_done, n + 1)
                nc.scalar.activation(k["w_att"][:, 4 * n:4 * n + 4, 2 * P:3 * P],
                                     ps_w[:, n, :].rearrange("p (h c) -> p h c", h=4), ACT.Copy).then_inc(vo_copied, 1)
            nc.scalar.activation(k["w_att"][:, :, 3 * P], b_qk[:, 0], ACT.Copy, scale=float(C) ** -0.5).then_inc(vo_copied, 1)
            nc.scalar.activation(k["w_att"][:, :, 3 * P + 1], b_qk[:, 1], ACT.Copy).then_inc(vo_copied, 1)

            def copy(s, i):
                if i is not None:
                    act.wait_ge(x_stored[s], 16 * i)
                act.wait_ge(x_turned, s + 1 if i is None else 2 * i + s + 1)
                nc.scalar.activation(x_t[:, s], ps_x[:, s, :], ACT.Copy).then_inc(x_copied, 1)
                at = s if i is None else 2 * i + s
                act.wait_ge(x_copied, at + 1)
                act.dma_start(d["x_t"][:, bass.ds(at * 512, 512)], x_t[:, s]).then_inc(x_stored[s], 16)
            copy(0, None)
            copy(1, None)
            with act.Fori(1, GROUPS // 2) as i:
                copy(0, i)
                copy(1, i)
            for s in range(2):
                act.wait_ge(x_stored[s], 16 * (GROUPS // 2))

        @block.vector
        def _(dve):
            dve.wait_ge(bias_done, 1)
            nc.vector.tensor_tensor(k["att_bias"][:], ps_b[:, 0:C], b_o[:], ALU.add).then_inc(bias_added, 1)
            dve.wait_ge(bias_added, 1)


def attention(nc, d, k, pairs=B * H // 2):
    QB = 8
    with ExitStack() as ctx:
        sb = lambda name, shape: ctx.enter_context(nc.sbuf_tensor(name, shape, F32))
        sem = semaphores(nc, ctx)
        ps = lambda name, shape: ctx.enter_context(nc.psum_tensor(name, shape, F32))
        xs, ws = sb("a_xs", [P, 2, T]), sb("a_ws", [P, 2, SLOT])
        q_t, k_t, v = sb("a_q_t", [P, 2, T]), sb("a_k_t", [P, 2, T]), sb("a_v", [P, 2, TILES, C])
        s = sb("a_s", [P, QB, T])
        top = sb("a_top", [P, 2, F])
        row_sum, row_inv = sb("a_row_sum", [P, 2, F]), sb("a_row_inv", [P, 2, F])
        col_sum, col_inv = sb("a_col_sum", [P, 2, L]), sb("a_col_inv", [P, 2, L])
        a_t = sb("a_a_t", [P, 2, TILES, P])
        ps_s, ps_t = ps("a_ps_s", [P, 2, T]), ps("a_ps_t", [P, 2, 512])
        ps_p, ps_z = ps("a_ps_p", [P, 512]), ps("a_ps_z", [P, 4, P])
        head_loaded = [sem("head_loaded0"), sem("head_loaded1")]
        projected, project_copied = sem("projected"), sem("project_copied")
        scored, maxed, shifted, exp1 = sem("scored"), sem("maxed"), sem("shifted"), sem("exp1")
        row_summed, row_inverted, scaled1, exp2 = sem("row_summed"), sem("row_inverted"), sem("scaled1"), sem("exp2")
        col_summed, col_inverted, scaled2 = sem("col_summed"), sem("col_inverted"), sem("scaled2")
        turned, turn_copied, weighted, added = sem("turned"), sem("turn_copied"), sem("weighted"), sem("added")
        block = ctx.enter_context(nc.Block())
        PROJ = 6
        AT = {0: 0, 1: 1, 2: 2, 3: 3, 5: 4, 6: 5}

        def heads(eng, head, tail):
            head(0, 0, True)
            head(1, 1, True)
            with eng.Fori(1, pairs) as i:
                head(2 * i, 0, False)
                head(2 * i + 1, 1, False)
            tail(2 * pairs)

        def lagged(n, par, j, lag, first):
            if first and 8 * n + j - lag < 0:
                return None, None
            return 8 * n + (j - lag), (8 * par + j - lag) % 16

        @block.sync
        def _(sp):
            def load(n, par, b, h):
                sp.dma_start(xs[:, par], d["x_t"][:, bass.ds(b * T, T)]).then_inc(head_loaded[par], 16)
                sp.dma_start(ws[:, par], k["w_att"][:, h, :]).then_inc(head_loaded[par], 16)
            load(0, 0, 0, 0)
            load(1, 1, 0, 1)
            with sp.Fori(1, pairs) as i:
                for par in range(2):
                    n = 2 * i + par
                    sp.wait_ge(projected, PROJ * (n - 1))
                    load(n, par, n // H, n % H)
            sp.wait_ge(projected, PROJ * (2 * pairs - 1))
            load(2 * pairs, 0, 0, 0)

        def project(pe, n, par, c):
            if c == 0:
                pe.wait_ge(head_loaded[par], 32 * (n // 2) + 32)
            if not isinstance(n, int) or PROJ * n + c > 0:
                pe.wait_ge(project_copied, PROJ * n + c)
            half = slice(512 * (c % 2), 512 * (c % 2) + 512)
            if c < 4:
                last = nc.tensor.matmul(ps_p[:], ws[:, par, (c // 2) * P:(c // 2 + 1) * P], xs[:, par, half], start=True, stop=True)
            else:
                for i in range(4):
                    at = (4 * (c - 4) + i) * P
                    last = nc.tensor.matmul(ps_p[:, i * P:(i + 1) * P], xs[:, par, at:at + P], ws[:, par, 2 * P:3 * P], start=True, stop=True)
            last.then_inc(projected, 1)

        @block.tensor
        def _(pe):
            def turn(t, u, half):
                if half == 0:
                    pe.wait_ge(scaled2, t + 1)
                if not isinstance(t, int) or t >= 1:
                    pe.wait_ge(turn_copied, 2 * t + half - 1)
                for i in range(4):
                    at = (4 * half + i) * P
                    last = transpose(nc, ps_t[:, half, i * P:(i + 1) * P], s[:, u % QB, at:at + P], k["ident"][:])
                last.then_inc(turned, 1)

            def weigh(t, u, four):
                pe.wait_ge(turn_copied, 2 * t + 2)
                if (not isinstance(t, int) or t >= 4) and u % 4 == 0:
                    pe.wait_ge(added, four)
                for i in range(TILES):
                    last = nc.tensor.matmul(ps_z[:, u % 4, :], a_t[:, u % 2, i, :], v[:, u // 8, i, :],
                                            start=(i == 0), stop=(i == TILES - 1))
                last.then_inc(weighted, 1)

            def head(n, par, first):
                for j in range(8):
                    t, u = lagged(n, par, j, 0, first)
                    if j == 0:
                        pe.wait_ge(project_copied, PROJ * (n + 1))
                    if not first or t >= 2:
                        pe.wait_ge(shifted, t - 1)
                    for half in range(2):
                        last = nc.tensor.matmul(ps_s[:, u % 2, half * 512:half * 512 + 512], q_t[:, par, j * P:(j + 1) * P],
                                                k_t[:, par, half * 512:half * 512 + 512], start=True, stop=True)
                    last.then_inc(scored, 1)
                    t5, u5 = lagged(n, par, j, 5, first)
                    if t5 is not None:
                        weigh(t5, u5, 2 * n + (j - 5) // 4)
                    t4, u4 = lagged(n, par, j, 4, first)
                    if t4 is not None:
                        turn(t4, u4, 0)
                        turn(t4, u4, 1)
                    if j in AT:
                        project(pe, n + 1, 1 - par, AT[j])

            for c in range(PROJ):
                project(pe, 0, 0, c)

            def tail(n):
                for j in range(5):
                    weigh(8 * n + j - 5, (j - 5) % 16, 2 * n + (j - 5) // 4)
                    if j < 4:
                        turn(8 * n + j - 4, (j - 4) % 16, 0)
                        turn(8 * n + j - 4, (j - 4) % 16, 1)
            heads(pe, head, tail)

        @block.scalar
        def _(act):
            def project_copy(n, par, c):
                act.wait_ge(projected, PROJ * n + c + 1)
                half = slice(512 * (c % 2), 512 * (c % 2) + 512)
                if c < 2:
                    i = nc.scalar.activation(q_t[:, par, half], ps_p[:], ACT.Identity, bias=ws[:, par, 3 * P:3 * P + 1], scale=float(C) ** -0.5)
                elif c < 4:
                    i = nc.scalar.activation(k_t[:, par, half], ps_p[:], ACT.Identity, bias=ws[:, par, 3 * P + 1:3 * P + 2])
                else:
                    at = 4 * (c - 4)
                    i = nc.scalar.activation(v[:, par, at:at + 4, :], ps_p[:].rearrange("p (i c) -> p i c", c=C), ACT.Copy)
                i.then_inc(project_copied, 1)

            def turn_copy(t, u):
                if not isinstance(t, int) or t >= 2:
                    act.wait_ge(weighted, t - 1)
                for half in range(2):
                    act.wait_ge(turned, 2 * t + half + 1)
                    nc.scalar.activation(a_t[:, u % 2, 4 * half:4 * half + 4, :], ps_t[:, half, :].rearrange("p (i q) -> p i q", q=P),
                                         ACT.Copy).then_inc(turn_copied, 1)

            def second(t, u):
                act.wait_ge(scaled1, t + 1)
                nc.scalar.activation(s[:, u % QB], s[:, u % QB], ACT.Exp).then_inc(exp2, 1)

            def head(n, par, first):
                for j in range(8):
                    t2, u2 = lagged(n, par, j, 2, first)
                    if t2 is not None:
                        second(t2, u2)
                    t4, u4 = lagged(n, par, j, 4, first)
                    if t4 is not None:
                        turn_copy(t4, u4)
                    t, u = lagged(n, par, j, 0, first)
                    act.wait_ge(shifted, t + 1)
                    nc.scalar.activation(s[:, u % QB], s[:, u % QB], ACT.Exp).then_inc(exp1, 1)
                    if j in AT:
                        project_copy(n + 1, 1 - par, AT[j])

            for c in range(PROJ):
                if c == 0:
                    act.wait_ge(head_loaded[0], 32)
                project_copy(0, 0, c)

            def tail(n):
                for j in range(4):
                    if j < 2:
                        second(8 * n + j - 2, (j - 2) % 16)
                    turn_copy(8 * n + j - 4, (j - 4) % 16)
            heads(act, head, tail)

        @block.gpsimd
        def _(pool):
            def rows(t, u):
                pool.wait_ge(row_inverted, t + 1)
                view = s[:, u % QB].rearrange("p (m g) -> p m g", g=F)
                pool.tensor_tensor(view, view, row_inv[:, u % 2, None, :].to_broadcast([P, L, F]), ALU.mult).then_inc(scaled1, 1)

            def columns(t, u):
                pool.wait_ge(col_inverted, t + 1)
                view = s[:, u % QB].rearrange("p (m g) -> p m g", g=F)
                pool.tensor_tensor(view, view, col_inv[:, u % 2, :, None].to_broadcast([P, L, F]), ALU.mult).then_inc(scaled2, 1)

            def head(n, par, first):
                for j in range(8):
                    t3, u3 = lagged(n, par, j, 3, first)
                    if t3 is not None:
                        columns(t3, u3)
                    t1, u1 = lagged(n, par, j, 1, first)
                    if t1 is not None:
                        rows(t1, u1)

            def tail(n):
                for j in range(3):
                    columns(8 * n + j - 3, (j - 3) % 16)
                    if j < 1:
                        rows(8 * n + j - 1, (j - 1) % 16)
            heads(pool, head, tail)

        @block.vector
        def _(dve):
            def columns(t, u):
                dve.wait_ge(exp2, t + 1)
                if not isinstance(t, int) or t >= 2:
                    dve.wait_ge(scaled2, t - 1)
                nc.vector.tensor_reduce(col_sum[:, u % 2], s[:, u % QB].rearrange("p (m g) -> p m g", g=F), AX.X, ALU.add).then_inc(col_summed, 1)
                dve.wait_ge(col_summed, t + 1)
                nc.vector.reciprocal(col_inv[:, u % 2], col_sum[:, u % 2]).then_inc(col_inverted, 1)

            def rows(t, u):
                dve.wait_ge(exp1, t + 1)
                if not isinstance(t, int) or t >= 2:
                    dve.wait_ge(scaled1, t - 1)
                nc.vector.tensor_reduce(row_sum[:, u % 2], s[:, u % QB].rearrange("p (m g) -> p g m", g=F), AX.X, ALU.add).then_inc(row_summed, 1)
                dve.wait_ge(row_summed, t + 1)
                nc.vector.reciprocal(row_inv[:, u % 2], row_sum[:, u % 2]).then_inc(row_inverted, 1)

            def add(t, u, n, four):
                dve.wait_ge(weighted, t + 1)
                at = (n // H) * TILES + (u % 8 - 3)
                out = k["acc"][:, bass.ds(at, 4), :]
                if not isinstance(t, int) or t >= 4:
                    dve.wait_ge(added, four)
                nc.vector.tensor_tensor(out, ps_z[:], out, ALU.add).then_inc(added, 1)

            def head(n, par, first):
                for j in range(8):
                    t6, u6 = lagged(n, par, j, 6, first)
                    if t6 is not None and u6 % 4 == 3:
                        add(t6, u6, n if j >= 6 else n - 1, 2 * n + (j - 6) // 4)
                    t, u = lagged(n, par, j, 0, first)
                    dve.wait_ge(scored, t + 1)
                    nc.vector.tensor_reduce(top[:, u % 2], ps_s[:, u % 2].rearrange("p (m g) -> p g m", g=F), AX.X, ALU.max).then_inc(maxed, 1)
                    t3, u3 = lagged(n, par, j, 3, first)
                    if t3 is not None:
                        columns(t3, u3)
                    dve.wait_ge(maxed, t + 1)
                    if not first or t >= QB:
                        dve.wait_ge(turned, 2 * (t - QB) + 2)
                    nc.vector.tensor_tensor(s[:, u % QB].rearrange("p (m g) -> p m g", g=F), ps_s[:, u % 2].rearrange("p (m g) -> p m g", g=F),
                                            top[:, u % 2, None, :].to_broadcast([P, L, F]), ALU.subtract).then_inc(shifted, 1)
                    t1, u1 = lagged(n, par, j, 1, first)
                    if t1 is not None:
                        rows(t1, u1)

            def tail(n):
                for j in range(6):
                    if j < 3:
                        columns(8 * n + j - 3, (j - 3) % 16)
                    if j < 1:
                        rows(8 * n + j - 1, (j - 1) % 16)
                    if (j - 6) % 4 == 3:
                        add(8 * n + j - 6, (j - 6) % 16, n - 1, 2 * n + (j - 6) // 4)
            heads(dve, head, tail)


def two_by_two(eng, count, step, depth, unroll=2):
    head = -(-depth // unroll) * unroll
    for n in range(head):
        step(n, n % unroll, 0)
    with eng.Fori(head // unroll, count // unroll) as i:
        for u in range(unroll):
            step(unroll * i + u, u, None)
    for n in range(count, count + depth):
        step(n, n % unroll, count)


def live(n, edge, lag, count):
    return edge is None or 0 <= n - lag < count


def past(n, k):
    return not isinstance(n, int) or n >= k


def feed_forward(nc, d, k):
    S = 4
    DEPTH = 6
    with ExitStack() as ctx:
        sb = lambda name, shape: ctx.enter_context(nc.sbuf_tensor(name, shape, F32))
        sem = semaphores(nc, ctx)
        ps = lambda name, shape: ctx.enter_context(nc.psum_tensor(name, shape, F32))
        x = sb("f_x", [P, 2, GROUP, C])
        z, zb = sb("f_z", [P, S, GROUP, C]), sb("f_zb", [P, S, GROUP, C])
        z_t, h_t = sb("f_z_t", [P, GROUP * P]), sb("f_h_t", [P, FC, GROUP * P])
        t, u, u_t = sb("f_t", [P, S, GROUP, C]), sb("f_u", [P, 2, GROUP, C]), sb("f_u_t", [P, 2, GROUP * P])
        stats, mean_var = sb("f_stats", [P, 3, GROUP, 6]), sb("f_mean_var", [P, 2, 3, GROUP, 2])
        rstd = sb("f_rstd", [P, 2, 3 * GROUP])
        w1, w2 = sb("f_w1", [P, FC, C]), sb("f_w2", [P, FC, P])
        w1_t, w2_t = sb("f_w1_t", [P, FC, P]), sb("f_w2_t", [P, FC, C])
        rows = sb("f_rows", [P, 5, C])
        b1, b1_rows = sb("f_b1", [P, FC]), sb("f_b1_rows", [FC, P])
        w_dt, b_dt = sb("f_w_dt", [P, 2 * HEADS]), sb("f_b_dt", [P, 2 * HEADS])
        zero, pause = sb("f_zero", [P, B, HALO]), sb("f_pause", [P, 1])
        power, eps = sb("f_power", [P, 3 * GROUP]), sb("f_eps", [P, 3 * GROUP])
        ps_w, ps_z, ps_h = ps("f_ps_w", [P, 512]), ps("f_ps_z", [P, 512]), ps("f_ps_h", [P, 2, 512])
        ps_y, ps_u, ps_dt = ps("f_ps_y", [P, GROUP, C]), ps("f_ps_u", [P, 512]), ps("f_ps_dt", [P, GROUP, 2 * HEADS])
        w_loaded, w_turned, w_copied, constants = sem("f_w_loaded"), sem("f_w_turned"), sem("f_w_copied"), sem("f_constants")
        x_loaded = [sem("f_x_loaded0"), sem("f_x_loaded1")]
        x_biased, summed, y_summed = sem("f_x_biased"), sem("f_summed"), sem("f_y_summed")
        seen = [sem(f"f_seen{m}") for m in range(3)]
        averaged = [sem(f"f_averaged{m}") for m in range(3)]
        unit = [sem(f"f_unit{m}") for m in range(3)]
        eps_added, rooted = sem("f_eps_added"), sem("f_rooted")
        z_gained, z_done, zb_done, t_gained, t_done = sem("f_z_gained"), sem("f_z_done"), sem("f_zb_done"), sem("f_t_gained"), sem("f_t_done")
        z_turned, z_copied, h_made, h_copied, y_made = sem("f_z_turned"), sem("f_z_copied"), sem("f_h_made"), sem("f_h_copied"), sem("f_y_made")
        kept, u_turned, u_copied, dt_made, dt_kept = sem("f_kept"), sem("f_u_turned"), sem("f_u_copied"), sem("f_dt_made"), sem("f_dt_kept")
        u_stored, edges_stored = [sem("f_u_stored0"), sem("f_u_stored1")], sem("f_edges_stored")
        block = ctx.enter_context(nc.Block())
        x_tiles = d["x"].rearrange("b l f c -> (b l f) c").rearrange("(g i p) c -> g p i c", i=GROUP, p=P)
        BO, G1, B1, G2, B2 = range(5)
        WLOADS = 5 + 3 + 4
        row = lambda name: d["L0_conv_" + name].rearrange("(a c) -> a c", a=1).to_broadcast([P, C])

        def steps(eng, step):
            two_by_two(eng, GROUPS, step, DEPTH, S)

        def on(n, edge, lag):
            return live(n, edge, lag, GROUPS)

        @block.sync
        def _(sp):
            for i, name in enumerate(("b2", "ln1_g", "ln1_b", "ln2_g", "ln2_b")):
                sp.dma_start(rows[:, i], row(name)).then_inc(w_loaded, 16)
            sp.dma_start(w1[:], d["L0_conv_w1"].rearrange("(j p) c -> p j c", p=P)).then_inc(w_loaded, 16)
            sp.dma_start(w2[:], d["L0_conv_w2"].rearrange("c (j p) -> c j p", p=P)).then_inc(w_loaded, 16)
            sp.dma_start(b1_rows[:], d["L0_conv_b1"].rearrange("(j p) -> j p", p=P)).then_inc(w_loaded, 16)
            for i, name in enumerate(DIRS):
                sp.dma_start(w_dt[:, HEADS * i:HEADS * i + HEADS], d[f"L1_attn_{name}_in_proj"][:, IN_PROJ - HEADS:IN_PROJ]).then_inc(w_loaded, 16)
                sp.dma_start(b_dt[:, HEADS * i:HEADS * i + HEADS],
                             d[f"L1_attn_{name}_dt_bias"].rearrange("(a h) -> a h", a=1).to_broadcast([P, HEADS])).then_inc(w_loaded, 16)

            def step(n, s, edge):
                if on(n, edge, 0):
                    if past(n, 2):
                        sp.wait_ge(summed, n - 1)
                    sp.dma_start(x[:, s % 2], x_tiles[n]).then_inc(x_loaded[s % 2], 16)
                if on(n, edge, 6):
                    sp.wait_ge(u_copied, n - 5)
                    half = HALO + 512 * (s % 2)
                    sp.dma_start(d["u_t"][:, (n - 6) // 2, half:half + 512], u_t[:, s % 2]).then_inc(u_stored[s % 2], 16)
            steps(sp, step)
            sp.dma_start(d["u_t"][:, :, 0:HALO], zero[:]).then_inc(edges_stored, 16)
            sp.dma_start(d["u_t"][:, :, HALO + T:], zero[:]).then_inc(edges_stored, 16)
            sp.wait_ge(edges_stored, 32)
            for par in range(2):
                sp.wait_ge(u_stored[par], 16 * (GROUPS // 2))

        @block.tensor
        def _(pe):
            pe.wait_ge(w_loaded, 16 * WLOADS)
            for j in range(FC):
                last = transpose(nc, ps_w[:, j * P:(j + 1) * P], w1[:, j, :], k["ident"][:])
            last.then_inc(w_turned, 1)
            pe.wait_ge(w_copied, 1)
            for j in range(FC):
                last = transpose(nc, ps_w[:, j * P:(j + 1) * P], w2[:, j, :], k["ident"][:])
            last.then_inc(w_turned, 1)
            pe.wait_ge(w_copied, 2)
            transpose(nc, ps_w[:, 0:FC], b1_rows[:], k["ident"][0:FC, 0:FC]).then_inc(w_turned, 1)

            def step(n, s, edge):
                if on(n, edge, 6):
                    i, q = n - 6, s % 2
                    pe.wait_ge(unit[2], i + 1)
                    if past(i, 1):
                        pe.wait_ge(u_copied, i)
                    for j in range(GROUP):
                        last = transpose(nc, ps_u[:, j * P:(j + 1) * P], u[:, q, j, :], k["ident"][:])
                    last.then_inc(u_turned, 1)
                if on(n, edge, 2):
                    i, q = n - 2, (s - 2) % S
                    pe.wait_ge(z_done, i + 1)
                    if past(i, 1):
                        pe.wait_ge(z_copied, i)
                    for j in range(GROUP):
                        last = transpose(nc, ps_z[:, j * P:(j + 1) * P], z[:, q, j, :], k["ident"][:])
                    last.then_inc(z_turned, 1)
                    pe.wait_ge(z_copied, i + 1)
                    for j in range(FC):
                        if past(i, 1) or j >= 2:
                            pe.wait_ge(h_copied, FC * i + j - 1)
                        nc.tensor.matmul(ps_h[:, j % 2, :], w1_t[:, j, :], z_t[:], start=True, stop=True).then_inc(h_made, 1)
                    pe.wait_ge(h_copied, FC * i + FC)
                    if past(i, 1):
                        pe.wait_ge(y_summed, i)
                    for g in range(GROUP):
                        for j in range(FC):
                            last = nc.tensor.matmul(ps_y[:, g, :], h_t[:, j, g * P:(g + 1) * P], w2_t[:, j, :], start=(j == 0), stop=(j == FC - 1))
                    last.then_inc(y_made, 1)
                if on(n, edge, 6):
                    i, q = n - 6, s % 2
                    pe.wait_ge(u_copied, i + 1)
                    if past(i, 1):
                        pe.wait_ge(dt_kept, i)
                    for j in range(GROUP):
                        last = nc.tensor.matmul(ps_dt[:, j, :], u_t[:, q, j * P:(j + 1) * P], w_dt[:], start=True, stop=True)
                    last.then_inc(dt_made, 1)
            steps(pe, step)

        @block.scalar
        def _(act):
            act.wait_ge(w_turned, 1)
            nc.scalar.activation(w1_t[:].rearrange("p j c -> p (j c)"), ps_w[:], ACT.Copy).then_inc(w_copied, 1)
            act.wait_ge(w_turned, 2)
            nc.scalar.activation(w2_t[:].rearrange("p j c -> p (j c)"), ps_w[:], ACT.Copy).then_inc(w_copied, 1)
            act.wait_ge(w_turned, 3)
            nc.scalar.activation(b1[:], ps_w[:, 0:FC], ACT.Copy).then_inc(w_copied, 1)
            act.wait_ge(w_copied, 3)

            def step(n, s, edge):
                if on(n, edge, 6):
                    i, q = n - 6, s % 2
                    act.wait_ge(u_turned, i + 1)
                    if past(i, 2):
                        act.wait_ge(dt_made, i - 1)
                        act.wait_ge(u_stored[q], 16 * (i // 2))
                    nc.scalar.activation(u_t[:, q], ps_u[:], ACT.Copy).then_inc(u_copied, 1)
                if on(n, edge, 5):
                    i, q = n - 5, (s - 5) % S
                    act.wait_ge(t_done, i + 1)
                    nc.scalar.activation(k["acc"][:, bass.ds(i * GROUP, GROUP), :], t[:, q], ACT.Copy).then_inc(kept, 1)
                if on(n, edge, 2):
                    i = n - 2
                    act.wait_ge(z_turned, i + 1)
                    if past(i, 1):
                        act.wait_ge(h_made, FC * i)
                    nc.scalar.activation(z_t[:], ps_z[:], ACT.Copy).then_inc(z_copied, 1)
                    if past(i, 1):
                        act.wait_ge(y_made, i)
                    for j in range(FC):
                        act.wait_ge(h_made, FC * i + j + 1)
                        nc.scalar.activation(h_t[:, j, :], ps_h[:, j % 2, :], ACT.Relu, bias=b1[:, j:j + 1]).then_inc(h_copied, 1)
            steps(act, step)

        @block.gpsimd
        def _(pool):
            pool.memset(power[:], -0.5).then_inc(constants, 1)
            pool.memset(eps[:], EPS).then_inc(constants, 1)
            pool.memset(mean_var[:], 1.0).then_inc(constants, 1)
            pool.memset(zero[:], 0.0).then_inc(constants, 1)
            pool.wait_ge(w_loaded, 16 * WLOADS)
            pool.wait_ge(constants, 4)

            def wide(r):
                return rows[:, r, None, :].to_broadcast([P, GROUP, C])

            def step(n, s, edge):
                if on(n, edge, 0):
                    pool.wait_ge(x_loaded[s % 2], 16 * (n // 2 + 1))
                    pool.tensor_tensor(x[:, s % 2], x[:, s % 2], k["att_bias"][:, None, :].to_broadcast([P, GROUP, C]), ALU.add).then_inc(x_biased, 1)
                if edge is None or n >= 2:
                    for m, lag in enumerate((2, 4, 6)):
                        if on(n, edge, lag):
                            pool.wait_ge(averaged[m], n - lag + 1)
                    q = (s - 1) % 2
                    if past(n, 4):
                        for m, lag in enumerate((2, 4, 6)):
                            if on(n - 2, edge, lag) and past(n - 2, lag):
                                pool.wait_ge(unit[m], n - 2 - lag + 1)
                    pool.tensor_tensor(rstd[:, q], mean_var[:, q].rearrange("p m g v -> p (m g) v")[:, :, 1], eps[:], ALU.add).then_inc(eps_added, 1)
                    pool.wait_ge(eps_added, n - 1)
                    pool.tensor_tensor(rstd[:, q], rstd[:, q], power[:], ALU.pow).then_inc(rooted, 1)
                if on(n, edge, 4):
                    i, q = n - 4, (s - 4) % S
                    pool.wait_ge(unit[1], i + 1)
                    pool.tensor_tensor(t[:, q], t[:, q], wide(G2), ALU.mult).then_inc(t_gained, 1)
                if on(n, edge, 2):
                    i, q = n - 2, (s - 2) % S
                    pool.wait_ge(unit[0], i + 1)
                    pool.tensor_tensor(z[:, q], z[:, q], wide(G1), ALU.mult).then_inc(z_gained, 1)
                    pool.wait_ge(z_gained, i + 1)
                    pool.tensor_tensor(z[:, q], z[:, q], wide(B1), ALU.add).then_inc(z_done, 1)
                if on(n, edge, 4):
                    i, q = n - 4, (s - 4) % S
                    pool.wait_ge(t_gained, i + 1)
                    pool.tensor_tensor(t[:, q], t[:, q], wide(B2), ALU.add).then_inc(t_done, 1)
                if on(n, edge, 2):
                    i, q = n - 2, (s - 2) % S
                    pool.wait_ge(z_done, i + 1)
                    pool.tensor_tensor(zb[:, q], z[:, q], wide(BO), ALU.add).then_inc(zb_done, 1)
            steps(pool, step)

        @block.vector
        def _(dve):
            dve.wait_ge(w_loaded, 16 * WLOADS)
            dve.wait_ge(constants, 4)

            def statistics(m, n, i, s, a):
                if past(i, 1):
                    dve.wait_ge(averaged[m], i)
                for j in range(GROUP):
                    last = nc.vector.bn_stats(stats[:, m, j, :], a[:, j, :])
                last.then_inc(seen[m], 1)
                dve.wait_ge(seen[m], i + 1)
                if past(n, 3):
                    dve.wait_ge(rooted, n - 2)
                nc.vector.memset(pause[:], 0.0)
                for j in range(GROUP):
                    last = nc.vector.bn_aggr(mean_var[:, s % 2, m, j, :], stats[:, m, j, :])
                last.then_inc(averaged[m], 1)

            def normalize(m, n, i, s, a, out):
                dve.wait_ge(rooted, n - 1)
                q = (s - 1) % 2
                for j in range(GROUP):
                    r = m * GROUP + j
                    last = nc.vector.tensor_scalar(out[:, j, :], a[:, j, :], mean_var[:, q, m, j, 0:1], rstd[:, q, r:r + 1],
                                                   ALU.subtract, ALU.mult)
                last.then_inc(unit[m], 1)

            def step(n, s, edge):
                if on(n, edge, 2):
                    i, q = n - 2, (s - 2) % S
                    normalize(0, n, i, s, z[:, q], z[:, q])
                if on(n, edge, 4):
                    i, q = n - 4, (s - 4) % S
                    normalize(1, n, i, s, t[:, q], t[:, q])
                if on(n, edge, 6):
                    i, q = n - 6, (s - 6) % S
                    if past(i, 2):
                        dve.wait_ge(u_turned, i - 1)
                    normalize(2, n, i, s, t[:, q], u[:, s % 2])
                if on(n, edge, 5):
                    i, q = n - 5, (s - 5) % S
                    dve.wait_ge(t_done, i + 1)
                    statistics(2, n, i, s, t[:, q])
                if on(n, edge, 3):
                    i, q = n - 3, (s - 3) % S
                    dve.wait_ge(y_made, i + 1)
                    dve.wait_ge(zb_done, i + 1)
                    if past(i, S):
                        dve.wait_ge(kept, i - S + 1)
                        dve.wait_ge(unit[2], i - S + 1)
                    nc.vector.tensor_tensor(t[:, q], ps_y[:], zb[:, q], ALU.add).then_inc(y_summed, 1)
                    dve.wait_ge(y_summed, i + 1)
                    statistics(1, n, i, s, t[:, q])
                if on(n, edge, 1):
                    i, q = n - 1, (s - 1) % S
                    dve.wait_ge(x_biased, i + 1)
                    if past(i, S):
                        dve.wait_ge(z_turned, i - S + 1)
                        dve.wait_ge(zb_done, i - S + 1)
                    nc.vector.tensor_tensor(z[:, q], x[:, (s - 1) % 2], k["acc"][:, bass.ds(i * GROUP, GROUP), :], ALU.add).then_inc(summed, 1)
                    dve.wait_ge(summed, i + 1)
                    statistics(0, n, i, s, z[:, q])
                if on(n, edge, 6):
                    i = n - 6
                    dve.wait_ge(dt_made, i + 1)
                    nc.vector.tensor_tensor(k["dt"][:, bass.ds(i * GROUP, GROUP), :], ps_dt[:],
                                            b_dt[:, None, :].to_broadcast([P, GROUP, 2 * HEADS]), ALU.add).then_inc(dt_kept, 1)
            steps(dve, step)


def scan(nc, d, k, side):
    fwd = side == 0
    name = "L1_attn_" + DIRS[side] + "_"
    inc, exc = (k["le"], k["gt"]) if fwd else (k["ge"], k["lt"])
    pre = f"m{side}_"
    HP = HEADS * HEAD
    with ExitStack() as ctx:
        sb = lambda n, shape: ctx.enter_context(nc.sbuf_tensor(pre + n, shape, F32))
        sem = semaphores(nc, ctx, pre)
        ps = lambda n, shape: ctx.enter_context(nc.psum_tensor(pre + n, shape, F32))
        in_proj, conv_w = sb("in_proj", [P, IN_PROJ]), sb("conv_w", [P, CONV, TAPS])
        w_conv, rows = sb("w_conv", [P, TAPS, CONV]), sb("rows", [5, P])
        cols, half_b = sb("cols", [P, 5]), sb("half_b", [P, 3])
        w_out_in, w_out = sb("w_out_in", [P, 2, C]), sb("w_out", [P, 2, C])
        a_log, a_pos, skip = sb("a_log", [P, HEADS]), sb("a_pos", [P, HEADS]), sb("skip", [P, HEADS])
        ones, power, eps = sb("ones", [P, P]), sb("power", [P, 1]), sb("eps", [P, 1])
        size, soft = sb("size", [P, ALL, HEADS]), sb("soft", [P, ALL, HEADS])
        dt, da = sb("dt", [P, ALL * HEADS]), sb("da", [P, ALL * HEADS])
        since, until = sb("since", [P, ALL * HEADS]), sb("until", [P, ALL * HEADS])
        whole = sb("whole", [D_STATE, ALL * HEADS])
        u_t = sb("u_t", [P, 2, P + 2 * HALO])
        gate_c, gate_z = sb("gate_c", [P, 3, P]), sb("gate_z", [P, D_INNER])
        x_t = sb("x_t", [P, 2, 2, P])
        b_t, c_t = sb("b_t", [D_STATE, 2, P]), sb("c_t", [D_STATE, 2, P])
        silu_z = sb("silu_z", [P, 2, D_INNER])
        spread, decay = sb("spread", [P, 2, HEADS, P]), sb("decay", [P, 2, HEADS, P])
        bc, weight = sb("bc", [P, 2, P]), sb("weight", [P, 2, HEADS, P])
        b_n = sb("b_n", [P, 2, D_STATE])
        x_dt, x_until, x_skip = sb("x_dt", [P, 2, HP]), sb("x_until", [P, 2, HP]), sb("x_skip", [P, 2, HP])
        state, faded = sb("state", [D_STATE, B * HP]), sb("faded", [D_STATE, 2, HP])
        y0, y1, y2, y3 = sb("y0", [P, 2, HP]), sb("y1", [P, 2, HP]), sb("y2", [P, 2, HP]), sb("y3", [P, 2, HP])
        square, mean, rstd = sb("square", [P, HP]), sb("mean", [P, 2]), sb("rstd", [P, 2])
        y_t = sb("y_t", [P, 2, P])
        ps_c, ps_z = ps("ps_c", [P, 3, P]), ps("ps_z", [P, 512])
        ps_n, ps_g, ps_l = ps("ps_n", [P, 512]), ps("ps_g", [P, 512]), ps("ps_l", [P, HEADS, P])
        ps_y, ps_s, ps_o = ps("ps_y", [P, 2, HP]), ps("ps_s", [P, 512]), ps("ps_o", [P, 512])
        w_loaded, const, rows_turned, rows_copied, taps_made = sem("w_loaded"), sem("const"), sem("rows_turned"), sem("rows_copied"), sem("taps_made")
        soft_step, dt_made, da_made, sums_made, sums_exp, steps_made = (sem("soft_step"), sem("dt_made"), sem("da_made"), sem("sums_made"),
                                                                         sem("sums_exp"), sem("steps_made"))
        u_loaded = [sem("u_loaded0"), sem("u_loaded1")]
        conv_made, z_made, conv_tanh, z_tanh = sem("conv_made"), sem("z_made"), sem("conv_tanh"), sem("z_tanh")
        conv_gate, z_gate, conv_done, z_done = sem("conv_gate"), sem("z_gate"), sem("conv_done"), sem("z_done")
        spread_made, decay_summed, decayed = sem("spread_made"), sem("decay_summed"), sem("decayed")
        x_turned, bc_made, bc_masked, x_scaled, weighted = sem("x_turned"), sem("bc_made"), sem("bc_masked"), sem("x_scaled"), sem("weighted")
        y_made, state_made, state_faded, state_done = sem("y_made"), sem("state_made"), sem("state_faded"), sem("state_done")
        y_since, y_summed, y_skipped, y_gated = sem("y_since"), sem("y_summed"), sem("y_skipped"), sem("y_gated")
        squared, averaged, rooted = sem("squared"), sem("averaged"), sem("rooted")
        y_turned, y_copied, out_made, out_added = sem("y_turned"), sem("y_copied"), sem("out_made"), sem("out_added")
        block = ctx.enter_context(nc.Block())
        ITEMS = B * TILES
        WLOADS = 7

        def where(n):
            return n % B, n // B if fwd else TILES - 1 - n // B

        def tile(n):
            b, c = where(n)
            return b * TILES + c

        def steps(eng, step):
            two_by_two(eng, ITEMS, step, 3)

        def heads4(v):
            return v.rearrange("p (h e) -> p h e", h=HEADS)

        def per_head(v, n):
            return v[:, bass.ds(tile(n) * HEADS, HEADS)][:, :, None]

        @block.sync
        def _(sp):
            sp.dma_start(in_proj[:], d[name + "in_proj"]).then_inc(w_loaded, 16)
            sp.dma_start(conv_w[:].rearrange("p c i -> p (c i)"),
                         d[name + "conv_w"].rearrange("(a c) i -> a (c i)", a=1).to_broadcast([P, CONV * TAPS])).then_inc(w_loaded, 16)
            sp.dma_start(rows[0:3], d[name + "conv_b"].rearrange("(j p) -> j p", p=P)).then_inc(w_loaded, 16)
            sp.dma_start(rows[3:5], d[name + "norm_w"].rearrange("(j p) -> j p", p=P)).then_inc(w_loaded, 16)
            sp.dma_start(w_out_in[:], d[name + "out_proj"].rearrange("(j p) c -> p j c", p=P)).then_inc(w_loaded, 16)
            sp.dma_start(a_log[:], d[name + "A_log"].rearrange("(a h) -> a h", a=1).to_broadcast([P, HEADS])).then_inc(w_loaded, 16)
            sp.dma_start(skip[:], d[name + "D"].rearrange("(a h) -> a h", a=1).to_broadcast([P, HEADS])).then_inc(w_loaded, 16)

            def step(n, par, edge):
                if live(n, edge, 0, ITEMS):
                    if past(n, 2):
                        sp.wait_ge(z_made, n - 1)
                    b, c = where(n)
                    sp.dma_start(u_t[:, par], d["u_t"].rearrange("p b t -> p (b t)")[:, bass.ds(b * (T + 2 * HALO) + c * P, P + 2 * HALO)]).then_inc(u_loaded[par], 16)
            steps(sp, step)

        @block.tensor
        def _(pe):
            pe.wait_ge(w_loaded, 16 * WLOADS)
            transpose(nc, ps_o[:, 0:5], rows[:], k["ident"][0:5, 0:5]).then_inc(rows_turned, 1)
            pe.wait_ge(da_made, 1)
            pe.wait_ge(const, 4)
            nc.tensor.matmul(ps_n[:, 0:ALL * HEADS], inc[:], da[:], start=True, stop=True).then_inc(sums_made, 1)
            nc.tensor.matmul(ps_g[:, 0:ALL * HEADS], exc[:], da[:], start=True, stop=True).then_inc(sums_made, 1)
            nc.tensor.matmul(ps_s[0:D_STATE, 0:ALL * HEADS], ones[:, 0:D_STATE], da[:], start=True, stop=True).then_inc(sums_made, 1)
            pe.wait_ge(rows_copied, 1)
            pe.wait_ge(taps_made, TAPS)
            pe.wait_ge(steps_made, 2)

            def step(n, par, edge):
                if live(n, edge, 3, ITEMS):
                    i, q = n - 3, 1 - par
                    pe.wait_ge(y_gated, i + 1)
                    if past(i, 1):
                        pe.wait_ge(out_added, i)
                    for j in range(2):
                        last = transpose(nc, ps_o[:, j * P:(j + 1) * P], y3[:, q, j * P:(j + 1) * P], k["ident"][:])
                    last.then_inc(y_turned, 1)
                if live(n, edge, 2, ITEMS):
                    i, q = n - 2, par
                    pe.wait_ge(weighted, i + 1)
                    pe.wait_ge(x_scaled, i + 1)
                    if past(i, 1):
                        pe.wait_ge(y_summed, i)
                    for h in range(HEADS):
                        nc.tensor.matmul(ps_y[:, 0, h * HEAD:(h + 1) * HEAD], weight[:, q, h, :], x_dt[:, q, h * HEAD:(h + 1) * HEAD], start=True, stop=True)
                    nc.tensor.matmul(ps_y[:, 1, :], c_t[:, q, :], state[:, bass.ds((i % B) * HP, HP)], start=True, stop=True).then_inc(y_made, 1)
                    if past(i, 1):
                        pe.wait_ge(state_done, i)
                    nc.tensor.matmul(ps_s[0:D_STATE, 0:HP], b_n[:, q, :], x_until[:, q, :], start=True, stop=True).then_inc(state_made, 1)
                if live(n, edge, 3, ITEMS):
                    i = n - 3
                    pe.wait_ge(y_copied, i + 1)
                    for j in range(2):
                        last = nc.tensor.matmul(ps_o[:, 2 * P:3 * P], y_t[:, j, :], w_out[:, j, :], start=(j == 0), stop=(j == 1))
                    last.then_inc(out_made, 1)
                if live(n, edge, 1, ITEMS):
                    i, q = n - 1, 1 - par
                    pe.wait_ge(conv_done, i + 1)
                    if past(i, 1):
                        pe.wait_ge(x_scaled, i)
                    for j in range(2):
                        transpose(nc, ps_n[:, j * P:(j + 1) * P], x_t[:, q, j, :], k["ident"][:])
                    transpose(nc, ps_n[:, 2 * P:2 * P + D_STATE], b_t[:, q, :], k["ident"][0:D_STATE, 0:D_STATE]).then_inc(x_turned, 1)
                    if past(i, 1):
                        pe.wait_ge(bc_masked, i)
                    nc.tensor.matmul(ps_g[:, 0:P], b_t[:, q, :], c_t[:, q, :], start=True, stop=True).then_inc(bc_made, 1)
                    pe.wait_ge(spread_made, i + 1)
                    if past(i, 1):
                        pe.wait_ge(decayed, i)
                    nc.tensor.matmul(ps_l[:].rearrange("p h l -> p (h l)"), exc[:], spread[:, q].rearrange("p h l -> p (h l)"), start=True, stop=True).then_inc(decay_summed, 1)
                if live(n, edge, 0, ITEMS):
                    pe.wait_ge(u_loaded[par], 16 * (n // 2 + 1))
                    if past(n, 1):
                        pe.wait_ge(conv_done, n)
                    for j in range(3):
                        for i in range(TAPS):
                            at = i if fwd else 2 * HALO - i
                            last = nc.tensor.matmul(ps_c[:, j, :], w_conv[:, i, j * P:(j + 1) * P], u_t[:, par, at:at + P], start=(i == 0), stop=(i == TAPS - 1))
                    last.then_inc(conv_made, 1)
                    if past(n, 1):
                        pe.wait_ge(z_done, n)
                    nc.tensor.matmul(ps_z[:, 0:D_INNER], u_t[:, par, HALO:HALO + P], in_proj[:, 0:D_INNER], start=True, stop=True).then_inc(z_made, 1)
            steps(pe, step)

        @block.scalar
        def _(act):
            raw = k["dt"][:, :, HEADS * side:HEADS * side + HEADS]
            nc.scalar.activation(size[:], raw, ACT.Abs).then_inc(soft_step, 1)
            act.wait_ge(soft_step, 1)
            nc.scalar.activation(soft[:], size[:], ACT.Exp, scale=-1.0).then_inc(soft_step, 1)
            act.wait_ge(soft_step, 2)
            nc.scalar.activation(size[:], soft[:], ACT.Ln, bias=1.0).then_inc(soft_step, 1)
            act.wait_ge(w_loaded, 16 * WLOADS)
            nc.scalar.activation(a_pos[:], a_log[:], ACT.Exp).then_inc(soft_step, 1)
            act.wait_ge(rows_turned, 1)
            nc.scalar.activation(cols[:], ps_o[:, 0:5], ACT.Copy).then_inc(rows_copied, 1)
            act.wait_ge(rows_copied, 1)
            nc.scalar.activation(half_b[:], cols[:, 0:3], ACT.Copy, scale=0.5).then_inc(rows_copied, 1)
            act.wait_ge(rows_copied, 2)
            for i, (out, src) in enumerate(((since, ps_n), (until, ps_g), (whole, ps_s))):
                act.wait_ge(sums_made, i + 1)
                nc.scalar.activation(out[:], src[0:out.shape[0], 0:ALL * HEADS], ACT.Exp).then_inc(sums_exp, 1)
            act.wait_ge(sums_exp, 3)

            def step(n, par, edge):
                if live(n, edge, 3, ITEMS):
                    i, q = n - 3, 1 - par
                    act.wait_ge(y_turned, i + 1)
                    if past(i, 1):
                        act.wait_ge(out_made, i)
                    nc.scalar.activation(y_t[:].rearrange("p j l -> p (j l)"), ps_o[:, 0:2 * P], ACT.Copy).then_inc(y_copied, 1)
                    if past(i, 2):
                        act.wait_ge(averaged, i - 1)
                    if past(i, 1):
                        act.wait_ge(squared, i)
                    nc.scalar.activation(square[:], y3[:, q], ACT.Square, scale=D_INNER ** -0.5, accum_out=mean[:, q:q + 1]).then_inc(squared, 1)
                if live(n, edge, 1, ITEMS):
                    i, q = n - 1, 1 - par
                    act.wait_ge(decay_summed, i + 1)
                    if past(i, 2):
                        act.wait_ge(weighted, i - 1)
                    nc.scalar.activation(decay[:, q], ps_l[:], ACT.Exp).then_inc(decayed, 1)
                if live(n, edge, 0, ITEMS):
                    act.wait_ge(conv_made, n + 1)
                    if past(n, 1):
                        act.wait_ge(conv_done, n)
                    for j in range(3):
                        last = nc.scalar.activation(gate_c[:, j, :], ps_c[:, j, :], ACT.Tanh, bias=half_b[:, j:j + 1], scale=0.5)
                    last.then_inc(conv_tanh, 1)
                    act.wait_ge(z_made, n + 1)
                    if past(n, 1):
                        act.wait_ge(z_done, n)
                    nc.scalar.activation(gate_z[:], ps_z[:, 0:D_INNER], ACT.Tanh, scale=0.5).then_inc(z_tanh, 1)
            steps(act, step)

        @block.gpsimd
        def _(pool):
            pool.memset(ones[:], 1.0).then_inc(const, 1)
            pool.memset(power[:], -0.5).then_inc(const, 1)
            pool.memset(state[:], 0.0).then_inc(const, 1)
            pool.memset(eps[:], EPS).then_inc(const, 1)
            pool.wait_ge(steps_made, 2)
            pool.wait_ge(const, 4)

            def step(n, par, edge):
                if live(n, edge, 2, ITEMS):
                    i, q = n - 2, par
                    pool.tensor_tensor(heads4(faded[:, q]), heads4(state[:, bass.ds((i % B) * HP, HP)]),
                                       per_head(whole, i).to_broadcast([D_STATE, HEADS, HEAD]), ALU.mult).then_inc(state_faded, 1)
                    pool.wait_ge(y_summed, i + 1)
                    pool.tensor_tensor(y2[:, q], y1[:, q], x_skip[:, q], ALU.add).then_inc(y_skipped, 1)
                    pool.wait_ge(y_skipped, i + 1)
                    if past(i, 2):
                        pool.wait_ge(squared, i - 1)
                        pool.wait_ge(y_turned, i - 1)
                    pool.tensor_tensor(y3[:, q], y2[:, q], silu_z[:, q], ALU.mult).then_inc(y_gated, 1)
                if live(n, edge, 3, ITEMS):
                    i, q = n - 3, 1 - par
                    pool.wait_ge(squared, i + 1)
                    if past(i, 2):
                        pool.wait_ge(out_added, i - 1)
                    pool.tensor_tensor(rstd[:, q:q + 1], mean[:, q:q + 1], eps[:], ALU.add).then_inc(averaged, 1)
                    pool.wait_ge(averaged, i + 1)
                    pool.tensor_tensor(rstd[:, q:q + 1], rstd[:, q:q + 1], power[:], ALU.pow).then_inc(rooted, 1)
                if live(n, edge, 0, ITEMS):
                    if past(n, 2):
                        pool.wait_ge(decay_summed, n - 1)
                    pool.tensor_tensor(spread[:, par], inc[:, None, :].to_broadcast([P, HEADS, P]),
                                       per_head(da, n).to_broadcast([P, HEADS, P]), ALU.mult).then_inc(spread_made, 1)
                if live(n, edge, 1, ITEMS):
                    i, q = n - 1, 1 - par
                    pool.wait_ge(decayed, i + 1)
                    pool.wait_ge(bc_masked, i + 1)
                    if past(i, 2):
                        pool.wait_ge(y_made, i - 1)
                    pool.tensor_tensor(weight[:, q], decay[:, q], bc[:, q, None, :].to_broadcast([P, HEADS, P]), ALU.mult).then_inc(weighted, 1)
            steps(pool, step)

        @block.vector
        def _(dve):
            dve.wait_ge(w_loaded, 16 * WLOADS)
            for i in range(TAPS):
                nc.vector.tensor_tensor(w_conv[:, i, :], in_proj[:, D_INNER:D_INNER + CONV], conv_w[:, :, i], ALU.mult).then_inc(taps_made, 1)
            dve.wait_ge(soft_step, 4)
            raw = k["dt"][:, :, HEADS * side:HEADS * side + HEADS]
            dt3, da3 = (v[:].rearrange("p (t h) -> p t h", h=HEADS) for v in (dt, da))
            nc.vector.scalar_tensor_tensor(out=dt3, in0=raw, scalar=0.0, in1=size[:], op0=ALU.max, op1=ALU.add).then_inc(dt_made, 1)
            dve.wait_ge(dt_made, 1)
            nc.vector.scalar_tensor_tensor(out=da3, in0=dt3, scalar=-1.0, in1=a_pos[:, None, :].to_broadcast([P, ALL, HEADS]),
                                           op0=ALU.mult, op1=ALU.mult).then_inc(da_made, 1)
            dve.wait_ge(rows_copied, 2)
            for j in range(2):
                last = nc.vector.tensor_scalar(w_out[:, j, :], w_out_in[:, j, :], cols[:, 3 + j:4 + j], None, ALU.mult)
            last.then_inc(steps_made, 1)
            dve.wait_ge(sums_exp, 3)
            nc.vector.tensor_tensor(until[:], until[:], dt[:], ALU.mult).then_inc(steps_made, 1)
            dve.wait_ge(steps_made, 2)

            def step(n, par, edge):
                if live(n, edge, 2, ITEMS):
                    i, q = n - 2, par
                    dve.wait_ge(y_made, i + 1)
                    nc.vector.tensor_tensor(heads4(y0[:, q]), heads4(ps_y[:, 1, :]), per_head(since, i).to_broadcast([P, HEADS, HEAD]), ALU.mult).then_inc(y_since, 1)
                    dve.wait_ge(state_made, i + 1)
                    dve.wait_ge(state_faded, i + 1)
                    nc.vector.tensor_tensor(state[:, bass.ds((i % B) * HP, HP)], faded[:, q], ps_s[0:D_STATE, 0:HP], ALU.add).then_inc(state_done, 1)
                    dve.wait_ge(y_since, i + 1)
                    if past(i, 2):
                        dve.wait_ge(y_skipped, i - 1)
                    nc.vector.tensor_tensor(y1[:, q], ps_y[:, 0, :], y0[:, q], ALU.add).then_inc(y_summed, 1)
                if live(n, edge, 1, ITEMS):
                    i, q = n - 1, 1 - par
                    dve.wait_ge(bc_made, i + 1)
                    if past(i, 2):
                        dve.wait_ge(weighted, i - 1)
                    nc.vector.tensor_tensor(bc[:, q], ps_g[:, 0:P], inc[:], ALU.mult).then_inc(bc_masked, 1)
                    dve.wait_ge(x_turned, i + 1)
                    if past(i, 2):
                        dve.wait_ge(state_made, i - 1)
                        dve.wait_ge(y_skipped, i - 1)
                    for out, factor in ((x_dt, per_head(dt, i)), (x_until, per_head(until, i)), (x_skip, skip[:, :, None])):
                        nc.vector.tensor_tensor(heads4(out[:, q]), heads4(ps_n[:, 0:HP]), factor.to_broadcast([P, HEADS, HEAD]), ALU.mult)
                    nc.vector.tensor_copy(b_n[:, q], ps_n[:, 2 * P:2 * P + D_STATE]).then_inc(x_scaled, 1)
                if live(n, edge, 3, ITEMS):
                    i, q = n - 3, 1 - par
                    dve.wait_ge(out_made, i + 1)
                    dve.wait_ge(rooted, i + 1)
                    out = k["acc"][:].rearrange("p t c -> p (t c)")[:, bass.ds(tile(i) * C, C)]
                    nc.vector.scalar_tensor_tensor(out=out, in0=ps_o[:, 2 * P:3 * P], scalar=rstd[:, q:q + 1], in1=out,
                                                   op0=ALU.mult, op1=ALU.add).then_inc(out_added, 1)
                if live(n, edge, 0, ITEMS):
                    dve.wait_ge(conv_tanh, n + 1)
                    nc.vector.tensor_scalar(gate_c[:], gate_c[:], 0.5, 0.5, ALU.mult, ALU.add).then_inc(conv_gate, 1)
                    dve.wait_ge(z_tanh, n + 1)
                    nc.vector.tensor_scalar(gate_z[:], gate_z[:], 0.5, 0.5, ALU.mult, ALU.add).then_inc(z_gate, 1)
                    dve.wait_ge(conv_gate, n + 1)
                    if past(n, 2):
                        dve.wait_ge(bc_made, n - 1)
                        dve.wait_ge(y_made, n - 1)
                    for j in range(2):
                        nc.vector.scalar_tensor_tensor(out=x_t[:, par, j, :], in0=ps_c[:, j, :], scalar=cols[:, j:j + 1], in1=gate_c[:, j, :],
                                                       op0=ALU.add, op1=ALU.mult)
                    for out, lo in ((b_t, 0), (c_t, D_STATE)):
                        rng = slice(lo, lo + D_STATE)
                        last = nc.vector.scalar_tensor_tensor(out=out[:, par], in0=ps_c[rng, 2, :], scalar=cols[rng, 2:3], in1=gate_c[rng, 2, :],
                                                              op0=ALU.add, op1=ALU.mult)
                    last.then_inc(conv_done, 1)
                    dve.wait_ge(z_gate, n + 1)
                    if past(n, 2):
                        dve.wait_ge(y_gated, n - 1)
                    nc.vector.tensor_tensor(silu_z[:, par], ps_z[:, 0:D_INNER], gate_z[:], ALU.mult).then_inc(z_done, 1)
            steps(dve, step)


RING = 16
SHARE = 8


def load_expert(sp, d, ring, e, r):
    hid = 4 * P
    sp.dma_start(ring["w1"][:, r], d["L1_ffn_weight1"].rearrange("e c h -> (e c) h")[bass.ds(e * (C + 1), C), :]).then_inc(ring["w1_loaded"][r], 16)
    sp.dma_start(ring["w2"][:, r], d["L1_ffn_weight2"].rearrange("e c h -> (e c) h")[bass.ds(e * (hid + 1), hid), :]
                 .rearrange("(j p) c -> p j c", p=P)).then_inc(ring["w2_loaded"][r], 16)


def route(nc, d, k, ring):
    with ExitStack() as ctx:
        sb = lambda name, shape: ctx.enter_context(nc.sbuf_tensor(name, shape, F32))
        sem = semaphores(nc, ctx)
        ps = lambda name, shape: ctx.enter_context(nc.psum_tensor(name, shape, F32))
        u, u_t = sb("r_u", [P, 2, GROUP, C]), sb("r_u_t", [P, 2, GROUP * P])
        stats, mean_var, rstd = sb("r_stats", [P, 2, GROUP, 6]), sb("r_mean_var", [P, 2, GROUP, 2]), sb("r_rstd", [P, 2, GROUP])
        gate_w, gate_t, gate_b = sb("r_gate_w", [E, C]), sb("r_gate_t", [C, E]), sb("r_gate_b", [P, 1])
        gate_row, ones, power = sb("r_gate_row", [1, 2 * E]), sb("r_ones", [1, 1]), sb("r_power", [P, GROUP])
        eps_row, pause = sb("r_eps_row", [P, GROUP]), sb("r_pause", [P, 1])
        prob, rest = sb("r_prob", [P, T]), sb("r_rest", [P, T])
        top, total, eight = sb("r_top", [P, 1]), sb("r_total", [P, 2]), sb("r_eight", [P, TOP])
        turned_c = sb("r_turned_c", [P, 2, 4, P])
        ps_w, ps_u, ps_r = ps("r_ps_w", [P, 512]), ps("r_ps_u", [P, 2, 512]), ps("r_ps_r", [P, 2, 512])
        ps_c, ps_p = ps("r_ps_c", [P, 2, 512]), ps("r_ps_p", [P, 4 * P])
        w_loaded, const, w_turned, w_copied = sem("r_w_loaded"), sem("r_const"), sem("r_w_turned"), sem("r_w_copied")
        seen, averaged, eps, rooted, normed, kept = sem("r_seen"), sem("r_averaged"), sem("r_eps"), sem("r_rooted"), sem("r_normed"), sem("r_kept")
        u_turned, u_copied, routed, biased = sem("r_u_turned"), sem("r_u_copied"), sem("r_routed"), sem("r_biased")
        maxed, exped, inverted, scaled, ranked, removed, chosen = (sem("r_maxed"), sem("r_exped"), sem("r_inverted"), sem("r_scaled"),
                                                                   sem("r_ranked"), sem("r_removed"), sem("r_chosen"))
        c_turned, c_copied, pooled, pool_copied = sem("r_c_turned"), sem("r_c_copied"), sem("r_pooled"), sem("r_pool_copied")
        block = ctx.enter_context(nc.Block())
        SETS = B // 2
        logits = k["chosen"]

        @block.sync
        def _(sp):
            sp.dma_start(gate_w[:], d["L1_ffn_gate_w"]).then_inc(w_loaded, 16)
            for i in range(2):
                sp.dma_start(gate_row[:, E * i:E * i + E], d["L1_ffn_gate_b"].rearrange("(a e) -> a e", a=1)).then_inc(w_loaded, 16)
            for r in range(RING):
                load_expert(sp, d, ring, r, r)

        @block.tensor
        def _(pe):
            pe.wait_ge(w_loaded, 48)
            transpose(nc, ps_w[:, 0:E], gate_w[:], k["ident"][0:E, 0:E])
            pe.wait_ge(const, 3)
            nc.tensor.matmul(ps_w[:, E:E + 1], gate_row[:], ones[:], start=True, stop=True).then_inc(w_turned, 1)
            pe.wait_ge(w_copied, 2)

            def tokens(g, s, s_int):
                pe.wait_ge(normed, g + 1)
                if s_int or s >= 2:
                    pe.wait_ge(u_copied, g - 1)
                for i in range(GROUP):
                    last = transpose(nc, ps_u[:, s % 2, i * P:(i + 1) * P], u[:, s % 2, i, :], k["ident"][:])
                last.then_inc(u_turned, 1)
                pe.wait_ge(u_copied, g + 1)
                if s_int or s >= 2:
                    pe.wait_ge(biased, g - 1)
                rows = slice(E * (s // 2), E * (s // 2) + E)
                nc.tensor.matmul(ps_r[rows, s % 2, :], gate_t[:], u_t[:, s % 2, :], start=True, stop=True).then_inc(routed, 1)
            for s in range(4):
                tokens(s, s, False)
            with pe.Fori(1, SETS) as i:
                for s in range(4):
                    tokens(4 * i + s, s, True)
            for s in range(SETS):
                pe.wait_ge(chosen, s + 1)
                for half in range(2):
                    n = 2 * s + half
                    if n >= 2:
                        pe.wait_ge(c_copied, n - 1)
                    for i in range(4):
                        at = (4 * half + i) * P
                        last = transpose(nc, ps_c[:, half, i * P:(i + 1) * P], logits[:, s, at:at + P], k["ident"][:])
                    last.then_inc(c_turned, 1)
                pe.wait_ge(c_copied, 2 * s + 2)
                pe.wait_ge(kept, GROUPS)
                for b in range(2):
                    for i in range(TILES):
                        last = nc.tensor.matmul(ps_p[:, 2 * P * (s % 2) + E * b:2 * P * (s % 2) + E * b + E], k["u"][:, (2 * s + b) * TILES + i, :],
                                                turned_c[:, i // 4, i % 4, E * b:E * b + E], start=(i == 0), stop=(i == TILES - 1))
                last.then_inc(pooled, 1)
                pe.wait_ge(pool_copied, s + 1)

        @block.scalar
        def _(act):
            act.wait_ge(w_turned, 1)
            nc.scalar.activation(gate_t[:], ps_w[:, 0:E], ACT.Copy).then_inc(w_copied, 1)
            nc.scalar.activation(gate_b[:], ps_w[:, E:E + 1], ACT.Copy).then_inc(w_copied, 1)
            act.wait_ge(w_copied, 2)

            def tokens(g, s, s_int, i):
                act.wait_ge(u_turned, g + 1)
                if s_int or s >= 2:
                    act.wait_ge(routed, g - 1)
                nc.scalar.activation(u_t[:, s % 2], ps_u[:, s % 2, :], ACT.Copy).then_inc(u_copied, 1)
                act.wait_ge(routed, g + 1)
                rows = slice(E * (s // 2), E * (s // 2) + E)
                out = logits[:].rearrange("p s t -> p (s t)")[rows, bass.ds(i * T + 512 * (s % 2), 512)]
                nc.scalar.activation(out, ps_r[rows, s % 2, :], ACT.Identity, bias=gate_b[rows, :]).then_inc(biased, 1)
            for s in range(4):
                tokens(s, s, False, 0)
            with act.Fori(1, SETS) as i:
                for s in range(4):
                    tokens(4 * i + s, s, True, i)
            for s in range(SETS):
                act.wait_ge(maxed, s + 1)
                if s >= 1:
                    act.wait_ge(chosen, s)
                nc.scalar.activation(prob[:], logits[:, s, :], ACT.Exp, bias=top[:], accum_out=total[:, 0:1]).then_inc(exped, 1)
                if s >= 1:
                    act.wait_ge(pooled, s)
                for half in range(2):
                    act.wait_ge(c_turned, 2 * s + half + 1)
                    nc.scalar.activation(turned_c[:, half].rearrange("p i e -> p (i e)"), ps_c[:, half, :], ACT.Copy).then_inc(c_copied, 1)
                act.wait_ge(pooled, s + 1)
                for b in range(2):
                    at = 2 * P * (s % 2) + E * b
                    last = nc.scalar.activation(k["pooled"][:, :, 2 * s + b], ps_p[:, at:at + E], ACT.Copy)
                last.then_inc(pool_copied, 1)

        @block.gpsimd
        def _(pool):
            pool.memset(power[:], -0.5).then_inc(const, 1)
            pool.memset(ones[:], 1.0).then_inc(const, 1)
            pool.memset(eps_row[:], EPS).then_inc(const, 1)
            pool.wait_ge(const, 3)

            def step(n, par, edge):
                if live(n, edge, 0, GROUPS):
                    pool.wait_ge(averaged, n + 1)
                    pool.tensor_tensor(rstd[:, par], mean_var[:, par, :, 1], eps_row[:], ALU.add).then_inc(eps, 1)
                    pool.wait_ge(eps, n + 1)
                    pool.tensor_tensor(rstd[:, par], rstd[:, par], power[:], ALU.pow).then_inc(rooted, 1)
                if live(n, edge, 1, GROUPS):
                    pool.wait_ge(normed, n)
                    pool.tensor_copy(k["u"][:, bass.ds((n - 1) * GROUP, GROUP), :], u[:, 1 - par]).then_inc(kept, 1)
            two_by_two(pool, GROUPS, step, 1)

        @block.vector
        def _(dve):
            def step(n, par, edge):
                if live(n, edge, 0, GROUPS):
                    if past(n, 2):
                        dve.wait_ge(averaged, n - 1)
                        dve.wait_ge(normed, n - 1)
                    for i in range(GROUP):
                        at = (n * GROUP + i) * C
                        last = nc.vector.bn_stats(stats[:, par, i, :], k["acc"][:].rearrange("p t c -> p (t c)")[:, bass.ds(at, C)])
                    last.then_inc(seen, 1)
                    dve.wait_ge(seen, n + 1)
                    nc.vector.memset(pause[:], 0.0)
                    for i in range(GROUP):
                        last = nc.vector.bn_aggr(mean_var[:, par, i, :], stats[:, par, i, :])
                    last.then_inc(averaged, 1)
                if live(n, edge, 1, GROUPS):
                    q, m = 1 - par, n - 1
                    dve.wait_ge(rooted, m + 1)
                    if past(m, 2):
                        dve.wait_ge(kept, m - 1)
                        dve.wait_ge(u_turned, m - 1)
                    for i in range(GROUP):
                        at = (m * GROUP + i) * C
                        last = nc.vector.tensor_scalar(u[:, q, i, :], k["acc"][:].rearrange("p t c -> p (t c)")[:, bass.ds(at, C)],
                                                       mean_var[:, q, i, 0:1], rstd[:, q, i:i + 1], ALU.subtract, ALU.mult)
                    last.then_inc(normed, 1)
            two_by_two(dve, GROUPS, step, 1)
            dve.wait_ge(biased, GROUPS)
            for s in range(SETS):
                if s >= 1:
                    dve.wait_ge(exped, s)
                nc.vector.tensor_reduce(top[:], logits[:, s, :], AX.X, ALU.max, negate=True).then_inc(maxed, 1)
                dve.wait_ge(exped, s + 1)
                nc.vector.reciprocal(total[:, 1:2], total[:, 0:1]).then_inc(inverted, 1)
                dve.wait_ge(inverted, s + 1)
                nc.vector.tensor_scalar(prob[:], prob[:], total[:, 1:2], None, ALU.mult).then_inc(scaled, 1)
                dve.wait_ge(scaled, s + 1)
                nc.vector.max(eight[:], prob[:]).then_inc(ranked, 1)
                dve.wait_ge(ranked, s + 1)
                nc.vector.match_replace(rest[:], eight[:], prob[:], 0.0).then_inc(removed, 1)
                dve.wait_ge(removed, s + 1)
                nc.vector.tensor_tensor(logits[:, s, :], prob[:], rest[:], ALU.subtract).then_inc(chosen, 1)


def experts(nc, d, k, ring):
    R = SHARE
    H1 = 4
    with ExitStack() as ctx:
        sb = lambda name, shape: ctx.enter_context(nc.sbuf_tensor(name, shape, F32))
        sem = semaphores(nc, ctx)
        ps = lambda name, shape: ctx.enter_context(nc.psum_tensor(name, shape, F32))
        w1, w2 = ring["w1"][:].rearrange("p r (j q) -> p r j q", q=P), ring["w2"]
        b1_rows, b1, b2 = sb("e_b1_rows", [E, H1, P]), sb("e_b1", [P, E, H1]), sb("e_b2", [E, C])
        h_sum, h = sb("e_h_sum", [P, 2, R, H1, B]), sb("e_h", [P, 2, R, H1, B])
        y_t, y = sb("e_y_t", [P, E, B]), sb("e_y", [P, B // 2, C])
        out = sb("e_out", [P, 4, 4, C])
        ps_b, ps_h, ps_y = ps("e_ps_b", [P, H1, P]), ps("e_ps_h", [P, 2, 2 * R * H1 * B]), ps("e_ps_y", [P, 512])
        ps_t, ps_o = ps("e_ps_t", [P, 512]), ps("e_ps_o", [P, 2, 4 * C])
        b_loaded, b_turned, b_copied = sem("e_b_loaded"), sem("e_b_turned"), sem("e_b_copied")
        h_made, h_biased, h_done, y_made, y_copied = sem("e_h_made"), sem("e_h_biased"), sem("e_h_done"), sem("e_y_made"), sem("e_y_copied")
        y_turned, y_biased, returned, summed = sem("e_y_turned"), sem("e_y_biased"), sem("e_returned"), sem("e_summed")
        stored = [sem(f"e_stored{i}") for i in range(4)]
        block = ctx.enter_context(nc.Block())
        w1_d, w2_d = d["L1_ffn_weight1"], d["L1_ffn_weight2"]
        out_tiles = d["out"].rearrange("b l f c -> (b l f) c").rearrange("(g i p) c -> g p i c", i=4, p=P)
        HID = H1 * P

        @block.sync
        def _(sp):
            sp.dma_start(b1_rows[:].rearrange("e j p -> e (j p)"), w1_d[:, C, :]).then_inc(b_loaded, 16)
            sp.dma_start(b2[:], w2_d[:, HID, :]).then_inc(b_loaded, 16)

            with sp.Fori(1, E // RING) as i:
                for r in range(RING):
                    sp.wait_ge(y_made, RING * i + (r - (RING - 1)))
                    load_expert(sp, d, ring, RING * i + r, r)
            for g in range(GROUPS):
                sp.wait_ge(summed, g + 1)
                sp.dma_start(out_tiles[g], out[:, g % 4]).then_inc(stored[g % 4], 16)
            for g in range(4):
                sp.wait_ge(stored[g], 16 * (GROUPS // 4))

        @block.tensor
        def _(pe):
            pe.wait_ge(b_loaded, 32)
            for j in range(H1):
                last = transpose(nc, ps_b[:, j, 0:E], b1_rows[:, j, :], k["ident"][0:E, 0:E])
            last.then_inc(b_turned, 1)

            def hidden(turn, half):
                n = 2 * turn + half
                if past(turn, 1):
                    pe.wait_ge(h_biased, n - 1)
                for r in range(R):
                    p = R * half + r
                    pe.wait_ge(ring["w1_loaded"][p], 16 * turn + 16)
                    for j in range(H1):
                        last = nc.tensor.matmul(ps_h[:, half, (r * H1 + j) * B:(r * H1 + j + 1) * B], w1[:, p, j, :],
                                                k["pooled"][:].rearrange("p e b -> p (e b)")[:, bass.ds((n * R + r) * B, B)], start=True, stop=True)
                last.then_inc(h_made, 1)

            def outputs(turn, half):
                n = 2 * turn + half
                pe.wait_ge(h_done, n + 1)
                if past(n, 1):
                    pe.wait_ge(y_copied, n)
                for r in range(R):
                    p = R * half + r
                    pe.wait_ge(ring["w2_loaded"][p], 16 * turn + 16)
                    for j in range(H1):
                        last = nc.tensor.matmul(ps_y[:, r * B:(r + 1) * B], w2[:, p, j, :], h[:, half, r, j, :], start=(j == 0), stop=(j == H1 - 1))
                    last.then_inc(y_made, 1)
            hidden(0, 0)
            hidden(0, 1)
            outputs(0, 0)
            with pe.Fori(1, E // RING) as i:
                hidden(i, 0)
                outputs(i - 1, 1)
                hidden(i, 1)
                outputs(i, 0)
            outputs(E // RING - 1, 1)
            pe.wait_ge(y_copied, E // R)
            for b in range(B):
                if b >= 1:
                    pe.wait_ge(y_biased, b)
                transpose(nc, ps_t[0:E, 0:C], y_t[:, :, b], k["ident"][:]).then_inc(y_turned, 1)
            pe.wait_ge(y_biased, B)
            for g in range(GROUPS):
                if g >= 2:
                    pe.wait_ge(summed, g - 1)
                b = g // 2
                rows = slice(E * (b % 2), E * (b % 2) + E)
                for i in range(4):
                    at = (4 * (g % 2) + i) * P
                    last = nc.tensor.matmul(ps_o[:, g % 2, i * C:(i + 1) * C], k["chosen"][rows, b // 2, at:at + P], y[rows, b // 2, :], start=True, stop=True)
                last.then_inc(returned, 1)

        @block.scalar
        def _(act):
            act.wait_ge(b_turned, 1)
            nc.scalar.activation(b1[:].rearrange("p e j -> p j e"), ps_b[:, :, 0:E], ACT.Copy).then_inc(b_copied, 1)

            def gelu(n, half):
                act.wait_ge(h_biased, n + 1)
                if past(n, 2):
                    act.wait_ge(y_made, R * (n - 1))
                nc.scalar.activation(h[:, half], h_sum[:, half], ACT.Gelu).then_inc(h_done, 1)

            def copy(n):
                act.wait_ge(y_made, R * n + R)
                nc.scalar.activation(y_t[:].rearrange("p e b -> p (e b)")[:, bass.ds(n * R * B, R * B)], ps_y[:, 0:R * B], ACT.Copy).then_inc(y_copied, 1)
            gelu(0, 0)
            gelu(1, 1)
            copy(0)
            with act.Fori(1, E // RING) as i:
                gelu(2 * i, 0)
                copy(2 * i - 1)
                gelu(2 * i + 1, 1)
                copy(2 * i)
            copy(E // R - 1)

        @block.vector
        def _(dve):
            dve.wait_ge(b_copied, 1)

            def biased(n, half):
                dve.wait_ge(h_made, n + 1)
                if past(n, 2):
                    dve.wait_ge(h_done, n - 1)
                bias = b1[:].rearrange("p e j -> p (e j)")[:, bass.ds(n * R * H1, R * H1)]
                nc.vector.tensor_tensor(h_sum[:, half].rearrange("p r j b -> p (r j) b"), ps_h[:, half, 0:R * H1 * B].rearrange("p (r b) -> p r b", b=B),
                                        bias[:, :, None].to_broadcast([P, R * H1, B]), ALU.add).then_inc(h_biased, 1)
            biased(0, 0)
            biased(1, 1)
            with dve.Fori(1, E // RING) as i:
                biased(2 * i, 0)
                biased(2 * i + 1, 1)
            for b in range(B):
                dve.wait_ge(y_turned, b + 1)
                rows = slice(E * (b % 2), E * (b % 2) + E)
                nc.vector.tensor_tensor(y[rows, b // 2, :], ps_t[0:E, 0:C], b2[:], ALU.add).then_inc(y_biased, 1)
            for g in range(GROUPS):
                dve.wait_ge(returned, g + 1)
                if g >= 4:
                    dve.wait_ge(stored[g % 4], 16 * (g // 4))
                nc.vector.tensor_tensor(out[:, g % 4], ps_o[:, g % 2, :].rearrange("p (i c) -> p i c", c=C), k["acc"][:, 4 * g:4 * g + 4, :], ALU.add).then_inc(summed, 1)


def hybrid(nc, d):
    with ExitStack() as ctx:
        k = {}

        def keep(name, shape):
            k[name] = ctx.enter_context(nc.sbuf_tensor(name, shape, F32))
        for name in ("ident", "le", "gt", "ge", "lt", "att_bias"):
            keep(name, [P, P])
        keep("acc", [P, ALL, C])
        keep("dt", [P, ALL, 2 * HEADS])
        with ExitStack() as early:
            k["w_att"] = early.enter_context(nc.sbuf_tensor("w_att", [P, H, SLOT], F32))
            setup(nc, d, k)
            attention(nc, d, k)
        feed_forward(nc, d, k)
        scan(nc, d, k, 0)
        scan(nc, d, k, 1)
        keep("chosen", [P, B // 2, T])
        keep("pooled", [P, E, B])
        ring = {"w1": ctx.enter_context(nc.sbuf_tensor("ring_w1", [P, RING, 4 * P], F32)),
                "w2": ctx.enter_context(nc.sbuf_tensor("ring_w2", [P, RING, 4, C], F32))}
        ring_sem = semaphores(nc, ctx)
        for w in ("w1", "w2"):
            ring[w + "_loaded"] = [ring_sem(f"ring_{w}_loaded{r}") for r in range(RING)]
        with ExitStack() as late:
            k["u"] = late.enter_context(nc.sbuf_tensor("u", [P, ALL, C], F32))
            route(nc, d, k, ring)
        experts(nc, d, k, ring)


def kernel(**inputs):
    import numpy as np
    import concourse.bacc as bacc
    from concourse.bass_utils import run_bass_kernel_spmd as run

    nc = bacc.Bacc("TRN2", target_bir_lowering=False, num_devices=1)
    arrays, d = {}, {}
    for name, value in inputs.items():
        arrays["in_" + name] = a = np.ascontiguousarray(value)
        d[name] = nc.dram_tensor("in_" + name, a.shape, mybir.dt.from_np(a.dtype), kind="ExternalInput").ap()
    d["out"] = nc.dram_tensor("out", (B, L, F, C), F32, kind="ExternalOutput").ap()
    d["x_t"] = nc.dram_tensor("x_t", (P, ALL * P), F32, kind="Internal").ap()
    d["u_t"] = nc.dram_tensor("u_t", (P, B, T + 2 * HALO), F32, kind="Internal").ap()
    hybrid(nc, d)
    return run(nc, [arrays], core_ids=[0]).results[0]["out"]
```

```python
from contextlib import ExitStack

import concourse.bass as bass
from concourse import mybir

F32 = mybir.dt.float32
ALU = mybir.AluOpType
ACT = mybir.ActivationFunctionType
AX = mybir.AxisListType

P = 128
B, L, F, C = 8, 64, 16, 128
T = L * F
TILES = T // P
ALL = B * TILES
H = 8
FF = 512
FC = FF // P
GROUP = 4
GROUPS = ALL // GROUP
EPS = 1e-5
SLOT = 3 * P + 2

D_INNER, D_STATE, HEADS, HEAD = 256, 64, 4, 64
CONV = D_INNER + 2 * D_STATE
TAPS = 4
HALO = TAPS - 1
IN_PROJ = 2 * D_INNER + 2 * D_STATE + HEADS
DIRS = ("fwd", "bwd")

E = 64
TOP = 8


def transpose(nc, out, in_, ident):
    return nc.tensor.transpose(out, in_, ident)


def semaphores(nc, ctx, pre=""):
    taken = []

    def clear(*_):
        numbers = sorted(s.num for s in taken)
        with nc.Block() as block:
            @block.gpsimd
            def _(pool):
                first = 0
                for i in range(1, len(numbers) + 1):
                    if i == len(numbers) or numbers[i] != numbers[i - 1] + 1:
                        pool.sem_clear(range(numbers[first], numbers[i - 1] + 1))
                        first = i

    def sem(name):
        taken.append(hold.enter_context(nc.semaphore(pre + name)))
        return taken[-1]
    hold = ctx.enter_context(ExitStack())
    ctx.callback(clear)
    return sem


def setup(nc, d, k):
    with ExitStack() as ctx:
        sb = lambda name, shape: ctx.enter_context(nc.sbuf_tensor(name, shape, F32))
        sem = semaphores(nc, ctx)
        x_in = sb("s_x_in", [P, 2, GROUP, C])
        x_t = sb("s_x_t", [P, 2, GROUP * P])
        w_qkv = sb("s_w_qkv", [P, 3, H, C])
        w_o = sb("s_w_o", [P, H * C])
        wo_t = sb("s_wo_t", [P, H, P])
        b_v = sb("s_b_v", [P, H])
        b_vb = sb("s_b_vb", [P, H, P])
        b_qk = sb("s_b_qk", [P, 2, H])
        b_o = sb("s_b_o", [P, C])
        ones = sb("s_ones", [P, P])
        ps_x = ctx.enter_context(nc.psum_tensor("s_ps_x", [P, 2, 512], F32))
        ps_w = ctx.enter_context(nc.psum_tensor("s_ps_w", [P, 2, 512], F32))
        ps_b = ctx.enter_context(nc.psum_tensor("s_ps_b", [P, 512], F32))
        blank, masks = sem("blank"), sem("masks")
        x_loaded = [sem("x_loaded0"), sem("x_loaded1")]
        x_turned, x_copied = sem("x_turned"), sem("x_copied")
        x_stored = [sem("x_stored0"), sem("x_stored1")]
        w_loaded, w_turned, w_copied = sem("w_loaded"), sem("w_turned"), sem("w_copied")
        vo_done, vo_copied = sem("vo_done"), sem("vo_copied")
        bias_scaled, bias_spread, bias_done, bias_added = sem("bias_scaled"), sem("bias_spread"), sem("bias_done"), sem("bias_added")
        block = ctx.enter_context(nc.Block())
        x_tiles = d["x"].rearrange("b l f c -> (b l f) c").rearrange("(g i p) c -> g p i c", i=GROUP, p=P)

        @block.sync
        def _(sp):
            for n, name in enumerate(("wq", "wk", "wv")):
                sp.dma_start(w_qkv[:, n], d["L0_conv_" + name].rearrange("(c h) d -> c h d", h=H)).then_inc(w_loaded, 16)
            sp.dma_start(w_o[:], d["L0_conv_wo"]).then_inc(w_loaded, 16)
            sp.dma_start(b_v[:], d["L0_conv_bv"].rearrange("(c h) -> c h", h=H)).then_inc(w_loaded, 16)
            sp.dma_start(b_qk[:, 0], d["L0_conv_bq"].rearrange("(c h) -> c h", h=H)).then_inc(w_loaded, 16)
            sp.dma_start(b_qk[:, 1], d["L0_conv_bk"].rearrange("(c h) -> c h", h=H)).then_inc(w_loaded, 16)
            sp.dma_start(b_o[:], d["L0_conv_bo"].rearrange("(a c) -> a c", a=1).to_broadcast([P, C])).then_inc(w_loaded, 16)
            for s in range(2):
                sp.dma_start(x_in[:, s], x_tiles[s]).then_inc(x_loaded[s], 16)
            with sp.Fori(1, GROUPS // 2) as i:
                for s in range(2):
                    sp.wait_ge(x_turned, 2 * i + s - 1)
                    sp.dma_start(x_in[:, s], x_tiles[2 * i + s]).then_inc(x_loaded[s], 16)

        @block.gpsimd
        def _(pool):
            pool.memset(k["ident"][:], 0.0).then_inc(blank, 1)
            pool.memset(ones[:], 1.0).then_inc(blank, 1)
            pool.wait_ge(blank, 2)
            pool.affine_select(out=k["ident"][:], in_=k["ident"][:], compare_op=ALU.not_equal, fill=1.0, base=0,
                               pattern=[[-1, P]], channel_multiplier=1).then_inc(masks, 1)
            for name, row, op in (("le", -1, ALU.is_ge), ("gt", 1, ALU.is_gt), ("ge", 1, ALU.is_ge), ("lt", -1, ALU.is_gt)):
                pool.affine_select(out=k[name][:], in_=ones[:], compare_op=op, fill=0.0, base=0,
                                   pattern=[[-row, P]], channel_multiplier=row).then_inc(masks, 1)
            pool.wait_ge(w_loaded, 16 * 8)
            pool.tensor_scalar(b_v[:], b_v[:], float(L), None, ALU.mult).then_inc(bias_scaled, 1)
            pool.wait_ge(bias_scaled, 1)
            pool.tensor_tensor(b_vb[:], ones[:, None, :].to_broadcast([P, H, P]),
                               b_v[:, :, None].to_broadcast([P, H, P]), ALU.mult).then_inc(bias_spread, 1)

        @block.tensor
        def _(pe):
            pe.wait_ge(masks, 5)
            pe.wait_ge(w_loaded, 16 * 8)
            for n in range(6):
                if n >= 2:
                    pe.wait_ge(w_copied, n - 1)
                for i in range(4):
                    h = 4 * (n % 2) + i
                    src = w_qkv[:, n // 2, h, :] if n < 4 else w_o[:, h::H]
                    last = transpose(nc, ps_w[:, n % 2, i * P:(i + 1) * P], src, k["ident"][:])
                last.then_inc(w_turned, 1)
            pe.wait_ge(w_copied, 6)
            for n in range(2):
                for i in range(4):
                    h = 4 * n + i
                    last = nc.tensor.matmul(ps_w[:, n, i * P:(i + 1) * P], w_qkv[:, 2, h, :], wo_t[:, h, :], start=True, stop=True)
                last.then_inc(vo_done, 1)
            pe.wait_ge(bias_spread, 1)
            for h in range(H):
                last = nc.tensor.matmul(ps_b[:, 0:C], b_vb[:, h, :], wo_t[:, h, :], start=(h == 0), stop=(h == H - 1))
            last.then_inc(bias_done, 1)

            def turn(n, g):
                pe.wait_ge(x_loaded[n], 16 * (g // 2 + 1) if isinstance(g, int) else 16 * g[0] + 16)
                for i in range(GROUP):
                    last = transpose(nc, ps_x[:, n, i * P:(i + 1) * P], x_in[:, n, i, :], k["ident"][:])
                last.then_inc(x_turned, 1)
            for s in range(2):
                turn(s, s)
            with pe.Fori(1, GROUPS // 2) as i:
                for s in range(2):
                    pe.wait_ge(x_copied, 2 * i + s - 1)
                    turn(s, (i,))

        @block.scalar
        def _(act):
            for n in range(6):
                act.wait_ge(w_turned, n + 1)
                heads = slice(4 * (n % 2), 4 * (n % 2) + 4)
                out = k["w_att"][:, heads, (n // 2) * P:(n // 2 + 1) * P] if n < 4 else wo_t[:, heads, :]
                nc.scalar.activation(out, ps_w[:, n % 2, :].rearrange("p (h c) -> p h c", h=4), ACT.Copy).then_inc(w_copied, 1)
            for n in range(2):
                act.wait_ge(vo_done, n + 1)
                nc.scalar.activation(k["w_att"][:, 4 * n:4 * n + 4, 2 * P:3 * P],
                                     ps_w[:, n, :].rearrange("p (h c) -> p h c", h=4), ACT.Copy).then_inc(vo_copied, 1)
            nc.scalar.activation(k["w_att"][:, :, 3 * P], b_qk[:, 0], ACT.Copy, scale=float(C) ** -0.5).then_inc(vo_copied, 1)
            nc.scalar.activation(k["w_att"][:, :, 3 * P + 1], b_qk[:, 1], ACT.Copy).then_inc(vo_copied, 1)

            def copy(s, i):
                if i is not None:
                    act.wait_ge(x_stored[s], 16 * i)
                act.wait_ge(x_turned, s + 1 if i is None else 2 * i + s + 1)
                nc.scalar.activation(x_t[:, s], ps_x[:, s, :], ACT.Copy).then_inc(x_copied, 1)
                at = s if i is None else 2 * i + s
                act.wait_ge(x_copied, at + 1)
                act.dma_start(d["x_t"][:, bass.ds(at * 512, 512)], x_t[:, s]).then_inc(x_stored[s], 16)
            copy(0, None)
            copy(1, None)
            with act.Fori(1, GROUPS // 2) as i:
                copy(0, i)
                copy(1, i)
            for s in range(2):
                act.wait_ge(x_stored[s], 16 * (GROUPS // 2))

        @block.vector
        def _(dve):
            dve.wait_ge(bias_done, 1)
            nc.vector.tensor_tensor(k["acc"][:], ps_b[:, None, 0:C].to_broadcast([P, ALL, C]), b_o[:, None, :].to_broadcast([P, ALL, C]),
                                    ALU.add).then_inc(bias_added, 1)
            dve.wait_ge(bias_added, 1)


def attention(nc, d, k, pairs=B * H // 2):
    QB = 8
    NEAR = F // 2
    DVE_SUMS = 10
    with ExitStack() as ctx:
        sb = lambda name, shape: ctx.enter_context(nc.sbuf_tensor(name, shape, F32))
        sem = semaphores(nc, ctx)
        ps = lambda name, shape: ctx.enter_context(nc.psum_tensor(name, shape, F32))
        xs, ws = sb("a_xs", [P, 2, T]), sb("a_ws", [P, 2, SLOT])
        q_t, k_t, v = sb("a_q_t", [P, 2, T]), sb("a_k_t", [P, 2, T]), sb("a_v", [P, 2, TILES, C])
        x_keys = sb("a_x_keys", [P, T])
        s = sb("a_s", [P, QB, T])
        minus_top = sb("a_minus_top", [P, 2, F])
        row_sum, row_inv = sb("a_row_sum", [P, 2, F]), sb("a_row_inv", [P, 2, F])
        col_sum, col_inv = sb("a_col_sum", [P, 2, L]), sb("a_col_inv", [P, 2, L])
        a_t = sb("a_a_t", [P, 2, TILES, P])
        ps_s, ps_t = ps("a_ps_s", [P, 2, T]), ps("a_ps_t", [P, 2, 512])
        ps_p, ps_z = ps("a_ps_p", [P, 512]), ps("a_ps_z", [P, 4, P])
        head_loaded = [sem("head_loaded0"), sem("head_loaded1")]
        keys_ordered, projected, project_copied = sem("keys_ordered"), sem("projected"), sem("project_copied")
        scored, maxed, shifted = sem("scored"), sem("maxed"), sem("shifted")
        exp_far, exp_near = sem("exp_far"), sem("exp_near")
        row_summed, row_inverted, scaled1, exp2 = sem("row_summed"), sem("row_inverted"), sem("scaled1"), sem("exp2")
        col_summed, col_inverted, scaled2 = sem("col_summed"), sem("col_inverted"), sem("scaled2")
        turned, turn_copied, weighted, added = sem("turned"), sem("turn_copied"), sem("weighted"), sem("added")
        block = ctx.enter_context(nc.Block())
        PROJ = 6
        AT = {0: 0, 2: 1, 3: 2, 4: 3, 5: 4, 6: 5}

        def heads(eng, head, tail):
            head(0, 0, True)
            head(1, 1, True)
            with eng.Fori(1, pairs) as i:
                head(2 * i, 0, False)
                head(2 * i + 1, 1, False)
            tail(2 * pairs)

        def lagged(n, par, j, lag, first):
            if first and 8 * n + j - lag < 0:
                return None, None
            return 8 * n + (j - lag), (8 * par + j - lag) % 16

        @block.sync
        def _(sp):
            def load(n, par, b, h):
                sp.dma_start(xs[:, par], d["x_t"][:, bass.ds(b * T, T)]).then_inc(head_loaded[par], 16)
                sp.dma_start(ws[:, par], k["w_att"][:, h, :]).then_inc(head_loaded[par], 16)
            load(0, 0, 0, 0)
            load(1, 1, 0, 1)
            with sp.Fori(1, pairs) as i:
                for par in range(2):
                    n = 2 * i + par
                    sp.wait_ge(projected, PROJ * (n - 1))
                    load(n, par, n // H, n % H)
            sp.wait_ge(projected, PROJ * (2 * pairs - 1))
            load(2 * pairs, 0, 0, 0)

        def project(pe, n, par, c):
            if c == 0:
                pe.wait_ge(head_loaded[par], 32 * (n // 2) + 32)
            if not isinstance(n, int) or PROJ * n + c > 0:
                pe.wait_ge(project_copied, PROJ * n + c)
            half = slice(512 * (c % 2), 512 * (c % 2) + 512)
            if c == 2:
                pe.wait_ge(keys_ordered, n + 1)
            if c < 4:
                x = xs[:, par, half] if c < 2 else x_keys[:, half]
                last = nc.tensor.matmul(ps_p[:], ws[:, par, (c // 2) * P:(c // 2 + 1) * P], x, start=True, stop=True)
            else:
                for i in range(4):
                    at = (4 * (c - 4) + i) * P
                    last = nc.tensor.matmul(ps_p[:, i * P:(i + 1) * P], x_keys[:, at:at + P], ws[:, par, 2 * P:3 * P], start=True, stop=True)
            last.then_inc(projected, 1)

        @block.tensor
        def _(pe):
            def turn(t, u, half):
                if half == 0:
                    pe.wait_ge(scaled2, t + 1)
                if not isinstance(t, int) or t >= 1:
                    pe.wait_ge(turn_copied, 2 * t + half - 1)
                for i in range(4):
                    at = (4 * half + i) * P
                    last = transpose(nc, ps_t[:, half, i * P:(i + 1) * P], s[:, u % QB, at:at + P], k["ident"][:])
                last.then_inc(turned, 1)

            def weigh(t, u, four):
                pe.wait_ge(turn_copied, 2 * t + 2)
                if (not isinstance(t, int) or t >= 4) and u % 4 == 0:
                    pe.wait_ge(added, four)
                for i in range(TILES):
                    last = nc.tensor.matmul(ps_z[:, u % 4, :], a_t[:, u % 2, i, :], v[:, u // 8, i, :],
                                            start=(i == 0), stop=(i == TILES - 1))
                last.then_inc(weighted, 1)

            def head(n, par, first):
                for j in range(8):
                    t, u = lagged(n, par, j, 0, first)
                    if j == 0:
                        pe.wait_ge(project_copied, PROJ * (n + 1))
                    if not first or t >= 2:
                        pe.wait_ge(exp_far, t - 1)
                    for half in (1, 0):
                        if half == 0 and (not first or t >= 2):
                            pe.wait_ge(shifted, t - 1)
                        nc.tensor.matmul(ps_s[:, u % 2, half * 512:half * 512 + 512], q_t[:, par, j * P:(j + 1) * P],
                                         k_t[:, par, half * 512:half * 512 + 512], start=True, stop=True).then_inc(scored, 1)
                    t5, u5 = lagged(n, par, j, 5, first)
                    if t5 is not None:
                        weigh(t5, u5, 2 * n + (j - 5) // 4)
                    t4, u4 = lagged(n, par, j, 4, first)
                    if t4 is not None:
                        turn(t4, u4, 0)
                        turn(t4, u4, 1)
                    if j in AT:
                        project(pe, n + 1, 1 - par, AT[j])

            for c in range(PROJ):
                project(pe, 0, 0, c)

            def tail(n):
                for j in range(5):
                    weigh(8 * n + j - 5, (j - 5) % 16, 2 * n + (j - 5) // 4)
                    if j < 4:
                        turn(8 * n + j - 4, (j - 4) % 16, 0)
                        turn(8 * n + j - 4, (j - 4) % 16, 1)
            heads(pe, head, tail)

        @block.scalar
        def _(act):
            def project_copy(n, par, c):
                act.wait_ge(projected, PROJ * n + c + 1)
                half = slice(512 * (c % 2), 512 * (c % 2) + 512)
                if c < 2:
                    i = nc.scalar.activation(q_t[:, par, half], ps_p[:], ACT.Identity, bias=ws[:, par, 3 * P:3 * P + 1], scale=float(C) ** -0.5)
                elif c < 4:
                    i = nc.scalar.activation(k_t[:, par, half], ps_p[:], ACT.Identity, bias=ws[:, par, 3 * P + 1:3 * P + 2])
                else:
                    at = 4 * (c - 4)
                    i = nc.scalar.activation(v[:, par, at:at + 4, :], ps_p[:].rearrange("p (i c) -> p i c", c=C), ACT.Copy)
                i.then_inc(project_copied, 1)

            def turn_copy(t, u, half):
                if half == 0 and (not isinstance(t, int) or t >= 2):
                    act.wait_ge(weighted, t - 1)
                act.wait_ge(turned, 2 * t + half + 1)
                nc.scalar.activation(a_t[:, u % 2, 4 * half:4 * half + 4, :], ps_t[:, half, :].rearrange("p (i q) -> p i q", q=P),
                                     ACT.Copy).then_inc(turn_copied, 1)

            def far(t, u):
                act.wait_ge(maxed, 2 * t + 1)
                if not isinstance(t, int) or t >= 2:
                    act.wait_ge(row_inverted, t - 1)
                if not isinstance(t, int) or t >= QB:
                    act.wait_ge(turned, 2 * (t - QB) + 2)
                for g in range(NEAR, F):
                    total = {} if g < DVE_SUMS else {"accum_out": row_sum[:, u % 2, g:g + 1]}
                    last = nc.scalar.activation(s[:, u % QB, g * L:(g + 1) * L], ps_s[:, u % 2, g * L:(g + 1) * L], ACT.Exp,
                                                bias=minus_top[:, u % 2, g:g + 1], **total)
                last.then_inc(exp_far, 1)

            def near(t, u):
                act.wait_ge(shifted, t + 1)
                nc.scalar.activation(s[:, u % QB, 0:NEAR * L], s[:, u % QB, 0:NEAR * L], ACT.Exp).then_inc(exp_near, 1)

            def second(t, u):
                act.wait_ge(scaled1, t + 1)
                nc.scalar.activation(s[:, u % QB], s[:, u % QB], ACT.Exp).then_inc(exp2, 1)

            def head(n, par, first):
                for j in range(8):
                    t, u = lagged(n, par, j, 0, first)
                    far(t, u)
                    t2, u2 = lagged(n, par, j, 2, first)
                    t4, u4 = lagged(n, par, j, 4, first)
                    if t4 is not None:
                        turn_copy(t4, u4, 0)
                        turn_copy(t4, u4, 1)
                    if t2 is not None:
                        second(t2, u2)
                    near(t, u)
                    if j in AT:
                        project_copy(n + 1, 1 - par, AT[j])

            for c in range(PROJ):
                if c == 0:
                    act.wait_ge(head_loaded[0], 32)
                project_copy(0, 0, c)

            def tail(n):
                for j in range(4):
                    if j < 2:
                        second(8 * n + j - 2, (j - 2) % 16)
                    for half in range(2):
                        turn_copy(8 * n + j - 4, (j - 4) % 16, half)
            heads(act, head, tail)

        @block.gpsimd
        def _(pool):
            def rows(t, u):
                pool.wait_ge(row_inverted, t + 1)
                view = s[:, u % QB].rearrange("p (g m) -> p g m", g=F)
                pool.tensor_tensor(view, view, row_inv[:, u % 2, :, None].to_broadcast([P, F, L]), ALU.mult).then_inc(scaled1, 1)

            def columns(t, u):
                pool.wait_ge(col_inverted, t + 1)
                view = s[:, u % QB].rearrange("p (g m) -> p g m", g=F)
                pool.tensor_tensor(view, view, col_inv[:, u % 2, None, :].to_broadcast([P, F, L]), ALU.mult).then_inc(scaled2, 1)

            def head(n, par, first):
                for j in range(8):
                    t3, u3 = lagged(n, par, j, 3, first)
                    if t3 is not None:
                        columns(t3, u3)
                    t1, u1 = lagged(n, par, j, 1, first)
                    if t1 is not None:
                        rows(t1, u1)

            def tail(n):
                for j in range(3):
                    columns(8 * n + j - 3, (j - 3) % 16)
                    if j < 1:
                        rows(8 * n + j - 1, (j - 1) % 16)
            heads(pool, head, tail)

        @block.vector
        def _(dve):
            def order_keys(n, par, last_head):
                dve.wait_ge(head_loaded[par], 32 * (n // 2) + 32)
                if last_head is not None:
                    dve.wait_ge(projected, last_head)
                nc.vector.tensor_copy(x_keys[:].rearrange("p (g m) -> p m g", g=F), xs[:, par].rearrange("p (m g) -> p m g", g=F)).then_inc(keys_ordered, 1)

            def top(t, u, half):
                dve.wait_ge(scored, 2 * t + 2 - half)
                cols = slice(NEAR * half, NEAR * half + NEAR)
                nc.vector.tensor_reduce(minus_top[:, u % 2, cols], ps_s[:, u % 2].rearrange("p (g m) -> p g m", g=F)[:, cols, :],
                                        AX.X, ALU.max, negate=True).then_inc(maxed, 1)

            def shift(t, u):
                dve.wait_ge(maxed, 2 * t + 2)
                if not isinstance(t, int) or t >= QB:
                    dve.wait_ge(turned, 2 * (t - QB) + 2)
                nc.vector.tensor_tensor(s[:, u % QB].rearrange("p (g m) -> p g m", g=F)[:, 0:NEAR, :],
                                        ps_s[:, u % 2].rearrange("p (g m) -> p g m", g=F)[:, 0:NEAR, :],
                                        minus_top[:, u % 2, 0:NEAR, None].to_broadcast([P, NEAR, L]), ALU.add).then_inc(shifted, 1)

            def column_sums(t, u):
                dve.wait_ge(exp2, t + 1)
                nc.vector.tensor_reduce(col_sum[:, u % 2], s[:, u % QB].rearrange("p (g m) -> p m g", g=F), AX.X, ALU.add).then_inc(col_summed, 1)

            def column_inverse(t, u):
                dve.wait_ge(col_summed, t + 1)
                if not isinstance(t, int) or t >= 2:
                    dve.wait_ge(scaled2, t - 1)
                nc.vector.reciprocal(col_inv[:, u % 2], col_sum[:, u % 2]).then_inc(col_inverted, 1)

            def row_sums(t, u):
                dve.wait_ge(exp_near, t + 1)
                nc.vector.tensor_reduce(row_sum[:, u % 2, 0:DVE_SUMS], s[:, u % QB].rearrange("p (g m) -> p g m", g=F)[:, 0:DVE_SUMS, :],
                                        AX.X, ALU.add).then_inc(row_summed, 1)

            def row_inverse(t, u):
                dve.wait_ge(row_summed, t + 1)
                dve.wait_ge(exp_far, t + 1)
                if not isinstance(t, int) or t >= 2:
                    dve.wait_ge(scaled1, t - 1)
                nc.vector.reciprocal(row_inv[:, u % 2], row_sum[:, u % 2]).then_inc(row_inverted, 1)

            def add(t, u, n, four):
                dve.wait_ge(weighted, t + 1)
                at = (n // H) * TILES + (u % 8 - 3)
                out = k["acc"][:, bass.ds(at, 4), :]
                if not isinstance(t, int) or t >= 4:
                    dve.wait_ge(added, four)
                nc.vector.tensor_tensor(out, ps_z[:], out, ALU.add).then_inc(added, 1)

            def head(n, par, first):
                for j in range(8):
                    t6, u6 = lagged(n, par, j, 6, first)
                    if t6 is not None and u6 % 4 == 3:
                        add(t6, u6, n if j >= 6 else n - 1, 2 * n + (j - 6) // 4)
                    t, u = lagged(n, par, j, 0, first)
                    t3, u3 = lagged(n, par, j, 3, first)
                    t1, u1 = lagged(n, par, j, 1, first)
                    if j == 0:
                        order_keys(n + 1, 1 - par, PROJ * (n + 1))
                    if not first or t >= 2:
                        dve.wait_ge(exp_far, t - 1)
                    top(t, u, 1)
                    if t3 is not None:
                        column_sums(t3, u3)
                    top(t, u, 0)
                    if t3 is not None:
                        column_inverse(t3, u3)
                    if t1 is not None:
                        row_sums(t1, u1)
                    shift(t, u)
                    if t1 is not None:
                        row_inverse(t1, u1)

            order_keys(0, 0, None)

            def tail(n):
                for j in range(6):
                    if j < 3:
                        column_sums(8 * n + j - 3, (j - 3) % 16)
                        column_inverse(8 * n + j - 3, (j - 3) % 16)
                    if j < 1:
                        row_sums(8 * n + j - 1, (j - 1) % 16)
                        row_inverse(8 * n + j - 1, (j - 1) % 16)
                    if (j - 6) % 4 == 3:
                        add(8 * n + j - 6, (j - 6) % 16, n - 1, 2 * n + (j - 6) // 4)
            heads(dve, head, tail)


def two_by_two(eng, count, step, depth, unroll=2):
    head = -(-depth // unroll) * unroll
    for n in range(head):
        step(n, n % unroll, 0)
    with eng.Fori(head // unroll, count // unroll) as i:
        for u in range(unroll):
            step(unroll * i + u, u, None)
    for n in range(count, count + depth):
        step(n, n % unroll, count)


def live(n, edge, lag, count):
    return edge is None or 0 <= n - lag < count


def past(n, k):
    return not isinstance(n, int) or n >= k


def feed_forward(nc, d, k):
    S = 4
    DEPTH = 7
    with ExitStack() as ctx:
        sb = lambda name, shape: ctx.enter_context(nc.sbuf_tensor(name, shape, F32))
        sem = semaphores(nc, ctx)
        ps = lambda name, shape: ctx.enter_context(nc.psum_tensor(name, shape, F32))
        x = sb("f_x", [P, 2, GROUP, C])
        z, zb = sb("f_z", [P, S, GROUP, C]), sb("f_zb", [P, S, GROUP, C])
        z_t, h_t = sb("f_z_t", [P, GROUP * P]), sb("f_h_t", [P, FC, GROUP * P])
        t, u, u_t = sb("f_t", [P, S, GROUP, C]), sb("f_u", [P, 2, GROUP, C]), sb("f_u_t", [P, 2, GROUP * P])
        stats, mean_var = sb("f_stats", [P, 3, GROUP, 6]), sb("f_mean_var", [P, 2, 3, GROUP, 2])
        rstd = sb("f_rstd", [P, 2, 3 * GROUP])
        w1, w2 = sb("f_w1", [P, FC, C]), sb("f_w2", [P, FC, P])
        w1_t, w2_t = sb("f_w1_t", [P, FC, P]), sb("f_w2_t", [P, FC, C])
        rows = sb("f_rows", [P, 5, C])
        b1, b1_rows = sb("f_b1", [P, FC]), sb("f_b1_rows", [FC, P])
        w_dt, b_dt = sb("f_w_dt", [P, 2 * HEADS]), sb("f_b_dt", [P, 2 * HEADS])
        zero, pause = sb("f_zero", [P, B, HALO]), sb("f_pause", [P, 1])
        power, eps = sb("f_power", [P, 3 * GROUP]), sb("f_eps", [P, 3 * GROUP])
        ps_w, ps_z, ps_h = ps("f_ps_w", [P, 512]), ps("f_ps_z", [P, 512]), ps("f_ps_h", [P, 2, 512])
        ps_y, ps_u, ps_dt = ps("f_ps_y", [P, GROUP, C]), ps("f_ps_u", [P, 512]), ps("f_ps_dt", [P, GROUP, 2 * HEADS])
        w_loaded, w_turned, w_copied, constants = sem("f_w_loaded"), sem("f_w_turned"), sem("f_w_copied"), sem("f_constants")
        x_loaded = [sem("f_x_loaded0"), sem("f_x_loaded1")]
        summed, y_summed = sem("f_summed"), sem("f_y_summed")
        seen = [sem(f"f_seen{m}") for m in range(3)]
        averaged = [sem(f"f_averaged{m}") for m in range(3)]
        unit = [sem(f"f_unit{m}") for m in range(3)]
        eps_added, rooted = sem("f_eps_added"), sem("f_rooted")
        z_gained, z_done, zb_done, t_gained, t_done = sem("f_z_gained"), sem("f_z_done"), sem("f_zb_done"), sem("f_t_gained"), sem("f_t_done")
        z_turned, z_copied, h_made, h_copied, y_made = sem("f_z_turned"), sem("f_z_copied"), sem("f_h_made"), sem("f_h_copied"), sem("f_y_made")
        kept, u_turned, u_copied, dt_made, dt_kept = sem("f_kept"), sem("f_u_turned"), sem("f_u_copied"), sem("f_dt_made"), sem("f_dt_kept")
        u_stored, edges_stored = [sem("f_u_stored0"), sem("f_u_stored1")], sem("f_edges_stored")
        block = ctx.enter_context(nc.Block())
        x_tiles = d["x"].rearrange("b l f c -> (b l f) c").rearrange("(g i p) c -> g p i c", i=GROUP, p=P)
        BO, G1, B1, G2, B2 = range(5)
        WLOADS = 5 + 3 + 4
        row = lambda name: d["L0_conv_" + name].rearrange("(a c) -> a c", a=1).to_broadcast([P, C])

        def steps(eng, step):
            two_by_two(eng, GROUPS, step, DEPTH, S)

        def on(n, edge, lag):
            return live(n, edge, lag, GROUPS)

        @block.sync
        def _(sp):
            for i, name in enumerate(("b2", "ln1_g", "ln1_b", "ln2_g", "ln2_b")):
                sp.dma_start(rows[:, i], row(name)).then_inc(w_loaded, 16)
            sp.dma_start(w1[:], d["L0_conv_w1"].rearrange("(j p) c -> p j c", p=P)).then_inc(w_loaded, 16)
            sp.dma_start(w2[:], d["L0_conv_w2"].rearrange("c (j p) -> c j p", p=P)).then_inc(w_loaded, 16)
            sp.dma_start(b1_rows[:], d["L0_conv_b1"].rearrange("(j p) -> j p", p=P)).then_inc(w_loaded, 16)
            for i, name in enumerate(DIRS):
                sp.dma_start(w_dt[:, HEADS * i:HEADS * i + HEADS], d[f"L1_attn_{name}_in_proj"][:, IN_PROJ - HEADS:IN_PROJ]).then_inc(w_loaded, 16)
                sp.dma_start(b_dt[:, HEADS * i:HEADS * i + HEADS],
                             d[f"L1_attn_{name}_dt_bias"].rearrange("(a h) -> a h", a=1).to_broadcast([P, HEADS])).then_inc(w_loaded, 16)

            def step(n, s, edge):
                if on(n, edge, 0):
                    if past(n, 2):
                        sp.wait_ge(summed, n - 1)
                    sp.dma_start(x[:, s % 2], x_tiles[n]).then_inc(x_loaded[s % 2], 16)
                if on(n, edge, 7):
                    sp.wait_ge(u_copied, n - 6)
                    half = HALO + 512 * ((s - 7) % 2)
                    sp.dma_start(d["u_t"][:, (n - 7) // 2, half:half + 512], u_t[:, (s - 7) % 2]).then_inc(u_stored[(s - 7) % 2], 16)
            steps(sp, step)
            sp.dma_start(d["u_t"][:, :, 0:HALO], zero[:]).then_inc(edges_stored, 16)
            sp.dma_start(d["u_t"][:, :, HALO + T:], zero[:]).then_inc(edges_stored, 16)
            sp.wait_ge(edges_stored, 32)
            for par in range(2):
                sp.wait_ge(u_stored[par], 16 * (GROUPS // 2))

        @block.tensor
        def _(pe):
            pe.wait_ge(w_loaded, 16 * WLOADS)
            for j in range(FC):
                last = transpose(nc, ps_w[:, j * P:(j + 1) * P], w1[:, j, :], k["ident"][:])
            last.then_inc(w_turned, 1)
            pe.wait_ge(w_copied, 1)
            for j in range(FC):
                last = transpose(nc, ps_w[:, j * P:(j + 1) * P], w2[:, j, :], k["ident"][:])
            last.then_inc(w_turned, 1)
            pe.wait_ge(w_copied, 2)
            transpose(nc, ps_w[:, 0:FC], b1_rows[:], k["ident"][0:FC, 0:FC]).then_inc(w_turned, 1)

            def step(n, s, edge):
                if on(n, edge, 7):
                    i, q = n - 7, (s - 7) % 2
                    pe.wait_ge(unit[2], i + 1)
                    if past(i, 1):
                        pe.wait_ge(u_copied, i)
                    for j in range(GROUP):
                        last = transpose(nc, ps_u[:, j * P:(j + 1) * P], u[:, q, j, :], k["ident"][:])
                    last.then_inc(u_turned, 1)
                if on(n, edge, 3):
                    i, q = n - 3, (s - 3) % S
                    pe.wait_ge(z_done, i + 1)
                    if past(i, 1):
                        pe.wait_ge(z_copied, i)
                    for j in range(GROUP):
                        last = transpose(nc, ps_z[:, j * P:(j + 1) * P], z[:, q, j, :], k["ident"][:])
                    last.then_inc(z_turned, 1)
                if on(n, edge, 7):
                    i, q = n - 7, (s - 7) % 2
                    pe.wait_ge(u_copied, i + 1)
                    if past(i, 1):
                        pe.wait_ge(dt_kept, i)
                    for j in range(GROUP):
                        last = nc.tensor.matmul(ps_dt[:, j, :], u_t[:, q, j * P:(j + 1) * P], w_dt[:], start=True, stop=True)
                    last.then_inc(dt_made, 1)
                if on(n, edge, 3):
                    i = n - 3
                    pe.wait_ge(z_copied, i + 1)
                    for j in range(FC):
                        if past(i, 1) or j >= 2:
                            pe.wait_ge(h_copied, FC * i + j - 1)
                        nc.tensor.matmul(ps_h[:, j % 2, :], w1_t[:, j, :], z_t[:], start=True, stop=True).then_inc(h_made, 1)
                    pe.wait_ge(h_copied, FC * i + FC)
                    if past(i, 1):
                        pe.wait_ge(y_summed, i)
                    for g in range(GROUP):
                        for j in range(FC):
                            last = nc.tensor.matmul(ps_y[:, g, :], h_t[:, j, g * P:(g + 1) * P], w2_t[:, j, :], start=(j == 0), stop=(j == FC - 1))
                    last.then_inc(y_made, 1)
            steps(pe, step)

        @block.scalar
        def _(act):
            act.wait_ge(w_turned, 1)
            nc.scalar.activation(w1_t[:].rearrange("p j c -> p (j c)"), ps_w[:], ACT.Copy).then_inc(w_copied, 1)
            act.wait_ge(w_turned, 2)
            nc.scalar.activation(w2_t[:].rearrange("p j c -> p (j c)"), ps_w[:], ACT.Copy).then_inc(w_copied, 1)
            act.wait_ge(w_turned, 3)
            nc.scalar.activation(b1[:], ps_w[:, 0:FC], ACT.Copy).then_inc(w_copied, 1)
            act.wait_ge(w_copied, 3)

            def step(n, s, edge):
                if on(n, edge, 7):
                    i, q = n - 7, (s - 7) % 2
                    act.wait_ge(u_turned, i + 1)
                    if past(i, 2):
                        act.wait_ge(dt_made, i - 1)
                        act.wait_ge(u_stored[q], 16 * (i // 2))
                    nc.scalar.activation(u_t[:, q], ps_u[:], ACT.Copy).then_inc(u_copied, 1)
                if on(n, edge, 6):
                    i, q = n - 6, (s - 6) % S
                    act.wait_ge(t_done, i + 1)
                    nc.scalar.activation(k["acc"][:, bass.ds(i * GROUP, GROUP), :], t[:, q], ACT.Copy).then_inc(kept, 1)
                if on(n, edge, 3):
                    i = n - 3
                    act.wait_ge(z_turned, i + 1)
                    if past(i, 1):
                        act.wait_ge(h_made, FC * i)
                    nc.scalar.activation(z_t[:], ps_z[:], ACT.Copy).then_inc(z_copied, 1)
                    if past(i, 1):
                        act.wait_ge(y_made, i)
                    for j in range(FC):
                        act.wait_ge(h_made, FC * i + j + 1)
                        nc.scalar.activation(h_t[:, j, :], ps_h[:, j % 2, :], ACT.Relu, bias=b1[:, j:j + 1]).then_inc(h_copied, 1)
            steps(act, step)

        @block.gpsimd
        def _(pool):
            pool.memset(power[:], -0.5).then_inc(constants, 1)
            pool.memset(eps[:], EPS).then_inc(constants, 1)
            pool.memset(mean_var[:], 1.0).then_inc(constants, 1)
            pool.memset(zero[:], 0.0).then_inc(constants, 1)
            pool.wait_ge(w_loaded, 16 * WLOADS)
            pool.wait_ge(constants, 4)

            def wide(r):
                return rows[:, r, None, :].to_broadcast([P, GROUP, C])

            def step(n, s, edge):
                if edge is None or n >= 2:
                    for m, lag in enumerate((2, 5, 7)):
                        if on(n, edge, lag):
                            pool.wait_ge(averaged[m], n - lag + 1)
                    q = (s - 1) % 2
                    if past(n, 4):
                        for m, lag in enumerate((2, 5, 7)):
                            if on(n - 2, edge, lag) and past(n - 2, lag):
                                pool.wait_ge(unit[m], n - 2 - lag + 1)
                    pool.tensor_tensor(rstd[:, q], mean_var[:, q].rearrange("p m g v -> p (m g) v")[:, :, 1], eps[:], ALU.add).then_inc(eps_added, 1)
                    pool.wait_ge(eps_added, n - 1)
                    pool.tensor_tensor(rstd[:, q], rstd[:, q], power[:], ALU.pow).then_inc(rooted, 1)
                if on(n, edge, 5):
                    i, q = n - 5, (s - 5) % S
                    pool.wait_ge(unit[1], i + 1)
                    pool.tensor_tensor(t[:, q], t[:, q], wide(G2), ALU.mult).then_inc(t_gained, 1)
                if on(n, edge, 2):
                    i, q = n - 2, (s - 2) % S
                    pool.wait_ge(unit[0], i + 1)
                    pool.tensor_tensor(z[:, q], z[:, q], wide(G1), ALU.mult).then_inc(z_gained, 1)
                    pool.wait_ge(z_gained, i + 1)
                    pool.tensor_tensor(z[:, q], z[:, q], wide(B1), ALU.add).then_inc(z_done, 1)
                if on(n, edge, 5):
                    i, q = n - 5, (s - 5) % S
                    pool.wait_ge(t_gained, i + 1)
                    pool.tensor_tensor(t[:, q], t[:, q], wide(B2), ALU.add).then_inc(t_done, 1)
                if on(n, edge, 2):
                    i, q = n - 2, (s - 2) % S
                    pool.wait_ge(z_done, i + 1)
                    pool.tensor_tensor(zb[:, q], z[:, q], wide(BO), ALU.add).then_inc(zb_done, 1)
            steps(pool, step)

        @block.vector
        def _(dve):
            dve.wait_ge(w_loaded, 16 * WLOADS)
            dve.wait_ge(constants, 4)

            def statistics(m, n, i, s, a):
                if past(i, 1):
                    dve.wait_ge(averaged[m], i)
                for j in range(GROUP):
                    last = nc.vector.bn_stats(stats[:, m, j, :], a[:, j, :])
                last.then_inc(seen[m], 1)
                dve.wait_ge(seen[m], i + 1)
                if past(n, 3):
                    dve.wait_ge(rooted, n - 2)
                nc.vector.memset(pause[:], 0.0)
                for j in range(GROUP):
                    last = nc.vector.bn_aggr(mean_var[:, s % 2, m, j, :], stats[:, m, j, :])
                last.then_inc(averaged[m], 1)

            def normalize(m, n, i, s, a, out):
                dve.wait_ge(rooted, n - 1)
                q = (s - 1) % 2
                for j in range(GROUP):
                    r = m * GROUP + j
                    last = nc.vector.tensor_scalar(out[:, j, :], a[:, j, :], mean_var[:, q, m, j, 0:1], rstd[:, q, r:r + 1],
                                                   ALU.subtract, ALU.mult)
                last.then_inc(unit[m], 1)

            def step(n, s, edge):
                if on(n, edge, 2):
                    i, q = n - 2, (s - 2) % S
                    normalize(0, n, i, s, z[:, q], z[:, q])
                if on(n, edge, 5):
                    i, q = n - 5, (s - 5) % S
                    normalize(1, n, i, s, t[:, q], t[:, q])
                if on(n, edge, 7):
                    i, q = n - 7, (s - 7) % S
                    if past(i, 2):
                        dve.wait_ge(u_turned, i - 1)
                    normalize(2, n, i, s, t[:, q], u[:, (s - 7) % 2])
                if on(n, edge, 6):
                    i, q = n - 6, (s - 6) % S
                    dve.wait_ge(t_done, i + 1)
                    statistics(2, n, i, s, t[:, q])
                if on(n, edge, 4):
                    i, q = n - 4, (s - 4) % S
                    dve.wait_ge(y_made, i + 1)
                    dve.wait_ge(zb_done, i + 1)
                    if past(i, S):
                        dve.wait_ge(kept, i - S + 1)
                        dve.wait_ge(unit[2], i - S + 1)
                    nc.vector.tensor_tensor(t[:, q], ps_y[:], zb[:, q], ALU.add).then_inc(y_summed, 1)
                    dve.wait_ge(y_summed, i + 1)
                    statistics(1, n, i, s, t[:, q])
                if on(n, edge, 1):
                    i, q = n - 1, (s - 1) % S
                    dve.wait_ge(x_loaded[(s - 1) % 2], 16 * (i // 2 + 1))
                    if past(i, S):
                        dve.wait_ge(z_turned, i - S + 1)
                        dve.wait_ge(zb_done, i - S + 1)
                    nc.vector.tensor_tensor(z[:, q], x[:, (s - 1) % 2], k["acc"][:, bass.ds(i * GROUP, GROUP), :], ALU.add).then_inc(summed, 1)
                    dve.wait_ge(summed, i + 1)
                    statistics(0, n, i, s, z[:, q])
                if on(n, edge, 7):
                    i = n - 7
                    dve.wait_ge(dt_made, i + 1)
                    nc.vector.tensor_tensor(k["dt"][:, bass.ds(i * GROUP, GROUP), :], ps_dt[:],
                                            b_dt[:, None, :].to_broadcast([P, GROUP, 2 * HEADS]), ALU.add).then_inc(dt_kept, 1)
            steps(dve, step)


def scan(nc, d, k, side):
    fwd = side == 0
    name = "L1_attn_" + DIRS[side] + "_"
    inc, exc = (k["le"], k["gt"]) if fwd else (k["ge"], k["lt"])
    pre = f"m{side}_"
    HP = HEADS * HEAD
    S = 4
    with ExitStack() as ctx:
        sb = lambda n, shape: ctx.enter_context(nc.sbuf_tensor(pre + n, shape, F32))
        sem = semaphores(nc, ctx, pre)
        ps = lambda n, shape: ctx.enter_context(nc.psum_tensor(pre + n, shape, F32))
        in_proj, conv_w = sb("in_proj", [P, IN_PROJ]), sb("conv_w", [P, CONV, TAPS])
        w_conv, rows = sb("w_conv", [P, TAPS, CONV]), sb("rows", [5, P])
        cols, half_b = sb("cols", [P, 5]), sb("half_b", [P, 3])
        w_out_in, w_out = sb("w_out_in", [P, 2, C]), sb("w_out", [P, 2, C])
        a_log, a_pos, skip = sb("a_log", [P, HEADS]), sb("a_pos", [P, HEADS]), sb("skip", [P, HEADS])
        ones, power, eps = sb("ones", [P, P]), sb("power", [P, 1]), sb("eps", [P, 1])
        size, soft = sb("size", [P, ALL, HEADS]), sb("soft", [P, ALL, HEADS])
        dt, da = sb("dt", [P, ALL * HEADS]), sb("da", [P, ALL * HEADS])
        since, until = sb("since", [P, ALL * HEADS]), sb("until", [P, ALL * HEADS])
        whole = sb("whole", [D_STATE, ALL * HEADS])
        u_t = sb("u_t", [P, 2, P + 2 * HALO])
        gate_c, gate_z = sb("gate_c", [P, 3, P]), sb("gate_z", [P, D_INNER])
        x_t = sb("x_t", [P, 2, 2, P])
        b_t, c_t = sb("b_t", [D_STATE, 2, P]), sb("c_t", [D_STATE, S, P])
        silu_z = sb("silu_z", [P, S, D_INNER])
        spread, decay = sb("spread", [P, 2, HEADS, P]), sb("decay", [P, 2, HEADS, P])
        bc, weight = sb("bc", [P, 2, P]), sb("weight", [P, 2, HEADS, P])
        b_n = sb("b_n", [P, 2, D_STATE])
        x_dt, x_until, x_skip = sb("x_dt", [P, 2, HP]), sb("x_until", [P, 2, HP]), sb("x_skip", [P, 2, HP])
        state, faded = sb("state", [D_STATE, B * HP]), sb("faded", [D_STATE, 2, HP])
        y0, y1, y2, y3 = sb("y0", [P, 2, HP]), sb("y1", [P, 2, HP]), sb("y2", [P, 2, HP]), sb("y3", [P, 2, HP])
        square, mean, rstd = sb("square", [P, HP]), sb("mean", [P, 2]), sb("rstd", [P, 2])
        y_t = sb("y_t", [P, 2, P])
        ps_c, ps_z = ps("ps_c", [P, 3, P]), ps("ps_z", [P, 512])
        ps_n, ps_g, ps_l = ps("ps_n", [P, 512]), ps("ps_g", [P, 512]), ps("ps_l", [P, HEADS, P])
        ps_y, ps_s, ps_o = ps("ps_y", [P, 2, HP]), ps("ps_s", [P, 512]), ps("ps_o", [P, 512])
        w_loaded, const, rows_turned, rows_copied, taps_made = sem("w_loaded"), sem("const"), sem("rows_turned"), sem("rows_copied"), sem("taps_made")
        soft_step, dt_made, da_made, sums_made, sums_exp, steps_made = (sem("soft_step"), sem("dt_made"), sem("da_made"), sem("sums_made"),
                                                                         sem("sums_exp"), sem("steps_made"))
        u_loaded = [sem("u_loaded0"), sem("u_loaded1")]
        conv_made, z_made, conv_tanh, z_tanh = sem("conv_made"), sem("z_made"), sem("conv_tanh"), sem("z_tanh")
        conv_gate, z_gate, conv_done, z_done = sem("conv_gate"), sem("z_gate"), sem("conv_done"), sem("z_done")
        spread_made, decay_summed, decayed = sem("spread_made"), sem("decay_summed"), sem("decayed")
        x_turned, bc_made, bc_masked, x_scaled, weighted = sem("x_turned"), sem("bc_made"), sem("bc_masked"), sem("x_scaled"), sem("weighted")
        y_made, state_made, state_faded, state_done = sem("y_made"), sem("state_made"), sem("state_faded"), sem("state_done")
        y_since, y_summed, y_skipped, y_gated = sem("y_since"), sem("y_summed"), sem("y_skipped"), sem("y_gated")
        squared, averaged, rooted = sem("squared"), sem("averaged"), sem("rooted")
        y_turned, y_copied, out_made, out_added = sem("y_turned"), sem("y_copied"), sem("out_made"), sem("out_added")
        block = ctx.enter_context(nc.Block())
        ITEMS = B * TILES
        WLOADS = 7

        def where(n):
            return n % B, n // B if fwd else TILES - 1 - n // B

        def tile(n):
            b, c = where(n)
            return b * TILES + c

        def steps(eng, step):
            two_by_two(eng, ITEMS, lambda n, s, edge: step(n, s % 2, s, edge), 3, S)

        def heads4(v):
            return v.rearrange("p (h e) -> p h e", h=HEADS)

        def per_head(v, n):
            return v[:, bass.ds(tile(n) * HEADS, HEADS)][:, :, None]

        @block.sync
        def _(sp):
            sp.dma_start(in_proj[:], d[name + "in_proj"]).then_inc(w_loaded, 16)
            sp.dma_start(conv_w[:].rearrange("p c i -> p (c i)"),
                         d[name + "conv_w"].rearrange("(a c) i -> a (c i)", a=1).to_broadcast([P, CONV * TAPS])).then_inc(w_loaded, 16)
            sp.dma_start(rows[0:3], d[name + "conv_b"].rearrange("(j p) -> j p", p=P)).then_inc(w_loaded, 16)
            sp.dma_start(rows[3:5], d[name + "norm_w"].rearrange("(j p) -> j p", p=P)).then_inc(w_loaded, 16)
            sp.dma_start(w_out_in[:], d[name + "out_proj"].rearrange("(j p) c -> p j c", p=P)).then_inc(w_loaded, 16)
            sp.dma_start(a_log[:], d[name + "A_log"].rearrange("(a h) -> a h", a=1).to_broadcast([P, HEADS])).then_inc(w_loaded, 16)
            sp.dma_start(skip[:], d[name + "D"].rearrange("(a h) -> a h", a=1).to_broadcast([P, HEADS])).then_inc(w_loaded, 16)

            def step(n, par, s, edge):
                if live(n, edge, 0, ITEMS):
                    if past(n, 2):
                        sp.wait_ge(z_made, n - 1)
                    b, c = where(n)
                    sp.dma_start(u_t[:, par], d["u_t"].rearrange("p b t -> p (b t)")[:, bass.ds(b * (T + 2 * HALO) + c * P, P + 2 * HALO)]).then_inc(u_loaded[par], 16)
            steps(sp, step)

        @block.tensor
        def _(pe):
            pe.wait_ge(w_loaded, 16 * WLOADS)
            transpose(nc, ps_o[:, 0:5], rows[:], k["ident"][0:5, 0:5]).then_inc(rows_turned, 1)
            pe.wait_ge(da_made, 1)
            pe.wait_ge(const, 4)
            nc.tensor.matmul(ps_n[:, 0:ALL * HEADS], inc[:], da[:], start=True, stop=True).then_inc(sums_made, 1)
            nc.tensor.matmul(ps_g[:, 0:ALL * HEADS], exc[:], da[:], start=True, stop=True).then_inc(sums_made, 1)
            nc.tensor.matmul(ps_s[0:D_STATE, 0:ALL * HEADS], ones[:, 0:D_STATE], da[:], start=True, stop=True).then_inc(sums_made, 1)
            pe.wait_ge(rows_copied, 1)
            pe.wait_ge(taps_made, TAPS)
            pe.wait_ge(steps_made, 2)

            def step(n, par, s, edge):
                if live(n, edge, 3, ITEMS):
                    i, q = n - 3, 1 - par
                    pe.wait_ge(y_gated, i + 1)
                    if past(i, 1):
                        pe.wait_ge(out_added, i)
                    for j in range(2):
                        last = transpose(nc, ps_o[:, j * P:(j + 1) * P], y3[:, q, j * P:(j + 1) * P], k["ident"][:])
                    last.then_inc(y_turned, 1)
                if live(n, edge, 2, ITEMS):
                    i, q = n - 2, par
                    pe.wait_ge(weighted, i + 1)
                    pe.wait_ge(x_scaled, i + 1)
                    if past(i, 1):
                        pe.wait_ge(y_summed, i)
                    for h in range(HEADS):
                        nc.tensor.matmul(ps_y[:, 0, h * HEAD:(h + 1) * HEAD], weight[:, q, h, :], x_dt[:, q, h * HEAD:(h + 1) * HEAD], start=True, stop=True)
                    nc.tensor.matmul(ps_y[:, 1, :], c_t[:, (s - 2) % S, :], state[:, bass.ds((i % B) * HP, HP)], start=True, stop=True).then_inc(y_made, 1)
                    if past(i, 1):
                        pe.wait_ge(state_done, i)
                    nc.tensor.matmul(ps_s[0:D_STATE, 0:HP], b_n[:, q, :], x_until[:, q, :], start=True, stop=True).then_inc(state_made, 1)
                if live(n, edge, 3, ITEMS):
                    i = n - 3
                    pe.wait_ge(y_copied, i + 1)
                    for j in range(2):
                        last = nc.tensor.matmul(ps_o[:, 2 * P:3 * P], y_t[:, j, :], w_out[:, j, :], start=(j == 0), stop=(j == 1))
                    last.then_inc(out_made, 1)
                if live(n, edge, 1, ITEMS):
                    i, q = n - 1, 1 - par
                    pe.wait_ge(conv_done, i + 1)
                    if past(i, 1):
                        pe.wait_ge(x_scaled, i)
                    for j in range(2):
                        transpose(nc, ps_n[:, j * P:(j + 1) * P], x_t[:, q, j, :], k["ident"][:])
                    transpose(nc, ps_n[:, 2 * P:2 * P + D_STATE], b_t[:, q, :], k["ident"][0:D_STATE, 0:D_STATE]).then_inc(x_turned, 1)
                    if past(i, 1):
                        pe.wait_ge(bc_masked, i)
                    nc.tensor.matmul(ps_g[:, 0:P], b_t[:, q, :], c_t[:, (s - 1) % S, :], start=True, stop=True).then_inc(bc_made, 1)
                    pe.wait_ge(spread_made, i + 1)
                    if past(i, 1):
                        pe.wait_ge(decayed, i)
                    nc.tensor.matmul(ps_l[:].rearrange("p h l -> p (h l)"), exc[:], spread[:, q].rearrange("p h l -> p (h l)"), start=True, stop=True).then_inc(decay_summed, 1)
                if live(n, edge, 0, ITEMS):
                    pe.wait_ge(u_loaded[par], 16 * (n // 2 + 1))
                    if past(n, 1):
                        pe.wait_ge(conv_done, n)
                    for j in range(3):
                        for i in range(TAPS):
                            at = i if fwd else 2 * HALO - i
                            last = nc.tensor.matmul(ps_c[:, j, :], w_conv[:, i, j * P:(j + 1) * P], u_t[:, par, at:at + P], start=(i == 0), stop=(i == TAPS - 1))
                    last.then_inc(conv_made, 1)
                    if past(n, 1):
                        pe.wait_ge(z_done, n)
                    nc.tensor.matmul(ps_z[:, 0:D_INNER], u_t[:, par, HALO:HALO + P], in_proj[:, 0:D_INNER], start=True, stop=True).then_inc(z_made, 1)
            steps(pe, step)

        @block.scalar
        def _(act):
            raw = k["dt"][:, :, HEADS * side:HEADS * side + HEADS]
            nc.scalar.activation(size[:], raw, ACT.Abs).then_inc(soft_step, 1)
            act.wait_ge(soft_step, 1)
            nc.scalar.activation(soft[:], size[:], ACT.Exp, scale=-1.0).then_inc(soft_step, 1)
            act.wait_ge(soft_step, 2)
            nc.scalar.activation(size[:], soft[:], ACT.Ln, bias=1.0).then_inc(soft_step, 1)
            act.wait_ge(w_loaded, 16 * WLOADS)
            nc.scalar.activation(a_pos[:], a_log[:], ACT.Exp).then_inc(soft_step, 1)
            act.wait_ge(rows_turned, 1)
            nc.scalar.activation(cols[:], ps_o[:, 0:5], ACT.Copy).then_inc(rows_copied, 1)
            act.wait_ge(rows_copied, 1)
            nc.scalar.activation(half_b[:], cols[:, 0:3], ACT.Copy, scale=0.5).then_inc(rows_copied, 1)
            act.wait_ge(rows_copied, 2)
            for i, (out, src) in enumerate(((since, ps_n), (until, ps_g), (whole, ps_s))):
                act.wait_ge(sums_made, i + 1)
                nc.scalar.activation(out[:], src[0:out.shape[0], 0:ALL * HEADS], ACT.Exp).then_inc(sums_exp, 1)
            act.wait_ge(sums_exp, 3)

            def step(n, par, s, edge):
                if live(n, edge, 3, ITEMS):
                    i, q = n - 3, 1 - par
                    act.wait_ge(y_turned, i + 1)
                    if past(i, 1):
                        act.wait_ge(out_made, i)
                    nc.scalar.activation(y_t[:].rearrange("p j l -> p (j l)"), ps_o[:, 0:2 * P], ACT.Copy).then_inc(y_copied, 1)
                    if past(i, 2):
                        act.wait_ge(averaged, i - 1)
                    if past(i, 1):
                        act.wait_ge(squared, i)
                    nc.scalar.activation(square[:], y3[:, q], ACT.Square, scale=D_INNER ** -0.5, accum_out=mean[:, q:q + 1]).then_inc(squared, 1)
                if live(n, edge, 1, ITEMS):
                    i, q = n - 1, 1 - par
                    act.wait_ge(decay_summed, i + 1)
                    if past(i, 2):
                        act.wait_ge(weighted, i - 1)
                    nc.scalar.activation(decay[:, q], ps_l[:], ACT.Exp).then_inc(decayed, 1)
                if live(n, edge, 0, ITEMS):
                    act.wait_ge(conv_made, n + 1)
                    if past(n, 1):
                        act.wait_ge(conv_done, n)
                    for j in range(3):
                        last = nc.scalar.activation(gate_c[:, j, :], ps_c[:, j, :], ACT.Tanh, bias=half_b[:, j:j + 1], scale=0.5)
                    last.then_inc(conv_tanh, 1)
                    act.wait_ge(z_made, n + 1)
                    if past(n, 1):
                        act.wait_ge(z_done, n)
                    nc.scalar.activation(gate_z[:], ps_z[:, 0:D_INNER], ACT.Tanh, scale=0.5).then_inc(z_tanh, 1)
            steps(act, step)

        @block.gpsimd
        def _(pool):
            pool.memset(ones[:], 1.0).then_inc(const, 1)
            pool.memset(power[:], -0.5).then_inc(const, 1)
            pool.memset(state[:], 0.0).then_inc(const, 1)
            pool.memset(eps[:], EPS).then_inc(const, 1)
            pool.wait_ge(steps_made, 2)
            pool.wait_ge(const, 4)

            def step(n, par, s, edge):
                if live(n, edge, 2, ITEMS):
                    i, q = n - 2, par
                    pool.tensor_tensor(heads4(faded[:, q]), heads4(state[:, bass.ds((i % B) * HP, HP)]),
                                       per_head(whole, i).to_broadcast([D_STATE, HEADS, HEAD]), ALU.mult).then_inc(state_faded, 1)
                if live(n, edge, 0, ITEMS):
                    if past(n, 2):
                        pool.wait_ge(decay_summed, n - 1)
                    pool.tensor_tensor(spread[:, par], inc[:, None, :].to_broadcast([P, HEADS, P]),
                                       per_head(da, n).to_broadcast([P, HEADS, P]), ALU.mult).then_inc(spread_made, 1)
                if live(n, edge, 3, ITEMS):
                    i, q = n - 3, 1 - par
                    pool.wait_ge(squared, i + 1)
                    if past(i, 2):
                        pool.wait_ge(out_added, i - 1)
                    pool.tensor_tensor(rstd[:, q:q + 1], mean[:, q:q + 1], eps[:], ALU.add).then_inc(averaged, 1)
                    pool.wait_ge(averaged, i + 1)
                    pool.tensor_tensor(rstd[:, q:q + 1], rstd[:, q:q + 1], power[:], ALU.pow).then_inc(rooted, 1)
                if live(n, edge, 2, ITEMS):
                    i, q = n - 2, par
                    pool.wait_ge(y_summed, i + 1)
                    pool.tensor_tensor(y2[:, q], y1[:, q], x_skip[:, q], ALU.add).then_inc(y_skipped, 1)
                    pool.wait_ge(y_skipped, i + 1)
                    if past(i, 2):
                        pool.wait_ge(squared, i - 1)
                        pool.wait_ge(y_turned, i - 1)
                    pool.tensor_tensor(y3[:, q], y2[:, q], silu_z[:, (s - 2) % S], ALU.mult).then_inc(y_gated, 1)
                if live(n, edge, 1, ITEMS):
                    i, q = n - 1, 1 - par
                    pool.wait_ge(decayed, i + 1)
                    pool.wait_ge(bc_masked, i + 1)
                    if past(i, 2):
                        pool.wait_ge(y_made, i - 1)
                    pool.tensor_tensor(weight[:, q], decay[:, q], bc[:, q, None, :].to_broadcast([P, HEADS, P]), ALU.mult).then_inc(weighted, 1)
            steps(pool, step)

        @block.vector
        def _(dve):
            dve.wait_ge(w_loaded, 16 * WLOADS)
            for i in range(TAPS):
                nc.vector.tensor_tensor(w_conv[:, i, :], in_proj[:, D_INNER:D_INNER + CONV], conv_w[:, :, i], ALU.mult).then_inc(taps_made, 1)
            dve.wait_ge(soft_step, 4)
            raw = k["dt"][:, :, HEADS * side:HEADS * side + HEADS]
            dt3, da3 = (v[:].rearrange("p (t h) -> p t h", h=HEADS) for v in (dt, da))
            nc.vector.scalar_tensor_tensor(out=dt3, in0=raw, scalar=0.0, in1=size[:], op0=ALU.max, op1=ALU.add).then_inc(dt_made, 1)
            dve.wait_ge(dt_made, 1)
            nc.vector.scalar_tensor_tensor(out=da3, in0=dt3, scalar=-1.0, in1=a_pos[:, None, :].to_broadcast([P, ALL, HEADS]),
                                           op0=ALU.mult, op1=ALU.mult).then_inc(da_made, 1)
            dve.wait_ge(rows_copied, 2)
            for j in range(2):
                last = nc.vector.tensor_scalar(w_out[:, j, :], w_out_in[:, j, :], cols[:, 3 + j:4 + j], None, ALU.mult)
            last.then_inc(steps_made, 1)
            dve.wait_ge(sums_exp, 3)
            nc.vector.tensor_tensor(until[:], until[:], dt[:], ALU.mult).then_inc(steps_made, 1)
            dve.wait_ge(steps_made, 2)

            def step(n, par, s, edge):
                if live(n, edge, 2, ITEMS):
                    i, q = n - 2, par
                    dve.wait_ge(y_made, i + 1)
                    nc.vector.tensor_tensor(heads4(y0[:, q]), heads4(ps_y[:, 1, :]), per_head(since, i).to_broadcast([P, HEADS, HEAD]), ALU.mult).then_inc(y_since, 1)
                    dve.wait_ge(state_made, i + 1)
                    dve.wait_ge(state_faded, i + 1)
                    nc.vector.tensor_tensor(state[:, bass.ds((i % B) * HP, HP)], faded[:, q], ps_s[0:D_STATE, 0:HP], ALU.add).then_inc(state_done, 1)
                    dve.wait_ge(y_since, i + 1)
                    if past(i, 2):
                        dve.wait_ge(y_skipped, i - 1)
                    nc.vector.tensor_tensor(y1[:, q], ps_y[:, 0, :], y0[:, q], ALU.add).then_inc(y_summed, 1)
                if live(n, edge, 1, ITEMS):
                    i, q = n - 1, 1 - par
                    dve.wait_ge(bc_made, i + 1)
                    if past(i, 2):
                        dve.wait_ge(weighted, i - 1)
                    nc.vector.tensor_tensor(bc[:, q], ps_g[:, 0:P], inc[:], ALU.mult).then_inc(bc_masked, 1)
                    dve.wait_ge(x_turned, i + 1)
                    if past(i, 2):
                        dve.wait_ge(state_made, i - 1)
                        dve.wait_ge(y_skipped, i - 1)
                    for out, factor in ((x_dt, per_head(dt, i)), (x_until, per_head(until, i)), (x_skip, skip[:, :, None])):
                        nc.vector.tensor_tensor(heads4(out[:, q]), heads4(ps_n[:, 0:HP]), factor.to_broadcast([P, HEADS, HEAD]), ALU.mult)
                    nc.vector.tensor_copy(b_n[:, q], ps_n[:, 2 * P:2 * P + D_STATE]).then_inc(x_scaled, 1)
                if live(n, edge, 3, ITEMS):
                    i, q = n - 3, 1 - par
                    dve.wait_ge(out_made, i + 1)
                    dve.wait_ge(rooted, i + 1)
                    out = k["acc"][:].rearrange("p t c -> p (t c)")[:, bass.ds(tile(i) * C, C)]
                    nc.vector.scalar_tensor_tensor(out=out, in0=ps_o[:, 2 * P:3 * P], scalar=rstd[:, q:q + 1], in1=out,
                                                   op0=ALU.mult, op1=ALU.add).then_inc(out_added, 1)
                if live(n, edge, 0, ITEMS):
                    dve.wait_ge(conv_tanh, n + 1)
                    nc.vector.tensor_scalar(gate_c[:], gate_c[:], 0.5, 0.5, ALU.mult, ALU.add).then_inc(conv_gate, 1)
                    dve.wait_ge(z_tanh, n + 1)
                    nc.vector.tensor_scalar(gate_z[:], gate_z[:], 0.5, 0.5, ALU.mult, ALU.add).then_inc(z_gate, 1)
                    dve.wait_ge(conv_gate, n + 1)
                    if past(n, 2):
                        dve.wait_ge(bc_made, n - 1)
                    if past(n, S):
                        dve.wait_ge(y_made, n - S + 1)
                    for j in range(2):
                        nc.vector.scalar_tensor_tensor(out=x_t[:, par, j, :], in0=ps_c[:, j, :], scalar=cols[:, j:j + 1], in1=gate_c[:, j, :],
                                                       op0=ALU.add, op1=ALU.mult)
                    for out, lo in ((b_t[:, par], 0), (c_t[:, s], D_STATE)):
                        rng = slice(lo, lo + D_STATE)
                        last = nc.vector.scalar_tensor_tensor(out=out, in0=ps_c[rng, 2, :], scalar=cols[rng, 2:3], in1=gate_c[rng, 2, :],
                                                              op0=ALU.add, op1=ALU.mult)
                    last.then_inc(conv_done, 1)
                    dve.wait_ge(z_gate, n + 1)
                    if past(n, S):
                        dve.wait_ge(y_gated, n - S + 1)
                    nc.vector.tensor_tensor(silu_z[:, s], ps_z[:, 0:D_INNER], gate_z[:], ALU.mult).then_inc(z_done, 1)
            steps(dve, step)


RING = 16
QUAD = 4
PAD = P // QUAD


def load_w1(sp, d, ring, e, r):
    sp.dma_start(ring["w1"][:, r], d["L1_ffn_weight1"].rearrange("e c h -> (e c) h")[bass.ds(e * (C + 1), C), :]).then_inc(ring["w1_loaded"][r], 16)


def load_w2(sp, d, ring, e, r):
    hid = 4 * P
    sp.dma_start(ring["w2"][:, r], d["L1_ffn_weight2"].rearrange("e c h -> (e c) h")[bass.ds(e * (hid + 1), hid), :]
                 .rearrange("(p j) c -> p j c", p=P)).then_inc(ring["w2_loaded"][r], 16)


def route(nc, d, k, ring):
    with ExitStack() as ctx:
        sb = lambda name, shape: ctx.enter_context(nc.sbuf_tensor(name, shape, F32))
        sem = semaphores(nc, ctx)
        ps = lambda name, shape: ctx.enter_context(nc.psum_tensor(name, shape, F32))
        u, u_t = sb("r_u", [P, 2, GROUP, C]), sb("r_u_t", [P, 2, GROUP * P])
        stats, mean_var, rstd = sb("r_stats", [P, 2, GROUP, 6]), sb("r_mean_var", [P, 2, GROUP, 2]), sb("r_rstd", [P, 2, GROUP])
        gate_w, gate_t, gate_b = sb("r_gate_w", [E, C]), sb("r_gate_t", [C, E]), sb("r_gate_b", [P, 1])
        gate_row, ones, power = sb("r_gate_row", [1, 2 * E]), sb("r_ones", [1, 1]), sb("r_power", [P, GROUP])
        eps_row, pause = sb("r_eps_row", [P, GROUP]), sb("r_pause", [P, 1])
        prob, rest = sb("r_prob", [P, T]), sb("r_rest", [P, T])
        top, total, eight = sb("r_top", [P, 1]), sb("r_total", [P, 2]), sb("r_eight", [P, TOP])
        turned_c = sb("r_turned_c", [P, 2, 4, P])
        ps_w, ps_u, ps_r = ps("r_ps_w", [P, 512]), ps("r_ps_u", [P, 2, 512]), ps("r_ps_r", [P, 2, 512])
        ps_c, ps_p = ps("r_ps_c", [P, 2, 512]), ps("r_ps_p", [P, 4 * P])
        w_loaded, const, w_turned, w_copied = sem("r_w_loaded"), sem("r_const"), sem("r_w_turned"), sem("r_w_copied")
        seen, averaged, eps, rooted, normed, kept = sem("r_seen"), sem("r_averaged"), sem("r_eps"), sem("r_rooted"), sem("r_normed"), sem("r_kept")
        u_turned, u_copied, routed, biased = sem("r_u_turned"), sem("r_u_copied"), sem("r_routed"), sem("r_biased")
        maxed, exped, inverted, scaled, ranked, removed, chosen = (sem("r_maxed"), sem("r_exped"), sem("r_inverted"), sem("r_scaled"),
                                                                   sem("r_ranked"), sem("r_removed"), sem("r_chosen"))
        c_turned, c_copied, pooled, pool_copied = sem("r_c_turned"), sem("r_c_copied"), sem("r_pooled"), sem("r_pool_copied")
        block = ctx.enter_context(nc.Block())
        SETS = B // 2
        logits = k["chosen"]

        @block.sync
        def _(sp):
            sp.dma_start(gate_w[:], d["L1_ffn_gate_w"]).then_inc(w_loaded, 16)
            for i in range(2):
                sp.dma_start(gate_row[:, E * i:E * i + E], d["L1_ffn_gate_b"].rearrange("(a e) -> a e", a=1)).then_inc(w_loaded, 16)
            for r in range(RING):
                load_w1(sp, d, ring, r, r)
                load_w2(sp, d, ring, r, r)

        @block.tensor
        def _(pe):
            pe.wait_ge(w_loaded, 48)
            transpose(nc, ps_w[:, 0:E], gate_w[:], k["ident"][0:E, 0:E])
            pe.wait_ge(const, 3)
            nc.tensor.matmul(ps_w[:, E:E + 1], gate_row[:], ones[:], start=True, stop=True).then_inc(w_turned, 1)
            pe.wait_ge(w_copied, 2)

            def tokens(g, s, s_int):
                pe.wait_ge(normed, g + 1)
                if s_int or s >= 2:
                    pe.wait_ge(u_copied, g - 1)
                for i in range(GROUP):
                    last = transpose(nc, ps_u[:, s % 2, i * P:(i + 1) * P], u[:, s % 2, i, :], k["ident"][:])
                last.then_inc(u_turned, 1)
                pe.wait_ge(u_copied, g + 1)
                if s_int or s >= 2:
                    pe.wait_ge(biased, g - 1)
                rows = slice(E * (s // 2), E * (s // 2) + E)
                nc.tensor.matmul(ps_r[rows, s % 2, :], gate_t[:], u_t[:, s % 2, :], start=True, stop=True).then_inc(routed, 1)
            for s in range(4):
                tokens(s, s, False)
            with pe.Fori(1, SETS) as i:
                for s in range(4):
                    tokens(4 * i + s, s, True)
            for s in range(SETS):
                pe.wait_ge(chosen, s + 1)
                for half in range(2):
                    n = 2 * s + half
                    if n >= 2:
                        pe.wait_ge(c_copied, n - 1)
                    for i in range(4):
                        at = (4 * half + i) * P
                        last = transpose(nc, ps_c[:, half, i * P:(i + 1) * P], logits[:, s, at:at + P], k["ident"][:])
                    last.then_inc(c_turned, 1)
                pe.wait_ge(c_copied, 2 * s + 2)
                pe.wait_ge(kept, GROUPS)
                for b in range(2):
                    for i in range(TILES):
                        last = nc.tensor.matmul(ps_p[:, 2 * P * (s % 2) + E * b:2 * P * (s % 2) + E * b + E], k["u"][:, (2 * s + b) * TILES + i, :],
                                                turned_c[:, i // 4, i % 4, E * b:E * b + E], start=(i == 0), stop=(i == TILES - 1))
                last.then_inc(pooled, 1)
                pe.wait_ge(pool_copied, s + 1)

        @block.scalar
        def _(act):
            act.wait_ge(w_turned, 1)
            nc.scalar.activation(gate_t[:], ps_w[:, 0:E], ACT.Copy).then_inc(w_copied, 1)
            nc.scalar.activation(gate_b[:], ps_w[:, E:E + 1], ACT.Copy).then_inc(w_copied, 1)
            act.wait_ge(w_copied, 2)

            def tokens(g, s, s_int, i):
                act.wait_ge(u_turned, g + 1)
                if s_int or s >= 2:
                    act.wait_ge(routed, g - 1)
                nc.scalar.activation(u_t[:, s % 2], ps_u[:, s % 2, :], ACT.Copy).then_inc(u_copied, 1)
                act.wait_ge(normed, g + 1)
                nc.scalar.activation(k["u"][:, bass.ds(g * GROUP, GROUP), :], u[:, s % 2], ACT.Copy).then_inc(kept, 1)
                act.wait_ge(routed, g + 1)
                rows = slice(E * (s // 2), E * (s // 2) + E)
                out = logits[:].rearrange("p s t -> p (s t)")[rows, bass.ds(i * T + 512 * (s % 2), 512)]
                nc.scalar.activation(out, ps_r[rows, s % 2, :], ACT.Identity, bias=gate_b[rows, :]).then_inc(biased, 1)
            for s in range(4):
                tokens(s, s, False, 0)
            with act.Fori(1, SETS) as i:
                for s in range(4):
                    tokens(4 * i + s, s, True, i)

            def exps(s):
                act.wait_ge(maxed, s + 1)
                if s >= 1:
                    act.wait_ge(chosen, s)
                nc.scalar.activation(prob[:], logits[:, s, :], ACT.Exp, bias=top[:], accum_out=total[:, 0:1]).then_inc(exped, 1)
            exps(0)
            for s in range(SETS):
                if s + 1 < SETS:
                    exps(s + 1)
                if s >= 1:
                    act.wait_ge(pooled, s)
                for half in range(2):
                    act.wait_ge(c_turned, 2 * s + half + 1)
                    nc.scalar.activation(turned_c[:, half].rearrange("p i e -> p (i e)"), ps_c[:, half, :], ACT.Copy).then_inc(c_copied, 1)
                act.wait_ge(pooled, s + 1)
                for b in range(2):
                    at = 2 * P * (s % 2) + E * b
                    last = nc.scalar.activation(k["pooled"][:, :, 2 * s + b], ps_p[:, at:at + E], ACT.Copy)
                last.then_inc(pool_copied, 1)

        @block.gpsimd
        def _(pool):
            pool.memset(power[:], -0.5).then_inc(const, 1)
            pool.memset(ones[:], 1.0).then_inc(const, 1)
            pool.memset(eps_row[:], EPS).then_inc(const, 1)
            pool.wait_ge(const, 3)

            def step(n, par, edge):
                if live(n, edge, 0, GROUPS):
                    pool.wait_ge(averaged, n + 1)
                    pool.tensor_tensor(rstd[:, par], mean_var[:, par, :, 1], eps_row[:], ALU.add).then_inc(eps, 1)
                    pool.wait_ge(eps, n + 1)
                    pool.tensor_tensor(rstd[:, par], rstd[:, par], power[:], ALU.pow).then_inc(rooted, 1)
            two_by_two(pool, GROUPS, step, 1)

        @block.vector
        def _(dve):
            def step(n, par, edge):
                if live(n, edge, 0, GROUPS):
                    if past(n, 2):
                        dve.wait_ge(averaged, n - 1)
                        dve.wait_ge(normed, n - 1)
                    for i in range(GROUP):
                        at = (n * GROUP + i) * C
                        last = nc.vector.bn_stats(stats[:, par, i, :], k["acc"][:].rearrange("p t c -> p (t c)")[:, bass.ds(at, C)])
                    last.then_inc(seen, 1)
                    dve.wait_ge(seen, n + 1)
                    nc.vector.memset(pause[:], 0.0)
                    for i in range(GROUP):
                        last = nc.vector.bn_aggr(mean_var[:, par, i, :], stats[:, par, i, :])
                    last.then_inc(averaged, 1)
                if live(n, edge, 1, GROUPS):
                    q, m = 1 - par, n - 1
                    dve.wait_ge(rooted, m + 1)
                    if past(m, 2):
                        dve.wait_ge(kept, m - 1)
                        dve.wait_ge(u_turned, m - 1)
                    for i in range(GROUP):
                        at = (m * GROUP + i) * C
                        last = nc.vector.tensor_scalar(u[:, q, i, :], k["acc"][:].rearrange("p t c -> p (t c)")[:, bass.ds(at, C)],
                                                       mean_var[:, q, i, 0:1], rstd[:, q, i:i + 1], ALU.subtract, ALU.mult)
                    last.then_inc(normed, 1)
            two_by_two(dve, GROUPS, step, 1)
            dve.wait_ge(biased, GROUPS)
            for s in range(SETS):
                if s >= 1:
                    dve.wait_ge(exped, s)
                nc.vector.tensor_reduce(top[:], logits[:, s, :], AX.X, ALU.max, negate=True).then_inc(maxed, 1)
                dve.wait_ge(exped, s + 1)
                nc.vector.reciprocal(total[:, 1:2], total[:, 0:1]).then_inc(inverted, 1)
                dve.wait_ge(inverted, s + 1)
                nc.vector.tensor_scalar(prob[:], prob[:], total[:, 1:2], None, ALU.mult).then_inc(scaled, 1)
                dve.wait_ge(scaled, s + 1)
                nc.vector.max(eight[:], prob[:]).then_inc(ranked, 1)
                dve.wait_ge(ranked, s + 1)
                nc.vector.match_replace(rest[:], eight[:], prob[:], 0.0).then_inc(removed, 1)
                dve.wait_ge(removed, s + 1)
                nc.vector.tensor_tensor(logits[:, s, :], prob[:], rest[:], ALU.subtract).then_inc(chosen, 1)


def experts(nc, d, k, ring):
    QUADS = E // QUAD
    TURN = RING // QUAD
    H1 = 4
    with ExitStack() as ctx:
        sb = lambda name, shape: ctx.enter_context(nc.sbuf_tensor(name, shape, F32))
        sem = semaphores(nc, ctx)
        ps = lambda name, shape: ctx.enter_context(nc.psum_tensor(name, shape, F32))
        w1, w2 = ring["w1"], ring["w2"]
        b1_rows, b1, b2 = sb("e_b1_rows", [E, P, H1]), sb("e_b1", [P, E, H1]), sb("e_b2", [P, C])
        tokens = sb("e_tokens", [P, 2, QUAD, PAD])
        h_raw, h_sum = sb("e_h_raw", [P, 2, H1 * P]), sb("e_h_sum", [P, 2, H1, QUAD, B])
        h = sb("e_h", [P, 2, H1, QUAD, PAD])
        y_quad, y = sb("e_y_quad", [P, 2, C]), sb("e_y", [P, B // 2, C])
        out = sb("e_out", [P, 4, 4, C])
        ps_h, ps_t = ps("e_ps_h", [P, 2, 512]), ps("e_ps_t", [P, 2, 512])
        ps_y, ps_o = ps("e_ps_y", [P, 2, 512]), ps("e_ps_o", [P, 2, 4 * C])
        b_loaded, b_turned, b_copied, blank = sem("e_b_loaded"), sem("e_b_turned"), sem("e_b_copied"), sem("e_blank")
        staged, h_made, h_copied, h_turned = sem("e_staged"), sem("e_h_made"), sem("e_h_copied"), sem("e_h_turned")
        h_biased, h_done, y_made, y_copied = sem("e_h_biased"), sem("e_h_done"), sem("e_y_made"), sem("e_y_copied")
        y_stored, y_loaded = [sem("e_y_stored0"), sem("e_y_stored1")], sem("e_y_loaded")
        y_biased, returned, summed = sem("e_y_biased"), sem("e_returned"), sem("e_summed")
        stored = [sem(f"e_stored{i}") for i in range(4)]
        block = ctx.enter_context(nc.Block())
        w1_d, w2_d = d["L1_ffn_weight1"], d["L1_ffn_weight2"]
        out_tiles = d["out"].rearrange("b l f c -> (b l f) c").rearrange("(g i p) c -> g p i c", i=4, p=P)
        HID = H1 * P

        def steps(eng, step):
            two_by_two(eng, QUADS, step, 1, TURN)

        @block.sync
        def _(sp):
            sp.dma_start(b1_rows[:].rearrange("e p j -> e (p j)"), w1_d[:, C, :]).then_inc(b_loaded, 16)
            for x in range(2):
                sp.dma_start(b2[E * x:E * x + E], w2_d[:, HID, :]).then_inc(b_loaded, 16)

            with sp.Fori(1, E // RING) as i:
                for u in range(TURN):
                    sp.wait_ge(h_made, TURN * i + (u + 1 - TURN))
                    for r in range(QUAD):
                        load_w1(sp, d, ring, RING * i + (QUAD * u + r), QUAD * u + r)
                    sp.wait_ge(y_made, TURN * i + (u + 1 - TURN))
                    for r in range(QUAD):
                        load_w2(sp, d, ring, RING * i + (QUAD * u + r), QUAD * u + r)
            for slot in range(2):
                sp.wait_ge(y_stored[slot], 16 * QUAD * (QUADS // 2))
            for x in range(2):
                sp.dma_start(y[E * x:E * x + E], d["y"].rearrange("(k x) e c -> x e k c", x=2)[x]).then_inc(y_loaded, 16)
            for g in range(GROUPS):
                sp.wait_ge(summed, g + 1)
                sp.dma_start(out_tiles[g], out[:, g % 4]).then_inc(stored[g % 4], 16)
            for g in range(4):
                sp.wait_ge(stored[g], 16 * (GROUPS // 4))

        @block.tensor
        def _(pe):
            pe.wait_ge(b_loaded, 48)
            for j in range(H1):
                last = transpose(nc, ps_t[:, 0, j * E:(j + 1) * E], b1_rows[:, :, j], k["ident"][0:E, 0:E])
            last.then_inc(b_turned, 1)
            pe.wait_ge(b_copied, 1)
            pe.wait_ge(blank, 2)

            def step(n, u, edge):
                if live(n, edge, 0, QUADS):
                    s = u % 2
                    pe.wait_ge(staged, n + 1)
                    if past(n, 2):
                        pe.wait_ge(h_copied, n - 1)
                    for r in range(QUAD):
                        place = QUAD * u + r
                        pe.wait_ge(ring["w1_loaded"][place], 16 * (n // TURN) + 16)
                        last = nc.tensor.matmul(ps_h[PAD * r:PAD * r + PAD, s, :], tokens[:, s, r, :], w1[:, place, :], start=True, stop=True)
                    last.then_inc(h_made, 1)
                if live(n, edge, 1, QUADS):
                    m, s, quad = n - 1, (u - 1) % 2, (u - 1) % TURN
                    pe.wait_ge(h_done, m + 1)
                    if past(m, 2):
                        pe.wait_ge(y_copied, m - 1)
                    for r in range(QUAD):
                        place = QUAD * quad + r
                        pe.wait_ge(ring["w2_loaded"][place], 16 * (m // TURN) + 16)
                        for j in range(H1):
                            last = nc.tensor.matmul(ps_y[PAD * r:PAD * r + PAD, s, 0:C], h[:, s, j, r, :], w2[:, place, j, :], start=(j == 0), stop=(j == H1 - 1))
                    last.then_inc(y_made, 1)
                if live(n, edge, 0, QUADS):
                    s = u % 2
                    pe.wait_ge(h_copied, n + 1)
                    if past(n, 2):
                        pe.wait_ge(h_biased, n - 1)
                    for j in range(H1):
                        last = transpose(nc, ps_t[:, s, j * P:(j + 1) * P], h_raw[:, s, j::H1], k["ident"][:])
                    last.then_inc(h_turned, 1)
            steps(pe, step)
            pe.wait_ge(y_biased, 1)
            for g in range(GROUPS):
                if g >= 2:
                    pe.wait_ge(summed, g - 1)
                b = g // 2
                rows = slice(E * (b % 2), E * (b % 2) + E)
                for i in range(4):
                    at = (4 * (g % 2) + i) * P
                    last = nc.tensor.matmul(ps_o[:, g % 2, i * C:(i + 1) * C], k["chosen"][rows, b // 2, at:at + P], y[rows, b // 2, :], start=True, stop=True)
                last.then_inc(returned, 1)

        @block.scalar
        def _(act):
            act.wait_ge(b_turned, 1)
            nc.scalar.activation(b1[:].rearrange("p e j -> p j e"), ps_t[:, 0, 0:H1 * E].rearrange("p (j e) -> p j e", e=E), ACT.Copy).then_inc(b_copied, 1)

            def step(n, u, edge):
                if live(n, edge, 0, QUADS):
                    act.wait_ge(h_made, n + 1)
                    if past(n, 2):
                        act.wait_ge(h_turned, n - 1)
                    nc.scalar.activation(h_raw[:, u % 2], ps_h[:, u % 2, :], ACT.Copy).then_inc(h_copied, 1)
                if live(n, edge, 1, QUADS):
                    m, s = n - 1, (u - 1) % 2
                    act.wait_ge(y_made, m + 1)
                    if past(m, 2):
                        act.wait_ge(y_stored[s], 16 * QUAD * (m // 2))
                    nc.scalar.activation(y_quad[:, s], ps_y[:, s, 0:C], ACT.Copy).then_inc(y_copied, 1)
                    act.wait_ge(y_copied, m + 1)
                    for r in range(QUAD):
                        act.dma_start(d["y"].rearrange("b e c -> b (e c)")[:, bass.ds((QUAD * m + r) * C, C)],
                                      y_quad[PAD * r:PAD * r + B, s, :]).then_inc(y_stored[s], 16)
                if live(n, edge, 0, QUADS):
                    act.wait_ge(h_biased, n + 1)
                    if past(n, 2):
                        act.wait_ge(y_made, n - 1)
                    nc.scalar.activation(h[:, u % 2, :, :, 0:B], h_sum[:, u % 2], ACT.Gelu).then_inc(h_done, 1)
            act.wait_ge(blank, 2)
            steps(act, step)

        @block.gpsimd
        def _(pool):
            pool.memset(tokens[:], 0.0).then_inc(blank, 1)
            pool.memset(h[:], 0.0).then_inc(blank, 1)
            pool.wait_ge(blank, 2)

            def step(n, u, edge):
                if live(n, edge, 0, QUADS):
                    if past(n, 2):
                        pool.wait_ge(h_made, n - 1)
                    pool.tensor_copy(tokens[:, u % 2, :, 0:B], k["pooled"][:, bass.ds(QUAD * n, QUAD), :]).then_inc(staged, 1)
            steps(pool, step)

        @block.vector
        def _(dve):
            dve.wait_ge(b_copied, 1)

            def step(n, u, edge):
                if live(n, edge, 0, QUADS):
                    s = u % 2
                    dve.wait_ge(h_turned, n + 1)
                    if past(n, 2):
                        dve.wait_ge(h_done, n - 1)
                    bias = b1[:].rearrange("p e j -> p (e j)")[:, bass.ds(n * QUAD * H1, QUAD * H1)].rearrange("p (r j) -> p j r", j=H1)
                    nc.vector.tensor_tensor(h_sum[:, s], ps_t[:, s, :].rearrange("p (j r b) -> p j r b", j=H1, r=QUAD)[:, :, :, 0:B],
                                            bias[:, :, :, None].to_broadcast([P, H1, QUAD, B]), ALU.add).then_inc(h_biased, 1)
            steps(dve, step)
            dve.wait_ge(y_loaded, 32)
            nc.vector.tensor_tensor(y[:], y[:], b2[:, None, :].to_broadcast([P, B // 2, C]), ALU.add).then_inc(y_biased, 1)
            for g in range(GROUPS):
                dve.wait_ge(returned, g + 1)
                if g >= 4:
                    dve.wait_ge(stored[g % 4], 16 * (g // 4))
                nc.vector.tensor_tensor(out[:, g % 4], ps_o[:, g % 2, :].rearrange("p (i c) -> p i c", c=C), k["acc"][:, 4 * g:4 * g + 4, :], ALU.add).then_inc(summed, 1)


def hybrid(nc, d):
    with ExitStack() as ctx:
        k = {}

        def keep(name, shape):
            k[name] = ctx.enter_context(nc.sbuf_tensor(name, shape, F32))
        for name in ("ident", "le", "gt", "ge", "lt"):
            keep(name, [P, P])
        keep("acc", [P, ALL, C])
        keep("dt", [P, ALL, 2 * HEADS])
        with ExitStack() as early:
            k["w_att"] = early.enter_context(nc.sbuf_tensor("w_att", [P, H, SLOT], F32))
            setup(nc, d, k)
            attention(nc, d, k)
        feed_forward(nc, d, k)
        scan(nc, d, k, 0)
        scan(nc, d, k, 1)
        keep("chosen", [P, B // 2, T])
        keep("pooled", [P, E, B])
        ring = {"w1": ctx.enter_context(nc.sbuf_tensor("ring_w1", [P, RING, 4 * P], F32)),
                "w2": ctx.enter_context(nc.sbuf_tensor("ring_w2", [P, RING, 4, C], F32))}
        ring_sem = semaphores(nc, ctx)
        for w in ("w1", "w2"):
            ring[w + "_loaded"] = [ring_sem(f"ring_{w}_loaded{r}") for r in range(RING)]
        with ExitStack() as late:
            k["u"] = late.enter_context(nc.sbuf_tensor("u", [P, ALL, C], F32))
            route(nc, d, k, ring)
        experts(nc, d, k, ring)


def kernel(**inputs):
    import numpy as np
    import concourse.bacc as bacc
    from concourse.bass_utils import run_bass_kernel_spmd as run

    nc = bacc.Bacc("TRN2", target_bir_lowering=False, num_devices=1)
    arrays, d = {}, {}
    for name, value in inputs.items():
        arrays["in_" + name] = a = np.ascontiguousarray(value)
        d[name] = nc.dram_tensor("in_" + name, a.shape, mybir.dt.from_np(a.dtype), kind="ExternalInput").ap()
    d["out"] = nc.dram_tensor("out", (B, L, F, C), F32, kind="ExternalOutput").ap()
    d["x_t"] = nc.dram_tensor("x_t", (P, ALL * P), F32, kind="Internal").ap()
    d["y"] = nc.dram_tensor("y", (B, E, C), F32, kind="Internal").ap()
    d["u_t"] = nc.dram_tensor("u_t", (P, B, T + 2 * HALO), F32, kind="Internal").ap()
    hybrid(nc, d)
    return run(nc, [arrays], core_ids=[0]).results[0]["out"]
```
